# Optimizing a Trainium2 kernel written in Bass

```python
import numpy as np
import jax
import jax.numpy as jnp

def _softmax(x, axis=-1):
    return jax.nn.softmax(x, axis=axis)
def _gelu(x):
    return jax.nn.gelu(x, approximate=True)
def _silu(x):
    return jax.nn.silu(x)
def _sigmoid(x):
    return jax.nn.sigmoid(x)
def _layernorm(x, axis=-1, eps=1e-5):
    m = jnp.mean(x, axis=axis, keepdims=True)
    v = jnp.var(x, axis=axis, keepdims=True)
    return (x - m) / jnp.sqrt(v + eps)
def _scatter_add(tgt, idx, src, axis=0):
    return tgt.at[idx].add(src)
def _segment_sum(src, seg, n):
    return jax.ops.segment_sum(src, seg, n)

kernel_name = 'mk_metaformer_d1_conv_nchw128_8407f7'

def setup_inputs(seed: int = 0):
    np.random.seed(seed)
    _w = jnp.asarray
    def _rec_inputs():
        import jax
        import jax.numpy as jnp
        _gk = jax.random.key(seed)
        x = -8.268e-05 + 0.9999 * jax.random.normal(jax.random.fold_in(_gk, 1), (32, 128, 112, 112), jnp.float32)
        return x
    x = _rec_inputs()
    def _L0_conv_setup():
        import jax, jax.numpy as jnp
        import numpy as np
        from jax import lax
        STRIDE = (1, 1)
        PAD = ((1, 1), (1, 1))

        def ste_sign(x, alpha):
            q = jnp.sign(x)
            e = jnp.tanh(alpha * x)
            return lax.stop_gradient(q - e) + e

        def dwconv(x, w, channels):
            return lax.conv_general_dilated(x, w, window_strides=STRIDE, padding=PAD, dimension_numbers=('NCHW', 'OIHW', 'NCHW'), feature_group_count=channels)
        key = jax.random.key(seed)
        k1, k2 = jax.random.split(key)
        x = jax.random.normal(k1, (32, 128, 112, 112), dtype=jnp.float32)
        weight = jax.random.normal(k2, (128, 1, 3, 3), dtype=jnp.float32)
        alpha_x = jnp.ones((), dtype=jnp.float32)
        alpha_w = jnp.ones((), dtype=jnp.float32)
        return {'x': x, 'weight': weight, 'alpha_x': alpha_x, 'alpha_w': alpha_w}
    _L0_conv_all = _L0_conv_setup()
    _L0_conv_in = {k: v for k, v in _L0_conv_all.items() if k in ('weight', 'alpha_x', 'alpha_w', )}
    del _L0_conv_all

    def _L0_ffn_setup():
        import jax, jax.numpy as jnp
        import numpy as np
        BN_EPS = 1e-05
        key = jax.random.key(seed)
        k1, k2, k3 = jax.random.split(key, 3)
        B, T, I, H = (64, 2048, 128, 128)
        x = jax.random.normal(k1, (B, T, I), dtype=jnp.float32)
        W = jax.random.normal(k2, (H, I), dtype=jnp.float32) * (1.0 / np.sqrt(I))
        V = jnp.linalg.qr(jax.random.normal(k3, (H, H), dtype=jnp.float32))[0]
        gamma = jnp.ones((H,), dtype=jnp.float32)
        beta = jnp.zeros((H,), dtype=jnp.float32)
        return {'x': x, 'W': W, 'V': V, 'gamma': gamma, 'beta': beta}
    _L0_ffn_all = _L0_ffn_setup()
    _L0_ffn_in = {k: v for k, v in _L0_ffn_all.items() if k in ('W', 'V', 'gamma', 'beta', )}
    del _L0_ffn_all

    return {
        "x": x,
        "L0_conv_weight": _L0_conv_in["weight"],
        "L0_conv_alpha_x": _L0_conv_in["alpha_x"],
        "L0_conv_alpha_w": _L0_conv_in["alpha_w"],
        "L0_ffn_W": _L0_ffn_in["W"],
        "L0_ffn_V": _L0_ffn_in["V"],
        "L0_ffn_gamma": _L0_ffn_in["gamma"],
        "L0_ffn_beta": _L0_ffn_in["beta"],
    }

def reference(x, L0_conv_weight, L0_conv_alpha_x, L0_conv_alpha_w, L0_ffn_W, L0_ffn_V, L0_ffn_gamma, L0_ffn_beta):
    import jax
    import jax.numpy as jnp
    def _L0_conv_ref(x, weight, alpha_x, alpha_w):
        import jax, jax.numpy as jnp
        import numpy as np
        from jax import lax
        STRIDE = (1, 1)
        PAD = ((1, 1), (1, 1))

        def ste_sign(x, alpha):
            q = jnp.sign(x)
            e = jnp.tanh(alpha * x)
            return lax.stop_gradient(q - e) + e

        def dwconv(x, w, channels):
            return lax.conv_general_dilated(x, w, window_strides=STRIDE, padding=PAD, dimension_numbers=('NCHW', 'OIHW', 'NCHW'), feature_group_count=channels)
        channels = weight.shape[0]
        xq = ste_sign(x, alpha_x)
        wq = ste_sign(weight, alpha_w)
        out = dwconv(xq, weight, channels) + dwconv(x, wq, channels)
        return out

    def _L0_ffn_ref(x, W, V, gamma, beta):
        import jax, jax.numpy as jnp
        import numpy as np
        BN_EPS = 1e-05
        B, T, H = (x.shape[0], x.shape[1], W.shape[0])
        Wx = jnp.einsum('bti,hi->bth', x, W)
        flat = Wx.reshape(B * T, H)
        mean = jnp.mean(flat, axis=0)
        var = jnp.var(flat, axis=0)
        Wx = ((flat - mean) * jax.lax.rsqrt(var + BN_EPS) * gamma + beta).reshape(B, T, H)
        Vt = V.T

        def step(yt, wx_t):
            yt = jax.nn.sigmoid(wx_t + yt @ Vt)
            return (yt, yt)
        y0 = jnp.zeros((B, H), dtype=Wx.dtype)
        _, ys = jax.lax.scan(step, y0, jnp.swapaxes(Wx, 0, 1))
        return jnp.swapaxes(ys, 0, 1)

    def _gn(v, G=32, eps=1e-5):
        B_, C_, H_, W_ = v.shape
        g = v.reshape(B_, G, C_ // G, H_, W_)
        m = jnp.mean(g, axis=(2, 3, 4), keepdims=True)
        s = jnp.var(g, axis=(2, 3, 4), keepdims=True)
        return ((g - m) / jnp.sqrt(s + eps)).reshape(v.shape)

    def _ln_c(v, eps=1e-6):
        m = jnp.mean(v, axis=1, keepdims=True)
        s = jnp.var(v, axis=1, keepdims=True)
        return (v - m) / jnp.sqrt(s + eps)

    def _ln_t(v, eps=1e-5):
        m = jnp.mean(v, axis=-1, keepdims=True)
        s = jnp.var(v, axis=-1, keepdims=True)
        return (v - m) / jnp.sqrt(s + eps)

    def _to_tokens(v):
        B_, C_, H_, W_ = v.shape
        return v.reshape(B_, C_, H_ * W_).transpose(0, 2, 1)
    def _from_tokens(t, like):
        B_, C_, H_, W_ = like.shape
        return t.transpose(0, 2, 1).reshape(B_, C_, H_, W_)

    x = x + _L0_conv_ref(_ln_c(x), L0_conv_weight, L0_conv_alpha_x, L0_conv_alpha_w)
    t = _to_tokens(x)
    t = t + _L0_ffn_ref(_ln_t(t), L0_ffn_W, L0_ffn_V, L0_ffn_gamma, L0_ffn_beta)
    x = _from_tokens(t, x)
    return x


_drawn_inputs = setup_inputs


def setup_inputs(seed=0):
    import zlib

    import numpy as np

    out = dict(_drawn_inputs(seed))
    spreads = {'L0_ffn_gamma': (1.0, 0.6), 'L0_ffn_beta': (0.0, 2.0)}
    factors = {'L0_ffn_V': 2.853}
    for name, (base, spread) in spreads.items():
        noise = np.random.default_rng([zlib.crc32(name.encode()), seed]).standard_normal(out[name].shape)
        drawn = base * np.exp(spread * noise) if base else spread * noise
        out[name] = jnp.asarray(drawn.astype(out[name].dtype))
    for name, factor in factors.items():
        out[name] = (out[name] * factor).astype(out[name].dtype)
    return out
```

```python
from contextlib import ExitStack

import concourse.bass as bass
from concourse import mybir

F32 = mybir.dt.float32
F32R = mybir.dt.float32r
BF16 = mybir.dt.bfloat16
I32 = mybir.dt.int32
ACT = mybir.ActivationFunctionType
ALU = mybir.AluOpType
AX = mybir.AxisListType

NB, CH, HT, WD = 32, 128, 112, 112
TAPS = 3

CL, WR = 8, 16
CC = CH // CL
BR = WR - 2
BANDS = HT // BR
BG = 4
GROUPS = NB // BG
TILES = BANDS * GROUPS
TN = BG * WD
PAIRS = CC // 2
PITCH = WD + 2
LEAD = 1
XBUFS = 3
LN1_EPS, LN2_EPS, BN_EPS = 1e-6, 1e-5, 1e-5


def wait(eng, sem, count):
    if isinstance(count, int) and count <= 0:
        return
    eng.wait_ge(sem, count)


def conv_phase(nc, x, weight, x2, stat2):
    with ExitStack() as ctx:
        def sb(name, shape, dt=F32):
            return ctx.enter_context(nc.sbuf_tensor(name, shape, dt))

        def ps(name, shape, dt=F32):
            return ctx.enter_context(nc.psum_tensor(name, shape, dt))

        def sem(name):
            return ctx.enter_context(nc.semaphore(name))

        X = sb("X", [128, XBUFS, CC, TN])
        band_hi = sb("band_hi", [128, CC, TAPS, 128], F32R)
        band_lo = sb("band_lo", [128, CC, TAPS, 128], F32R)
        band_sg = sb("band_sg", [128, CC, TAPS, 128], F32R)
        xn = sb("xn", [128, 2, 2, TN])
        xn_hi = sb("xn_hi", [128, 2, 2, BG, PITCH], F32R)
        xn_lo = sb("xn_lo", [128, 2, 2, BG, PITCH], F32R)
        xn_sg = sb("xn_sg", [128, 2, 2, BG, PITCH], F32R)
        acc_sq1 = sb("acc_sq1", [128, 2, TN])
        acc_sq2 = sb("acc_sq2", [128, 2, TN])
        acc_d = sb("acc_d", [128, 2, TN])
        mean1 = sb("mean1", [128, XBUFS, TN])
        rstd1 = sb("rstd1", [128, TN])
        newton = sb("newton", [128, TN])
        stat_out = sb("stat_out", [WR, 2, TN])
        same_row = sb("same_row", [128, 128])
        masks = sb("masks", [128, BANDS + 1])
        row_mask = masks[:, 0:BANDS]
        eps1 = masks[:, BANDS:BANDS + 1]
        conv = ps("conv", [128, 2, 512])
        sq = ps("sq", [128, 2, 512])
        sq2b = ps("sq2b", [128, 2, 512])
        stats = ps("stats", [128, 2, 512])
        full = X[:, 2].rearrange("p c n -> p (c n)")[:, 0:CC * TAPS * 128].rearrange(
            "p (c d m) -> p c d m", c=CC, d=TAPS)
        diag = X[:, 1].rearrange("p c n -> p (c n)")[:, 0:TAPS * 128].rearrange("p (d m) -> p d m", m=128)
        wcol = X[:, 1].rearrange("p c n -> p (c n)")[:, TAPS * 128:TAPS * 128 + CC * TAPS * TAPS].rearrange(
            "p (c k) -> p c k", c=CC)

        x_loaded, x2_stored = sem("x_loaded"), sem("x2_stored")
        w_loaded, masks_ready, full_ready = sem("w_loaded"), sem("masks_ready"), sem("full_ready")
        band_ready, pads_zero = sem("band_ready"), sem("pads_zero")
        x_cleared = sem("x_cleared")
        mean1_summed, mean1_ready = sem("mean1_summed"), sem("mean1_ready")
        centered, sq1_ready, sq1_added = sem("centered"), sem("sq1_ready"), sem("sq1_added")
        var1_summed, seed_ready, rstd_step, rstd_ready = sem("var1_summed"), sem("seed_ready"), sem("rstd_step"), sem("rstd_ready")
        var1_eps = sem("var1_eps")
        xn_ready, hi_ready, sg_ready, lo_ready = sem("xn_ready"), sem("hi_ready"), sem("sg_ready"), sem("lo_ready")
        conv_done, d_ready, d_added = sem("conv_done"), sem("d_ready"), sem("d_added")
        sq2_ready, sq2_added, x2_ready = sem("sq2_ready"), sem("sq2_added"), sem("x2_ready")
        stat2_summed, stat2_ready, stat2_stored = sem("stat2_summed"), sem("stat2_ready"), sem("stat2_stored")

        block = ctx.enter_context(nc.Block())
        LOAD = 16 * CL * BG
        x_rows = x.rearrange("b (cl cc) h w -> b cl h cc w", cc=CC)
        x2_rows = x2.rearrange("(cl cc) r b q w -> cl q b r cc w", cc=CC)
        stat2_rows = stat2.rearrange("s r b q w -> s q r b w")
        flat = lambda t: t.rearrange("p a b -> p (a b)")

        @block.sync
        def _(sp):
            def load_tile(q, g, buf):
                top, bottom = isinstance(q, int) and q == 0, isinstance(q, int) and q == BANDS - 1
                lo, hi = (1 if top else 0), (WR - 1 if bottom else WR)
                for cl in range(CL):
                    for b in range(BG):
                        dst = X[cl * WR + lo:cl * WR + hi, buf].rearrange("p c (b w) -> p c b w", b=BG)[:, :, b]
                        src = x_rows[bass.ds(g * BG + b, 1), cl]
                        sp.dma_start(dst, src[0, bass.ds(BR * q - 1 + lo, hi - lo)]).then_inc(x_loaded, 16)

            def store_tile(q, g, buf):
                for cl in range(CL):
                    for b in range(BG):
                        src = X[cl * WR + 1:cl * WR + 1 + BR, buf].rearrange("p c (b w) -> p c b w", b=BG)[:, :, b]
                        sp.dma_start(x2_rows[cl, bass.ds(q, 1), bass.ds(g * BG + b, 1)][0, 0], src).then_inc(x2_stored, 16)

            def store_stats(q, g):
                for s in range(2):
                    src = stat_out[1:1 + BR, s].rearrange("p (b w) -> p b w", b=BG)
                    sp.dma_start(stat2_rows[s, bass.ds(q, 1)][0, :, bass.ds(g * BG, BG)], src).then_inc(stat2_stored, 16)

            sp.wait_ge(x_cleared, 3)
            for cl in range(CL):
                src = weight[cl * CC:(cl + 1) * CC].rearrange("c o i j -> o (c i j)")
                sp.dma_start(wcol[cl * WR:(cl + 1) * WR].rearrange("p c k -> p (c k)"),
                             src.broadcast_to([WR, CC * TAPS * TAPS])).then_inc(w_loaded, 16)
            load_tile(0, 0, 0)
            sp.wait_ge(band_ready, 2)
            sp.wait_ge(mean1_summed, 1)
            load_tile(0, 1, 1)
            sp.wait_ge(mean1_summed, 2)
            load_tile(0, 2, 2)

            def wait_then_address(sem, count):
                wait(sp, sem, count)
                sp.wait_ge(band_ready, 2)

            def step(t, q, g, load_q, load_g):
                def held(value):
                    return value if isinstance(value, int) else sp.snap(value)

                buf = held(t % XBUFS)
                x2_count, stat2_count = held((t + 1) * PAIRS), held(t + 1)
                summed_count, stored_count = held(t + XBUFS), held((t + 1) * LOAD)
                if load_q is not None:
                    wait_then_address(mean1_summed, summed_count)
                wait_then_address(x2_ready, x2_count)
                store_tile(q, g, buf)
                wait_then_address(stat2_ready, stat2_count)
                store_stats(q, g)
                if load_q is not None:
                    wait_then_address(x2_stored, stored_count)
                    load_tile(load_q, load_g, buf)

            ahead = GROUPS - XBUFS
            for t in range(ahead):
                step(t, 0, t, 0, t + XBUFS)
            with sp.Fori(ahead, TILES - GROUPS - XBUFS) as t:
                t = sp.snap(t)
                step(t, t // GROUPS, t % GROUPS, (t + XBUFS) // GROUPS, (t + XBUFS) % GROUPS)
            for t in range(TILES - GROUPS - XBUFS, TILES):
                n = t + XBUFS
                step(t, t // GROUPS, t % GROUPS, *((n // GROUPS, n % GROUPS) if n < TILES else (None, None)))
            sp.wait_ge(x2_stored, TILES * LOAD)
            sp.wait_ge(stat2_stored, TILES * 32)

        @block.gpsimd
        def _(pool):
            nc.gpsimd.memset(X[:, 1], 0.0).then_inc(masks_ready, 1)
            nc.gpsimd.memset(X[:, 2, CC - 3:CC], 0.0).then_inc(x_cleared, 1)
            pool.wait_ge(masks_ready, 1)
            nc.gpsimd.memset(newton[:, 0:1], 0.0).then_inc(x_cleared, 1)
            step = 1
            for dy in range(TAPS):
                pool.wait_ge(masks_ready, step)
                nc.gpsimd.affine_select(out=diag[:, dy], in_=diag[:, dy], compare_op=ALU.not_equal, fill=1.0,
                                        base=1 - dy, pattern=[[-1, 128]], channel_multiplier=1).then_inc(masks_ready, 1)
                step += 1
                for base, cm, pat in ((0, 1, [[-WR, CL], [0, WR]]), (WR - 1, -1, [[WR, CL], [0, WR]])):
                    pool.wait_ge(masks_ready, step)
                    nc.gpsimd.affine_select(out=diag[:, dy].rearrange("p (c r) -> p c r", r=WR),
                                            in_=diag[:, dy].rearrange("p (c r) -> p c r", r=WR),
                                            compare_op=ALU.is_ge, fill=0.0, base=base, pattern=pat,
                                            channel_multiplier=cm).then_inc(masks_ready, 1)
                    step += 1
                for ro in (0, WR - 1):
                    pool.wait_ge(masks_ready, step)
                    nc.gpsimd.memset(diag[:, dy].rearrange("p (c r) -> p c r", r=WR)[:, :, ro], 0.0).then_inc(masks_ready, 1)
                    step += 1
            nc.gpsimd.memset(same_row[:, :], 0.0).then_inc(masks_ready, 1)
            nc.gpsimd.memset(row_mask[:, :], 1.0).then_inc(masks_ready, 1)
            nc.gpsimd.memset(eps1[:, :], LN1_EPS).then_inc(masks_ready, 1)
            step += 3
            for k in range(1 - CL, CL):
                pool.wait_ge(masks_ready, step)
                nc.gpsimd.affine_select(out=same_row[:, :], in_=same_row[:, :], compare_op=ALU.not_equal, fill=1.0 / CH,
                                        base=k * WR, pattern=[[-1, 128]], channel_multiplier=1).then_inc(masks_ready, 1)
                step += 1
            for cl in range(CL):
                for q, r in ((0, 0), (BANDS - 1, WR - 1)):
                    pool.wait_ge(masks_ready, step)
                    nc.gpsimd.affine_select(out=row_mask[:, q:q + 1], in_=row_mask[:, q:q + 1], compare_op=ALU.not_equal,
                                            fill=0.0, base=-(cl * WR + r), pattern=[[0, 1]],
                                            channel_multiplier=1).then_inc(masks_ready, 1)
                    step += 1
            pool.wait_ge(masks_ready, step)
            for ring in (xn_hi, xn_lo, xn_sg):
                for side in (0, PITCH - 1):
                    nc.gpsimd.memset(ring[:, :, :, :, side].bitcast(F32), 0.0).then_inc(pads_zero, 1)

            def center(t, k):
                if k == 0:
                    wait(pool, mean1_ready, t + 1)
                part = X[:, t % XBUFS, 2 * k:2 * k + 2]
                nc.gpsimd.tensor_tensor(part, part, mean1[:, t % XBUFS].unsqueeze(1).broadcast_to([128, 2, TN]),
                                        ALU.subtract).then_inc(centered, 1)

            def low_part(t, k):
                n = t * PAIRS + k
                wait(pool, hi_ready, n + 1)
                wait(pool, conv_done, 2 * (n - 1))
                nc.gpsimd.tensor_tensor(xn_lo[:, k % 2, :, :, 1:1 + WD], xn[:, k % 2].rearrange("p c (b w) -> p c b w", b=BG),
                                        xn_hi[:, k % 2, :, :, 1:1 + WD].bitcast(F32), ALU.subtract).then_inc(lo_ready, 1)

            def add_mean(t, k):
                n = t * PAIRS + k
                wait(pool, d_added, n + 1)
                wait(pool, sq2_ready, n + 1)
                part = X[:, t % XBUFS, 2 * k:2 * k + 2]
                nc.gpsimd.tensor_tensor(part, part, mean1[:, t % XBUFS].unsqueeze(1).broadcast_to([128, 2, TN]),
                                        ALU.add).then_inc(x2_ready, 1)

            def tile(t, has_prev, has_next, has_next2):
                for k in range(PAIRS):
                    s = k + LEAD
                    if s < PAIRS:
                        if has_next:
                            center(t + 1, s)
                    elif has_next2:
                        center(t + 2, s - PAIRS)
                    low_part(t, k)
                    if k > 0:
                        add_mean(t, k - 1)
                    elif has_prev:
                        add_mean(t - 1, PAIRS - 1)

            for k in range(PAIRS):
                center(0, k)
            for k in range(LEAD):
                center(1, k)
            tile(0, False, True, True)
            with pool.Fori(1, TILES - 2) as t:
                tile(pool.snap(t), True, True, True)
            tile(TILES - 2, True, True, False)
            tile(TILES - 1, True, False, False)
            add_mean(TILES - 1, PAIRS - 1)

        @block.scalar
        def _(act):
            act.wait_ge(full_ready, 1)
            nc.scalar.activation(band_sg[:, :, :, :].rearrange("p c d m -> p (c d m)"),
                                 full.rearrange("p c d m -> p (c d m)"), ACT.Sign).then_inc(band_ready, 1)

            def copy_mean(t):
                wait(act, mean1_summed, t + 1)
                wait(act, x2_ready, (t - XBUFS + 1) * PAIRS)
                nc.scalar.activation(mean1[:, t % XBUFS], stats[:, 0, 0:TN], ACT.Copy).then_inc(mean1_ready, 1)

            def square1(t, k):
                n = t * PAIRS + k
                wait(act, centered, n + 1)
                wait(act, sq1_added, n)
                nc.scalar.activation(sq[:, :, 0:TN], X[:, t % XBUFS, 2 * k:2 * k + 2], ACT.Square).then_inc(sq1_ready, 1)

            def seed(t):
                wait(act, var1_summed, t + 1)
                nc.scalar.activation(stats[:, 1, 0:TN], stats[:, 1, 0:TN], ACT.Identity, bias=eps1[:, 0:1]).then_inc(var1_eps, 1)
                wait(act, var1_eps, t + 1)
                wait(act, xn_ready, t * PAIRS)
                nc.scalar.activation(rstd1[:, :], stats[:, 1, 0:TN], ACT.Abs_reciprocal_sqrt).then_inc(seed_ready, 1)
                wait(act, seed_ready, 2 * t + 1)
                nc.scalar.activation(newton[:, :], rstd1[:, :], ACT.Square).then_inc(seed_ready, 1)

            def split(t, k):
                n = t * PAIRS + k
                wait(act, xn_ready, n + 1)
                wait(act, conv_done, 2 * (n - 1))
                src = xn[:, k % 2].rearrange("p c (b w) -> p c b w", b=BG)
                for c in range(2):
                    i = nc.scalar.activation(xn_hi[:, k % 2, c, :, 1:1 + WD], src[:, c], ACT.Copy)
                i.then_inc(hi_ready, 1)
                for c in range(2):
                    i = nc.scalar.activation(xn_sg[:, k % 2, c, :, 1:1 + WD], src[:, c], ACT.Sign)
                i.then_inc(sg_ready, 1)

            def square2(t, k):
                n = t * PAIRS + k
                wait(act, d_ready, 2 * n + 2)
                wait(act, sq2_added, n)
                nc.scalar.activation(sq2b[:, :, 0:TN], X[:, t % XBUFS, 2 * k:2 * k + 2], ACT.Square).then_inc(sq2_ready, 1)

            def copy_stats(t):
                wait(act, stat2_summed, t + 1)
                wait(act, stat2_stored, 32 * t)
                nc.scalar.activation(stat_out[:, :, :], stats[0:WR, :, 0:TN], ACT.Copy).then_inc(stat2_ready, 1)

            def tile(t, has_prev, has_next, has_next2):
                for k in range(PAIRS):
                    s = k + LEAD
                    split(t, k)
                    if s < PAIRS:
                        if has_next:
                            square1(t + 1, s)
                    elif has_next2:
                        square1(t + 2, s - PAIRS)
                    if k > 0:
                        square2(t, k - 1)
                    elif has_prev:
                        square2(t - 1, PAIRS - 1)
                    if k == 2 and has_prev:
                        copy_stats(t - 1)
                    if k == 6 and has_next2:
                        copy_mean(t + 2)
                    if k == 7 and has_next:
                        seed(t + 1)

            copy_mean(0)
            for k in range(PAIRS):
                square1(0, k)
            copy_mean(1)
            seed(0)
            for k in range(LEAD):
                square1(1, k)
            tile(0, False, True, True)
            with act.Fori(1, TILES - 2) as t:
                tile(act.snap(t), True, True, True)
            tile(TILES - 2, True, True, False)
            tile(TILES - 1, True, False, False)
            square2(TILES - 1, PAIRS - 1)
            copy_stats(TILES - 1)

        @block.vector
        def _(dve):
            nc.vector.memset(X[:, 0], 0.0).then_inc(x_cleared, 1)
            dve.wait_ge(w_loaded, 16 * CL)
            dve.wait_ge(masks_ready, 1 + 5 * TAPS)
            n = 0
            for cc in range(CC):
                for dx in range(TAPS):
                    for dy in range(TAPS):
                        w1 = wcol[:, cc, dy * TAPS + dx:dy * TAPS + dx + 1]
                        if dy == 0:
                            i = nc.vector.tensor_scalar(full[:, cc, dx], diag[:, dy], w1, None, ALU.mult)
                        else:
                            dve.wait_ge(rstd_step, n)
                            i = nc.vector.scalar_tensor_tensor(full[:, cc, dx], diag[:, dy], w1, full[:, cc, dx],
                                                               ALU.mult, ALU.add)
                        i.then_inc(rstd_step, 1)
                        n += 1
            base = n
            dve.wait_ge(rstd_step, base)
            nc.vector.tensor_copy(band_hi[:, :, :, :].rearrange("p c d m -> p (c d m)"),
                                  full.rearrange("p c d m -> p (c d m)")).then_inc(full_ready, 1)
            dve.wait_ge(full_ready, 1)
            nc.vector.tensor_tensor(band_lo[:, :, :, :].rearrange("p c d m -> p (c d m)"),
                                    full.rearrange("p c d m -> p (c d m)"),
                                    band_hi[:, :, :, :].rearrange("p c d m -> p (c d m)").bitcast(F32),
                                    ALU.subtract).then_inc(band_ready, 1)
            dve.wait_ge(masks_ready, 1 + 5 * TAPS + 3 + 2 * CL - 1 + 2 * CL)

            def add_square1(t, k):
                n = t * PAIRS + k
                wait(dve, sq1_ready, n + 1)
                if k == 0:
                    wait(dve, var1_summed, t)
                    nc.vector.tensor_copy(acc_sq1[:, :, :], sq[:, :, 0:TN]).then_inc(sq1_added, 1)
                else:
                    wait(dve, sq1_added, n)
                    nc.vector.tensor_tensor(acc_sq1[:, :, :], acc_sq1[:, :, :], sq[:, :, 0:TN], ALU.add).then_inc(sq1_added, 1)

            def finish_rstd(t, q):
                wait(dve, seed_ready, 2 * t + 2)
                nc.vector.tensor_tensor(newton[:, :], newton[:, :], stats[:, 1, 0:TN], ALU.mult).then_inc(rstd_step, 1)
                wait(dve, rstd_step, base + 2 * t + 1)
                nc.vector.tensor_scalar(newton[:, :], newton[:, :], -0.5, 1.5, ALU.mult, ALU.add).then_inc(rstd_step, 1)
                wait(dve, rstd_step, base + 2 * t + 2)
                nc.vector.scalar_tensor_tensor(rstd1[:, :], rstd1[:, :], row_mask[:, bass.ds(q, 1)], newton[:, :],
                                               ALU.mult, ALU.mult).then_inc(rstd_ready, 1)

            def normalize(t, k):
                n = t * PAIRS + k
                wait(dve, rstd_ready, t + 1)
                wait(dve, sg_ready, n - 1)
                wait(dve, lo_ready, n - 1)
                nc.vector.tensor_tensor(xn[:, k % 2], X[:, t % XBUFS, 2 * k:2 * k + 2],
                                        rstd1[:, :].unsqueeze(1).broadcast_to([128, 2, TN]), ALU.mult).then_inc(xn_ready, 1)

            def add_conv(t, k, c):
                n = 2 * (t * PAIRS + k) + c
                part = X[:, t % XBUFS, 2 * k + c]
                wait(dve, conv_done, n + 1)
                nc.vector.tensor_tensor(part, part, conv[:, c, 0:TN], ALU.add).then_inc(d_ready, 1)

            def sum_d(t, k):
                n = t * PAIRS + k
                part = X[:, t % XBUFS, 2 * k:2 * k + 2]
                wait(dve, d_ready, 2 * n + 2)
                if k == 0:
                    wait(dve, stat2_summed, t)
                    nc.vector.tensor_scalar(acc_d[:, :, :], part, 1.0, None, ALU.mult).then_inc(d_added, 1)
                else:
                    wait(dve, d_added, n)
                    nc.vector.tensor_tensor(acc_d[:, :, :], acc_d[:, :, :], part, ALU.add).then_inc(d_added, 1)

            def add_square2(t, k):
                n = t * PAIRS + k
                wait(dve, sq2_ready, n + 1)
                if k == 0:
                    nc.vector.tensor_copy(acc_sq2[:, :, :], sq2b[:, :, 0:TN]).then_inc(sq2_added, 1)
                else:
                    wait(dve, sq2_added, n)
                    nc.vector.tensor_tensor(acc_sq2[:, :, :], acc_sq2[:, :, :], sq2b[:, :, 0:TN], ALU.add).then_inc(sq2_added, 1)

            def tile(t, q_next, has_prev, has_next, has_next2):
                for k in range(PAIRS):
                    s = k + LEAD
                    normalize(t, k)
                    before = (t, k - 1) if k >= 1 else (t - 1, PAIRS - 1) if has_prev else None
                    before2 = (t, k - 2) if k >= 2 else (t - 1, PAIRS + k - 2) if has_prev else None
                    if before is not None:
                        add_conv(*before, 0)
                    if before2 is not None:
                        add_square2(*before2)
                    if s < PAIRS:
                        if has_next:
                            add_square1(t + 1, s)
                    elif has_next2:
                        add_square1(t + 2, s - PAIRS)
                    if before is not None:
                        add_conv(*before, 1)
                        sum_d(*before)
                if has_next:
                    finish_rstd(t + 1, q_next)

            for k in range(PAIRS):
                add_square1(0, k)
            finish_rstd(0, 0)
            for k in range(LEAD):
                add_square1(1, k)
            tile(0, 0, False, True, True)
            with dve.Fori(1, TILES - 2) as t:
                t = dve.snap(t)
                tile(t, dve.snap((t + 1) // GROUPS), True, True, True)
            tile(TILES - 2, BANDS - 1, True, True, False)
            tile(TILES - 1, None, True, False, False)
            for c in range(2):
                add_conv(TILES - 1, PAIRS - 1, c)
            sum_d(TILES - 1, PAIRS - 1)
            add_square2(TILES - 1, PAIRS - 2)
            add_square2(TILES - 1, PAIRS - 1)

        @block.tensor
        def _(pe):
            pe.wait_ge(masks_ready, 1 + 5 * TAPS + 3 + 2 * CL - 1)

            def sum_mean(t, first, last):
                if first == 0:
                    wait(pe, x_loaded, (t + 1) * LOAD)
                    wait(pe, stat2_ready, t - 2)
                for c in range(first, last):
                    i = nc.tensor.matmul(stats[:, 0, 0:TN], same_row[:, :], X[:, t % XBUFS, c], start=c == 0, stop=c == CC - 1)
                if last == CC:
                    i.then_inc(mean1_summed, 1)

            def sum_var(t):
                wait(pe, sq1_added, (t + 1) * PAIRS)
                wait(pe, stat2_ready, t - 1)
                for c in range(2):
                    i = nc.tensor.matmul(stats[:, 1, 0:TN], same_row[:, :], acc_sq1[:, c], start=c == 0, stop=c == 1)
                i.then_inc(var1_summed, 1)

            def sum_stats2(t):
                wait(pe, sq2_added, (t + 1) * PAIRS)
                wait(pe, d_added, (t + 1) * PAIRS)
                wait(pe, mean1_ready, min(t + 3, TILES) if isinstance(t, int) else t + 3)
                wait(pe, rstd_ready, min(t + 2, TILES) if isinstance(t, int) else t + 2)
                for c in range(2):
                    nc.tensor.matmul(stats[:, 0, 0:TN], same_row[:, :], acc_d[:, c], start=c == 0, stop=c == 1)
                for c in range(2):
                    i = nc.tensor.matmul(stats[:, 1, 0:TN], same_row[:, :], acc_sq2[:, c], start=c == 0, stop=c == 1)
                i.then_inc(stat2_summed, 1)

            def convolve(t, k):
                n = t * PAIRS + k
                wait(pe, sg_ready, n + 1)
                wait(pe, lo_ready, n + 1)
                for c in range(2):
                    wait(pe, d_ready, 2 * n + c - 1)
                    todo = [(m, ring, dx) for dx in range(TAPS)
                            for m, ring in ((band_sg, xn_hi), (band_sg, xn_lo), (band_hi, xn_sg), (band_lo, xn_sg))]
                    for j, (m, ring, dx) in enumerate(todo):
                        i = nc.tensor.matmul(conv[:, c, 0:TN], m[:, 2 * k + c, dx], ring[:, k % 2, c, :, dx:dx + WD],
                                             start=j == 0, stop=j == len(todo) - 1)
                    i.then_inc(conv_done, 1)

            def tile(t, has_prev, has_next, has_next2):
                for k in range(PAIRS):
                    convolve(t, k)
                    if k == 0 and has_prev:
                        sum_stats2(t - 1)
                    if has_next2 and k in (4, 5):
                        sum_mean(t + 2, (k - 4) * CC // 2, (k - 3) * CC // 2)
                    if k == PAIRS - 1 - LEAD and has_next:
                        sum_var(t + 1)

            sum_mean(0, 0, CC)
            sum_var(0)
            pe.wait_ge(mean1_ready, 1)
            sum_mean(1, 0, CC)
            pe.wait_ge(band_ready, 2)
            pe.wait_ge(full_ready, 1)
            pe.wait_ge(pads_zero, 6)
            tile(0, False, True, True)
            with pe.Fori(1, TILES - 2) as t:
                tile(pe.snap(t), True, True, True)
            tile(TILES - 2, True, True, False)
            tile(TILES - 1, True, False, False)
            sum_stats2(TILES - 1)



STEPS = 8
BLOCKS = WD // STEPS
QUAD = 4
IMG_GROUPS = 2
IMGS = NB // IMG_GROUPS
COLS = IMGS * BANDS
PARTS = 3
HALF = BLOCKS // 2
WINDOW_BUFS = 3
TOLERANCE = 2.0 ** -22


def rstd_phase(nc, stat2, rparts):
    with ExitStack() as ctx:
        def sb(name, shape, dt=F32):
            return ctx.enter_context(nc.sbuf_tensor(name, shape, dt))

        def sem(name):
            return ctx.enter_context(nc.semaphore(name))

        moments = sb("moments", [COLS, 2, IMG_GROUPS, BR, WD])
        rstd = sb("rstd", [COLS, IMG_GROUPS, BR, WD])
        work = sb("work", [COLS, IMG_GROUPS, BR, WD])
        ident = sb("ident_r", [128, 128])
        left = sb("left", [WD, BR * IMG_GROUPS, COLS])
        part = [sb(f"part{i}", [WD, BR * IMG_GROUPS, COLS], BF16) for i in range(PARTS)]
        per_bank = 512 // COLS
        banks = BR * IMG_GROUPS // per_bank
        turned = ctx.enter_context(nc.psum_tensor("turned", [WD, banks, per_bank, COLS], F32))
        loaded, ident_ready, squared, var_ready, seeded = (sem(n) for n in ("loaded", "ident_ready", "squared", "var_ready", "seeded"))
        step, rstd_ready, turned_ready, left_ready, parts_stored = (sem(n) for n in ("step", "rstd_done", "turned_ready", "left_ready", "parts_stored"))
        part_ready = sem("part_ready")
        block = ctx.enter_context(nc.Block())
        flat = lambda t: t.rearrange("p g r w -> p (g r w)")

        @block.sync
        def _(sp):
            src = stat2.rearrange("s r (g b) q w -> s g (b q) r w", g=IMG_GROUPS)
            for s in range(2):
                for g in range(IMG_GROUPS):
                    sp.dma_start(moments[:, s, g], src[s, g]).then_inc(loaded, 16)
            dst = rparts.rearrange("r g p j s c -> p (j s) (r g) c")
            for i in range(PARTS):
                sp.wait_ge(part_ready, 1 + i)
                sp.dma_start(dst[i], part[i][:, :, :]).then_inc(parts_stored, 16)
            sp.wait_ge(parts_stored, 16 * PARTS)

        @block.gpsimd
        def _(pool):
            nc.gpsimd.memset(ident[:, :], 0.0).then_inc(ident_ready, 1)
            pool.wait_ge(ident_ready, 1)
            nc.gpsimd.affine_select(out=ident[:, :], in_=ident[:, :], compare_op=ALU.not_equal, fill=1.0, base=0,
                                    pattern=[[-1, 128]], channel_multiplier=1).then_inc(ident_ready, 1)

        @block.scalar
        def _(act):
            act.wait_ge(loaded, 16 * 4)
            nc.scalar.activation(flat(work[:, :, :, :]), flat(moments[:, 0]), ACT.Square).then_inc(squared, 1)
            act.wait_ge(var_ready, 1)
            nc.scalar.activation(flat(rstd[:, :, :, :]), flat(moments[:, 1]), ACT.Abs_reciprocal_sqrt).then_inc(seeded, 1)
            act.wait_ge(seeded, 1)
            nc.scalar.activation(flat(work[:, :, :, :]), flat(rstd[:, :, :, :]), ACT.Square).then_inc(seeded, 1)

        @block.vector
        def _(dve):
            dve.wait_ge(squared, 1)
            nc.vector.scalar_tensor_tensor(flat(moments[:, 1]), flat(moments[:, 1]), LN2_EPS, flat(work[:, :, :, :]),
                                           ALU.add, ALU.subtract).then_inc(var_ready, 1)
            dve.wait_ge(seeded, 2)
            nc.vector.tensor_tensor(flat(work[:, :, :, :]), flat(work[:, :, :, :]), flat(moments[:, 1]), ALU.mult).then_inc(step, 1)
            dve.wait_ge(step, 1)
            nc.vector.tensor_scalar(flat(work[:, :, :, :]), flat(work[:, :, :, :]), -0.5, 1.5, ALU.mult, ALU.add).then_inc(step, 1)
            dve.wait_ge(step, 2)
            nc.vector.tensor_tensor(flat(rstd[:, :, :, :]), flat(rstd[:, :, :, :]), flat(work[:, :, :, :]), ALU.mult).then_inc(rstd_ready, 1)
            dve.wait_ge(turned_ready, 1)
            rows = left[:, :, :].rearrange("p n c -> p (n c)")
            nc.vector.tensor_copy(left[:, :, :].rearrange("p (k n) c -> p k (n c)", k=banks),
                                  turned[:, :, :, :].rearrange("p k n c -> p k (n c)")).then_inc(left_ready, 1)
            for i in range(PARTS):
                dve.wait_ge(left_ready, 1 + i)
                to = part[i][:, :, :].rearrange("p n c -> p (n c)")
                nc.vector.tensor_copy(to, rows).then_inc(part_ready, 1)
                if i < PARTS - 1:
                    dve.wait_ge(part_ready, 1 + i)
                    nc.vector.tensor_tensor(rows, rows, to, ALU.subtract).then_inc(left_ready, 1)

        @block.tensor
        def _(pe):
            pe.wait_ge(ident_ready, 2)
            pe.wait_ge(rstd_ready, 1)
            for n in range(BR * IMG_GROUPS):
                r, g = n // IMG_GROUPS, n % IMG_GROUPS
                i = nc.tensor.transpose(turned[:, n // per_bank, n % per_bank], rstd[:, g, r], ident[:, :])
            i.then_inc(turned_ready, 1)



def window_loader(x2, rparts, X, R):
    x2_win = x2.rearrange("c r (g b) q w -> r g c (b q) w", g=IMG_GROUPS)
    r_win = rparts.rearrange("r g p j s c -> r g p s j c")

    def load(sp, row, g, buf, done):
        sp.dma_start(X[:, buf], x2_win[bass.ds(row, 1), g][0]).then_inc(done, 16)
        for p in range(PARTS):
            sp.dma_start(R[p * STEPS:(p + 1) * STEPS, buf], r_win[bass.ds(row, 1), g, p][0]).then_inc(done, 16)

    return load, x2_win, r_win


WINDOW_INC = 16 * (1 + PARTS)


def pool_constants(nc, pool, R, pick, pick_ready):
    nc.gpsimd.memset(R.rearrange("p k j c -> p (k j c)"), 0.0).then_inc(pick_ready, 1)
    nc.gpsimd.memset(pick.rearrange("p s m -> p (s m)"), 0.0).then_inc(pick_ready, 1)
    for part in range(PARTS):
        pool.wait_ge(pick_ready, 2 + part)
        nc.gpsimd.affine_select(out=pick, in_=pick, compare_op=ALU.not_equal, fill=1.0, base=-part * STEPS,
                                pattern=[[-1, STEPS], [0, 128]], channel_multiplier=1).then_inc(pick_ready, 1)


PICK_READY = 2 + PARTS


def statistics_phase(nc, x2, rparts, W, V, gamma, beta, wT, vT, bias_q):
    with ExitStack() as ctx:
        def sb(name, shape, dt=F32):
            return ctx.enter_context(nc.sbuf_tensor(name, shape, dt))

        def sem(name):
            return ctx.enter_context(nc.semaphore(name))

        quads = WD // QUAD
        total = BR * IMG_GROUPS * quads
        X = sb("X_stat", [128, IMG_GROUPS, COLS, WD])
        R = sb("R_stat", [128, IMG_GROUPS, BLOCKS, COLS], BF16)
        T = sb("T_stat", [128, 2, QUAD, COLS])
        pick = sb("pick_stat", [128, STEPS, 128], BF16)
        parts = sb("bn_parts", [128, total * 6])
        w_in, v_in, ident = sb("w_in", [128, 128]), sb("v_in", [128, 128]), sb("ident", [128, 128])
        small = sb("small", [128, 8])
        gam, bet, row_mean, scale, eps = (small[:, i:i + 1] for i in range(5))
        moments = small[:, 5:7]
        RB = ctx.enter_context(nc.psum_tensor("RB_stat", [128, 2, QUAD, COLS], F32))
        Q = ctx.enter_context(nc.psum_tensor("Q", [128, 2, QUAD, COLS], F32))
        turned = ctx.enter_context(nc.psum_tensor("turned_w", [128, 3, 128], F32))

        params_in, pick_ready, ident_ready = sem("params_in"), sem("pick_ready"), sem("ident_ready_s")
        w_in_x = [sem(f"window_in{g}") for g in range(IMG_GROUPS)]
        spread_done, scaled, projected, measured = sem("spread_done"), sem("scaled"), sem("projected"), sem("measured")
        w_centered, turned_ready, wT_ready, vT_ready = sem("w_centered"), sem("turned_w_ready"), sem("wT_ready"), sem("vT_ready")
        bn_step, std_ready = sem("bn_step"), sem("std_ready")
        load, _, _ = window_loader(x2, rparts, X, R)
        block = ctx.enter_context(nc.Block())

        def run_windows(eng, body):
            body(0, 0, 0, True)
            with eng.Fori(1, BLOCKS) as j:
                body(0, 0, eng.snap(j), False)
            body(0, 1, 0, False)
            with eng.Fori(1, BLOCKS) as j:
                body(0, 1, eng.snap(j), False)
            with eng.Fori(1, BR) as row:
                row = eng.snap(row)
                for g in range(IMG_GROUPS):
                    body(row, g, 0, False)
                    with eng.Fori(1, BLOCKS) as j:
                        body(row, g, eng.snap(j), False)

        def quad_index(row, g, j, i):
            return (row * IMG_GROUPS + g) * quads + 2 * j + i

        @block.sync
        def _(sp):
            for dst, src in ((w_in[:, :], W), (v_in[:, :], V), (gam, gamma.unsqueeze(1)), (bet, beta.unsqueeze(1))):
                sp.dma_start(dst, src).then_inc(params_in, 16)
            sp.wait_ge(pick_ready, 1)
            for g in range(IMG_GROUPS):
                load(sp, 0, g, g, w_in_x[g])
            with sp.Fori(1, BR) as row:
                row = sp.snap(row)
                for g in range(IMG_GROUPS):
                    through = sp.snap(quad_index(row - 1, g, BLOCKS, 0))
                    sp.wait_ge(scaled, through)
                    sp.wait_ge(params_in, 64)
                    load(sp, row, g, g, w_in_x[g])

        @block.gpsimd
        def _(pool):
            pool_constants(nc, pool, R[:, :, :, :], pick[:, :, :], pick_ready)
            nc.gpsimd.memset(ident[:, :], 0.0).then_inc(ident_ready, 1)
            pool.wait_ge(ident_ready, 1)
            nc.gpsimd.affine_select(out=ident[:, :], in_=ident[:, :], compare_op=ALU.not_equal, fill=1.0, base=0,
                                    pattern=[[-1, 128]], channel_multiplier=1).then_inc(ident_ready, 1)
            nc.gpsimd.memset(eps, BN_EPS).then_inc(ident_ready, 1)

        @block.scalar
        def _(act):
            act.wait_ge(bn_step, 1)
            act.wait_ge(ident_ready, 3)
            nc.scalar.activation(scale, moments[:, 1:2], ACT.Sqrt, bias=eps).then_inc(std_ready, 1)

        @block.vector
        def _(dve):
            dve.wait_ge(params_in, 64)
            nc.vector.tensor_reduce(row_mean, w_in[:, :], axis=AX.X, op=ALU.add).then_inc(w_centered, 1)
            dve.wait_ge(w_centered, 1)
            nc.vector.tensor_scalar(row_mean, row_mean, 1.0 / CH, None, ALU.mult).then_inc(w_centered, 1)
            dve.wait_ge(w_centered, 2)
            nc.vector.tensor_scalar(w_in[:, :], w_in[:, :], row_mean, None, ALU.subtract).then_inc(w_centered, 1)
            dve.wait_ge(turned_ready, 1)
            nc.vector.tensor_copy(wT, turned[:, 0]).then_inc(wT_ready, 1)
            nc.vector.tensor_copy(vT, turned[:, 1]).then_inc(vT_ready, 1)

            def body(row, g, j, first):
                for i in range(2):
                    n = quad_index(row, g, j, i)
                    if isinstance(j, int) and i == 0:
                        wait(dve, w_in_x[g], (row + 1) * WINDOW_INC)
                    wait(dve, spread_done, n + 1)
                    wait(dve, projected, n - 1)
                    src = X[:, g, :, bass.ds(j * STEPS + i * QUAD, QUAD)].rearrange("p c s -> p s c")
                    nc.vector.tensor_tensor(T[:, i], src, RB[:, i], ALU.mult).then_inc(scaled, 1)
                    if not first:
                        nc.vector.bn_stats(parts[:, bass.ds(6 * (n - 2), 6)], Q[:, i].rearrange("p s c -> p (s c)")).then_inc(measured, 1)

            run_windows(dve, body)
            for n in (total - 2, total - 1):
                dve.wait_ge(projected, n + 1)
                nc.vector.bn_stats(parts[:, 6 * n:6 * n + 6], Q[:, n % 2].rearrange("p s c -> p (s c)")).then_inc(measured, 1)
            dve.wait_ge(measured, total)
            nc.vector.bn_aggr(moments, parts[:, :]).then_inc(bn_step, 1)
            dve.wait_ge(std_ready, 1)
            nc.vector.reciprocal(scale, scale).then_inc(bn_step, 1)
            dve.wait_ge(bn_step, 2)
            nc.vector.tensor_tensor(scale, scale, gam, ALU.mult).then_inc(bn_step, 1)
            dve.wait_ge(bn_step, 3)
            nc.vector.tensor_tensor(row_mean, moments[:, 0:1], scale, ALU.mult).then_inc(bn_step, 1)
            nc.vector.tensor_scalar(w_in[:, :], w_in[:, :], scale, None, ALU.mult).then_inc(w_centered, 1)
            dve.wait_ge(bn_step, 4)
            nc.vector.tensor_tensor(bias_q, bet, row_mean, ALU.subtract).then_inc(bn_step, 1)
            dve.wait_ge(turned_ready, 2)
            nc.vector.tensor_copy(wT, turned[:, 2]).then_inc(wT_ready, 1)
            dve.wait_ge(wT_ready, 2)
            dve.wait_ge(bn_step, 5)

        @block.tensor
        def _(pe):
            pe.wait_ge(ident_ready, 2)
            pe.wait_ge(w_centered, 3)
            nc.tensor.transpose(turned[:, 0], w_in[:, :], ident[:, :])
            nc.tensor.transpose(turned[:, 1], v_in[:, :], ident[:, :]).then_inc(turned_ready, 1)
            pe.wait_ge(pick_ready, PICK_READY)
            pe.wait_ge(wT_ready, 1)

            def project(i, n):
                nc.tensor.matmul(Q[:, i].rearrange("p s c -> p (s c)"), wT, T[:, i].rearrange("p s c -> p (s c)"),
                                 start=True, stop=True).then_inc(projected, 1)

            def body(row, g, j, first):
                for i in range(2):
                    n = quad_index(row, g, j, i)
                    if isinstance(j, int) and i == 0:
                        wait(pe, w_in_x[g], (row + 1) * WINDOW_INC)
                    wait(pe, scaled, n - 1)
                    for s in range(QUAD):
                        x = nc.tensor.matmul(RB[:, i, s], pick[:, QUAD * i + s], R[:, g, j], start=s == 0, stop=s == QUAD - 1)
                    x.then_inc(spread_done, 1)
                    if first and i == 0:
                        continue
                    wait(pe, scaled, n)
                    wait(pe, measured, n - 2)
                    project(1 - i, n - 1)

            run_windows(pe, body)
            pe.wait_ge(scaled, total)
            pe.wait_ge(measured, total - 2)
            project(1, total - 1)
            pe.wait_ge(w_centered, 4)
            nc.tensor.transpose(turned[:, 2], w_in[:, :], ident[:, :]).then_inc(turned_ready, 1)


def scan_phase(nc, x2, rparts, wT, vT, bias_q, out):
    with ExitStack() as ctx:
        def sb(name, shape, dt=F32):
            return ctx.enter_context(nc.sbuf_tensor(name, shape, dt))

        def sem(name):
            return ctx.enter_context(nc.semaphore(name))

        X = sb("X_scan", [128, WINDOW_BUFS, COLS, WD])
        R = sb("R_scan", [128, WINDOW_BUFS, BLOCKS, COLS], BF16)
        T = sb("T_scan", [128, IMG_GROUPS, 2, QUAD, COLS])
        Y = sb("Y", [128, IMG_GROUPS, STEPS, COLS])
        pick = sb("pick_scan", [128, STEPS, 128], BF16)
        y_warm = sb("y_warm", [128, IMG_GROUPS, COLS])
        small = sb("small_scan", [128, 4])
        ones, agreed = small[:, 0:1], small[:, 1:3]
        verdict = sb("verdict", [1, 1], I32)
        Z = ctx.enter_context(nc.psum_tensor("Z", [128, IMG_GROUPS, 2, QUAD, COLS], F32))
        RB = ctx.enter_context(nc.psum_tensor("RB_scan", [128, IMG_GROUPS, 2, QUAD, COLS], F32))

        pick_ready, y_zero = sem("pick_ready_c"), sem("y_zero")
        both = range(IMG_GROUPS)
        window_in, spread_done, scaled, summed, y_ready, added = (
            [sem(f"{name}{g}") for g in both] for name in ("win_in", "spread", "scaled_c", "summed", "y_ready", "added"))
        restarted, out_stored = sem("restarted"), sem("out_stored")
        warm_kept, check_step, check_summed, verdict_in = sem("warm_kept"), sem("check_step"), sem("check_summed"), sem("verdict_in")
        q_in, q_spread, q_scaled, q_summed, q_y, q_added, q_out = (
            sem(n) for n in ("q_in", "q_spread", "q_scaled", "q_summed", "q_y", "q_added", "q_out"))
        load, x2_win, r_win = window_loader(x2, rparts, X, R)
        out_win = out.rearrange("b c (q r) w -> r b c q w", r=BR)
        block = ctx.enter_context(nc.Block())

        UNITS = 2 * BR + 2

        def alive(u):
            return tuple(g for g in both if g <= u <= UNITS - 2 + g)

        def run_units(eng, unit):
            for u in (0, 1):
                unit(u, u % 2, alive(u), alive(u + 1))
            with eng.Fori(1, BR) as k:
                k = eng.snap(k)
                unit(eng.snap(2 * k), 0, (0, 1), (0, 1))
                unit(eng.snap(2 * k + 1), 1, (0, 1), (0, 1))
            for u in (UNITS - 2, UNITS - 1):
                unit(u, u % 2, alive(u), alive(u + 1))

        def run_bodies(eng, u, parity, groups, then, body, before_last=None):
            def place(u, parity, g, b):
                window = (u + 1 - g) // 2
                return (IMG_GROUPS * window + g) % WINDOW_BUFS, (parity + 1 - g) % 2 * HALF + b

            def one(b, last):
                m = {g: (u - g) * HALF + b for g in sorted({*groups, *(then if last else ())})}
                now = {g: place(u, parity, g, b) for g in groups}
                if last:
                    after = {g: place(u + 1, 1 - parity, g, 0) for g in then}
                else:
                    after = {g: place(u, parity, g, b + 1) for g in groups}
                body(m, now, after)

            with eng.Fori(0, HALF - 1) as b:
                one(eng.snap(b), False)
            if before_last is not None:
                before_last()
            one(HALF - 1, True)

        def wait_window(eng, u, parity, then):
            if parity in then:
                wait(eng, window_in[parity], WINDOW_INC + WINDOW_INC * ((u + 2 - parity) // 2))
            if isinstance(u, int) and u == 0:
                wait(eng, window_in[1], WINDOW_INC)


        x_row = X[:, 0, 0:NB]
        t_seq = T[:, 0, 0].rearrange("p s c -> p (s c)")[:, 0:STEPS * NB].rearrange("p (s b) -> p s b", b=NB)
        y_seq = Y[:, 0].rearrange("p s c -> p (s c)")[:, 0:STEPS * NB].rearrange("p (s b) -> p s b", b=NB)
        z_seq = Z[:, 0, 0].rearrange("p s c -> p (s c)")[:, 0:STEPS * NB].rearrange("p (s b) -> p s b", b=NB)
        r_seq = RB[:, 0, 0].rearrange("p s c -> p (s c)")[:, 0:STEPS * NB].rearrange("p (s b) -> p s b", b=NB)
        ROW_INC = 16 * (1 + IMG_GROUPS * PARTS)

        def rows_in_time(eng, row_of, body):
            with eng.Fori(0, BANDS) as q:
                q = eng.snap(q)
                with eng.Fori(0, BR) as r:
                    r = eng.snap(r)
                    n = eng.snap(q * BR + r)
                    row_of(n, q, r)
                    if body is not None:
                        with eng.Fori(0, BLOCKS) as j:
                            j = eng.snap(j)
                            body(eng.snap(n * BLOCKS + j), n, q, j)

        def one_by_one_sync(sp):
            src = x2.rearrange("c r b q w -> r q c b w")
            dst = out.rearrange("b c (q r) w -> q r c b w", r=BR)

            def row(n, q, r):
                before, through = sp.snap(n * 16 + 16), sp.snap((n + 1) * BLOCKS + 1)
                sp.wait_ge(q_out, before)
                sp.wait_ge(pick_ready, 1)
                sp.dma_start(x_row, src[bass.ds(r, 1), bass.ds(q, 1)][0, 0]).then_inc(q_in, 16)
                for g in both:
                    for p in range(PARTS):
                        sp.dma_start(R[p * STEPS:(p + 1) * STEPS, g], r_win[bass.ds(r, 1), g, p][0]).then_inc(q_in, 16)
                sp.wait_ge(q_added, through)
                sp.wait_ge(pick_ready, 1)
                sp.dma_start(dst[bass.ds(q, 1), bass.ds(r, 1)][0, 0], x_row).then_inc(q_out, 16)

            sp.dma_start(R[0:1, 2, 0], R[0:1, 1, 0]).then_inc(q_out, 16)
            rows_in_time(sp, row, None)
            sp.wait_ge(q_out, (HT + 1) * 16)

        def one_by_one_scalar(act):
            def body(m, n, q, j):
                for s in range(STEPS):
                    if s == 0:
                        act.wait_ge(q_added, m + 1)
                    act.wait_ge(q_summed, m * STEPS + s + 1)
                    nc.scalar.activation(y_seq[:, s], z_seq[:, s], ACT.Sigmoid, bias=bias_q).then_inc(q_y, 1)
            rows_in_time(act, lambda n, q, r: None, body)

        def one_by_one_vector(dve):
            nc.vector.memset(y_seq[:, STEPS - 1], 0.0).then_inc(q_y, 1)
            nc.vector.memset(small[:, 3:4], 0.0).then_inc(q_added, 1)

            def body(m, n, q, j):
                part = x_row[:, :, bass.ds(j * STEPS, STEPS)]
                dve.wait_ge(q_in, (n + 1) * ROW_INC)
                dve.wait_ge(q_spread, m + 1)
                nc.vector.tensor_tensor(t_seq, part.rearrange("p b s -> p s b"), r_seq, ALU.mult).then_inc(q_scaled, 1)
                dve.wait_ge(q_y, (m + 1) * STEPS + 1)
                nc.vector.tensor_tensor(part, part, y_seq.rearrange("p s b -> p b s"), ALU.add).then_inc(q_added, 1)
            rows_in_time(dve, lambda n, q, r: None, body)

        def one_by_one_tensor(pe):
            def body(m, n, q, j):
                pe.wait_ge(q_in, (n + 1) * ROW_INC)
                pe.wait_ge(q_added, m + 1)
                for s in range(STEPS):
                    for g in both:
                        of_band = R[:, g, bass.ds(j, 1)][:, 0].rearrange("p (b q) -> p q b", q=BANDS)[:, bass.ds(q, 1)][:, 0]
                        x = nc.tensor.matmul(r_seq[:, s, g * IMGS:(g + 1) * IMGS], pick[:, s], of_band, start=True, stop=True)
                x.then_inc(q_spread, 1)
                pe.wait_ge(q_scaled, m + 1)
                nc.tensor.matmul(z_seq.rearrange("p s b -> p (s b)"), wT, t_seq.rearrange("p s b -> p (s b)"),
                                 start=True, stop=False, skip_group_check=True)
                for s in range(STEPS):
                    pe.wait_ge(q_y, m * STEPS + s + 1)
                    nc.tensor.matmul(z_seq[:, s], vT, y_seq[:, (s - 1) % STEPS], start=False, stop=True,
                                     skip_group_check=True).then_inc(q_summed, 1)
            rows_in_time(pe, lambda n, q, r: None, body)

        @block.sync
        def _(sp):
            sp.wait_ge(pick_ready, 1)
            for g in both:
                src, half = x2_win[BR - 1, g], WD // 2
                sp.dma_start(X[:, g, 1:COLS, half:WD], src[:, 0:COLS - 1, half:WD]).then_inc(window_in[g], 16)
                for p in range(PARTS):
                    r, rows = r_win[BR - 1, g, p], slice(p * STEPS, (p + 1) * STEPS)
                    sp.dma_start(R[rows, g, HALF:BLOCKS, 1:COLS], r[:, HALF:BLOCKS, 0:COLS - 1]).then_inc(window_in[g], 16)
            sp.wait_ge(scaled[0], 1)
            load(sp, 0, 0, 2, window_in[0])

            def window_through(w, g, refill):
                held = (lambda v: v) if isinstance(w, int) else sp.snap
                buf = held((IMG_GROUPS * w + g) % WINDOW_BUFS)
                through, stored = held(2 * (HALF + BLOCKS * w)), held((IMG_GROUPS * w + g - 1) * IMGS * 16)
                sp.wait_ge(added[g], through)
                sp.wait_ge(pick_ready, 1)
                if not isinstance(w, int) or w > 0:
                    for b in range(IMGS):
                        src = X[:, bass.ds(buf, 1), b * BANDS:(b + 1) * BANDS][:, 0]
                        sp.dma_start(out_win[bass.ds(w - 1, 1), g * IMGS + b][0], src).then_inc(out_stored, 16)
                if refill:
                    wait(sp, out_stored, stored)
                    sp.wait_ge(pick_ready, 1)
                    load(sp, w + g, 1 - g, buf, window_in[1 - g])

            window_through(0, 0, True)
            window_through(0, 1, True)
            with sp.Fori(1, BR - 1) as w:
                w = sp.snap(w)
                for g in both:
                    window_through(w, g, True)
            for w in (BR - 1, BR):
                for g in both:
                    window_through(w, g, w == BR - 1 and g == 0)
            sp.wait_ge(out_stored, BR * NB * 16)
            sp.wait_ge(verdict_in, 1)
            bad = sp.value_load(verdict[0:1, 0:1], min_val=0, max_val=1 << 20)
            with sp.If(bad > 0):
                one_by_one_sync(sp)
            sp.wait_ge(verdict_in, 1)

        @block.gpsimd
        def _(pool):
            pool_constants(nc, pool, R[:, :, :, :], pick[:, :, :], pick_ready)
            nc.gpsimd.memset(Y[:, :, STEPS - 1], 0.0).then_inc(y_zero, 1)
            nc.gpsimd.memset(ones, 1.0).then_inc(y_zero, 1)
            nc.gpsimd.memset(X[:, 0:IMG_GROUPS, 0, WD // 2:WD], 0.0).then_inc(y_zero, 1)

        @block.scalar
        def _(act):
            def body(m, now, after):
                for s in range(STEPS):
                    for g in now:
                        if s % QUAD == 0:
                            wait(act, added[g], 2 * m[g] + s // QUAD - 1)
                        wait(act, summed[g], m[g] * STEPS + s + 1)
                        nc.scalar.activation(Y[:, g, s], Z[:, g, s // QUAD, s % QUAD], ACT.Sigmoid, bias=bias_q).then_inc(y_ready[g], 1)

            def unit(u, parity, groups, then):
                with_first = isinstance(u, int) and u < IMG_GROUPS
                if with_first:
                    m = {g: (u - g) * HALF for g in groups}
                    body(m, groups, ())
                    with act.Fori(1, HALF) as b:
                        b = act.snap(b)
                        body({g: (u - g) * HALF + b for g in groups}, groups, ())
                else:
                    with act.Fori(0, HALF) as b:
                        b = act.snap(b)
                        body({g: (u - g) * HALF + b for g in groups}, groups, ())

            run_units(act, unit)
            act.wait_ge(verdict_in, 1)
            bad = act.value_load(verdict[0:1, 0:1], min_val=0, max_val=1 << 20)
            with act.If(bad > 0):
                one_by_one_scalar(act)
            act.wait_ge(verdict_in, 1)

        @block.vector
        def _(dve):
            def scale(g, m_next, place, i):
                buf, j = place
                wait(dve, spread_done[g], 2 * m_next + i + 1)
                src = X[:, buf, :, bass.ds(j * STEPS + i * QUAD, QUAD)].rearrange("p c s -> p s c")
                nc.vector.tensor_tensor(T[:, g, i], src, RB[:, g, i], ALU.mult).then_inc(scaled[g], 1)

            def add_states(g, m, place, i):
                buf, j = place
                wait(dve, y_ready[g], m * STEPS + (i + 1) * QUAD)
                part = X[:, buf, :, bass.ds(j * STEPS + i * QUAD, QUAD)]
                nc.vector.tensor_tensor(part, part, Y[:, g, i * QUAD:(i + 1) * QUAD].rearrange("p s c -> p c s"),
                                        ALU.add).then_inc(added[g], 1)

            def body(m, now, after):
                for i in range(2):
                    for g in after:
                        scale(g, m[g] + 1, after[g], i)
                    for g in now:
                        add_states(g, m[g], now[g], i)

            def unit(u, parity, groups, then):
                run_bodies(dve, u, parity, groups, then, body, lambda: wait_window(dve, u, parity, then))
                if isinstance(u, int) and u < IMG_GROUPS:
                    last = Y[:, u, STEPS - 1]
                    nc.vector.tensor_copy(y_warm[:, u], last).then_inc(warm_kept, 1)
                    dve.wait_ge(warm_kept, u + 1)
                    nc.vector.memset(last.rearrange("p (b q) -> p b q", q=BANDS)[:, :, 0:1], 0.0).then_inc(restarted, 1)

            dve.wait_ge(y_zero, 3)
            dve.wait_ge(window_in[0], WINDOW_INC)
            body({0: -1}, {}, {0: (0, HALF)})
            run_units(dve, unit)

            diff = T[:, 0].rearrange("p k s c -> p (k s c)")[:, 0:IMG_GROUPS * IMGS * (BANDS - 1)].rearrange(
                "p (g b q) -> p g b q", g=IMG_GROUPS, b=IMGS)
            for g in both:
                nc.vector.tensor_tensor(diff[:, g], Y[:, g, STEPS - 1].rearrange("p (b q) -> p b q", q=BANDS)[:, :, 0:BANDS - 1],
                                        y_warm[:, g].rearrange("p (b q) -> p b q", q=BANDS)[:, :, 1:BANDS],
                                        ALU.subtract).then_inc(check_step, 1)
            dve.wait_ge(check_step, 2)
            flat = diff.rearrange("p g b q -> p (g b q)")
            nc.vector.tensor_tensor(flat, flat, flat, ALU.mult).then_inc(check_step, 1)
            dve.wait_ge(check_step, 3)
            nc.vector.tensor_scalar(flat, flat, TOLERANCE * TOLERANCE, None, ALU.is_le).then_inc(check_step, 1)
            dve.wait_ge(check_step, 4)
            nc.vector.tensor_reduce(agreed[:, 0:1], flat, axis=AX.X, op=ALU.add).then_inc(check_step, 1)
            dve.wait_ge(check_summed, 1)
            count = float(CH * NB * (BANDS - 1))
            nc.vector.tensor_scalar(verdict[0:1, 0:1], RB[0:1, 0, 0, 0, 0:1], -1.0, count, ALU.mult, ALU.add).then_inc(verdict_in, 1)
            dve.wait_ge(verdict_in, 1)
            bad = dve.value_load(verdict[0:1, 0:1], min_val=0, max_val=1 << 20)
            with dve.If(bad > 0):
                one_by_one_vector(dve)
            dve.wait_ge(verdict_in, 1)

        @block.tensor
        def _(pe):
            def spread(g, place, i, half):
                buf, j = place
                for s in (2 * half, 2 * half + 1):
                    x = nc.tensor.matmul(RB[:, g, i, s], pick[:, QUAD * i + s], R[:, buf, j], start=s == 0, stop=s == QUAD - 1)
                if half == 1:
                    x.then_inc(spread_done[g], 1)

            def project(g, quad, i, half):
                if half == 0:
                    wait(pe, scaled[g], quad + 1)
                two = slice(2 * half, 2 * half + 2)
                nc.tensor.matmul(Z[:, g, i, two].rearrange("p s c -> p (s c)"), wT, T[:, g, i, two].rearrange("p s c -> p (s c)"),
                                 start=half == 0, stop=False, skip_group_check=True)

            def recur(g, m, s):
                wait(pe, y_ready[g], m * STEPS + s)
                nc.tensor.matmul(Z[:, g, s // QUAD, s % QUAD], vT, Y[:, g, (s - 1) % STEPS], start=False, stop=True,
                                 skip_group_check=True).then_inc(summed[g], 1)

            def body(m, now, after):
                for s in range(STEPS):
                    for g in now:
                        recur(g, m[g], s)
                    i, g, half = s // QUAD, s % QUAD // 2, s % 2
                    if (g in now) if i == 0 else (g in after):
                        project(g, 2 * m[g] + i + 1, 1 - i, half)
                    if g in after:
                        spread(g, after[g], i, half)

            def unit(u, parity, groups, then):
                run_bodies(pe, u, parity, groups, then, body, lambda: wait_window(pe, u, parity, then))
                if isinstance(u, int) and u < IMG_GROUPS:
                    pe.wait_ge(restarted, u + 1)

            pe.wait_ge(pick_ready, PICK_READY)
            pe.wait_ge(y_zero, 2)
            pe.wait_ge(window_in[0], WINDOW_INC)
            body({0: -1}, {}, {0: (0, HALF)})
            run_units(pe, unit)
            pe.wait_ge(check_step, 5)
            nc.tensor.matmul(RB[0:1, 0, 0, 0, 0:1], agreed[:, 0:1], ones, start=True, stop=True).then_inc(check_summed, 1)
            pe.wait_ge(verdict_in, 1)
            bad = pe.value_load(verdict[0:1, 0:1], min_val=0, max_val=1 << 20)
            with pe.If(bad > 0):
                one_by_one_tensor(pe)
            pe.wait_ge(verdict_in, 1)


def build(nc, x, conv_weight, W, V, gamma, beta, out):
    x2 = nc.dram_tensor("x2", (CH, BR, NB, BANDS, WD), F32, kind="Internal").ap()
    stat2 = nc.dram_tensor("stat2", (2, BR, NB, BANDS, WD), F32, kind="Internal").ap()
    rparts = nc.dram_tensor("rparts", (BR, IMG_GROUPS, PARTS, BLOCKS, STEPS, COLS), BF16, kind="Internal").ap()
    conv_phase(nc, x, conv_weight, x2, stat2)
    rstd_phase(nc, stat2, rparts)
    with ExitStack() as ctx:
        weights = ctx.enter_context(nc.sbuf_tensor("weights", [128, 2, 128], F32))
        bias = ctx.enter_context(nc.sbuf_tensor("bias", [128, 1], F32))
        statistics_phase(nc, x2, rparts, W, V, gamma, beta, weights[:, 0], weights[:, 1], bias[:, 0:1])
        scan_phase(nc, x2, rparts, weights[:, 0], weights[:, 1], bias[:, 0:1], out)


_INS = ['x', 'L0_conv_weight', 'L0_ffn_W', 'L0_ffn_V', 'L0_ffn_gamma', 'L0_ffn_beta']
_OUTS = [((NB, CH, HT, WD), 'float32')]


def kernel(**inputs):
    import numpy as _np
    import concourse.bacc as _bacc
    from concourse import mybir as _mybir
    from concourse.bass_utils import run_bass_kernel_spmd as _run
    nc = _bacc.Bacc("TRN2", target_bir_lowering=False, num_devices=1)
    arrays, args = {}, []
    for name in _INS:
        a = _np.ascontiguousarray(inputs[name])
        arrays[f"in_{name}_dram"] = a
        args.append(nc.dram_tensor(f"in_{name}_dram", a.shape, _mybir.dt.from_np(a.dtype), kind="ExternalInput").ap())
    for i, (shape, dtype) in enumerate(_OUTS):
        dt = _mybir.dt.from_np(_np.dtype(dtype))
        args.append(nc.dram_tensor(f"out_{i}_dram", shape, dt, kind="ExternalOutput").ap())
    build(nc, *args)
    r = _run(nc, [arrays], core_ids=[0])
    return r.results[0]["out_0_dram"]
```

```python
from contextlib import ExitStack

import concourse.bass as bass
from concourse import mybir

F32 = mybir.dt.float32
F32R = mybir.dt.float32r
BF16 = mybir.dt.bfloat16
I32 = mybir.dt.int32
ACT = mybir.ActivationFunctionType
ALU = mybir.AluOpType
AX = mybir.AxisListType

NB, CH, HT, WD = 32, 128, 112, 112
TAPS = 3

CL, WR = 8, 16
CC = CH // CL
BR = WR - 2
BANDS = HT // BR
BG = 2
GROUPS = NB // BG
TILES = BANDS * GROUPS
TN = BG * WD
SC = 4
SLOTS = CC // SC
BC = 2
BANKS = SC // BC
PITCH = WD + 2
LEAD = 2
XBUFS = 5
LN1_EPS, LN2_EPS, BN_EPS = 1e-6, 1e-5, 1e-5


def wait(eng, sem, count):
    if isinstance(count, int) and count <= 0:
        return
    eng.wait_ge(sem, count)


def conv_phase(nc, x, weight, x2, stat2):
    with ExitStack() as ctx:
        def sb(name, shape, dt=F32):
            return ctx.enter_context(nc.sbuf_tensor(name, shape, dt))

        def ps(name, shape, dt=F32):
            return ctx.enter_context(nc.psum_tensor(name, shape, dt))

        def sem(name):
            return ctx.enter_context(nc.semaphore(name))

        X = sb("X", [128, XBUFS, CC, TN])
        band_hi = sb("band_hi", [128, CC, TAPS, 128], F32R)
        band_lo = sb("band_lo", [128, CC, TAPS, 128], F32R)
        band_sg = sb("band_sg", [128, CC, TAPS, 128], F32R)
        xn = sb("xn", [128, 2, SC, TN])
        xn_hi = sb("xn_hi", [128, 2, SC, BG, PITCH], F32R)
        xn_lo = sb("xn_lo", [128, 2, SC, BG, PITCH], F32R)
        xn_sg = sb("xn_sg", [128, 2, SC, BG, PITCH], F32R)
        acc_sq1 = sb("acc_sq1", [128, 2, SC, TN])
        acc_sq2 = sb("acc_sq2", [128, 2, SC, TN])
        acc_d = sb("acc_d", [128, 2, SC, TN])
        mean1 = sb("mean1", [128, XBUFS, TN])
        rstd1 = sb("rstd1", [128, 2, TN])
        guess = sb("guess", [128, TN])
        newton = sb("newton", [128, TN])
        stat_out = sb("stat_out", [WR, 2, TN])
        same_row = sb("same_row", [128, 128])
        masks = sb("masks", [128, BANDS + 1])
        row_mask = masks[:, 0:BANDS]
        eps1 = masks[:, BANDS:BANDS + 1]
        conv = ps("conv", [128, BANKS, 512])
        sq = ps("sq", [128, BANKS, 512])
        sq2b = ps("sq2b", [128, BANKS, 512])
        stats = ps("stats", [128, 2, 2, 256])
        mean_sum, var_sum, stats2_sum = stats[:, 0, 0, 0:TN], stats[:, 1, 0, 0:TN], stats[:, :, 1, 0:TN]
        spare = X[:, 2:XBUFS].rearrange("p x c n -> p (x c n)")
        diag = spare[:, 0:TAPS * 128].rearrange("p (d m) -> p d m", m=128)
        wcol = spare[:, TAPS * 128:TAPS * 128 + CC * TAPS * TAPS].rearrange("p (c k) -> p c k", c=CC)
        full_at = CC * TN
        full = spare[:, full_at:full_at + CC * TAPS * 128].rearrange("p (c d m) -> p c d m", c=CC, d=TAPS)

        x_loaded, x2_stored = sem("x_loaded"), sem("x2_stored")
        w_loaded, masks_ready, full_ready = sem("w_loaded"), sem("masks_ready"), sem("full_ready")
        band_ready, pads_zero = sem("band_ready"), sem("pads_zero")
        x_cleared, tile_in = sem("x_cleared"), sem("tile_in")
        mean1_summed, mean1_ready = sem("mean1_summed"), sem("mean1_ready")
        centered, sq1_ready, sq1_added = sem("centered"), sem("sq1_ready"), sem("sq1_added")
        var1_summed, seed_ready, rstd_step, rstd_ready = sem("var1_summed"), sem("seed_ready"), sem("rstd_step"), sem("rstd_ready")
        var1_eps = sem("var1_eps")
        xn_ready, hi_ready, sg_ready, lo_ready = sem("xn_ready"), sem("hi_ready"), sem("sg_ready"), sem("lo_ready")
        conv_done, d_ready, d_added = sem("conv_done"), sem("d_ready"), sem("d_added")
        sq2_ready, sq2_added, x2_ready = sem("sq2_ready"), sem("sq2_added"), sem("x2_ready")
        stat2_summed, stat2_ready, stat2_stored = sem("stat2_summed"), sem("stat2_ready"), sem("stat2_stored")

        block = ctx.enter_context(nc.Block())
        LOAD = 16 * CL * BG
        x_rows = x.rearrange("b (cl cc) h w -> b cl h cc w", cc=CC)
        x2_rows = x2.rearrange("(cl cc) r b q w -> cl q b r cc w", cc=CC)
        stat2_rows = stat2.rearrange("s r b q w -> s q r b w")
        flat = lambda t: t.rearrange("p a b -> p (a b)")

        def lead_of(t, k, has_next, has_next2, lead=LEAD):
            s = k + lead
            if s < SLOTS:
                return (t + 1, s) if has_next else None
            return (t + 2, s - SLOTS) if has_next2 else None

        def before(t, k, by, has_prev):
            if k >= by:
                return t, k - by
            return (t - 1, SLOTS + k - by) if has_prev else None

        def following(t, k, has_next):
            if k + 1 < SLOTS:
                return t, k + 1
            return (t + 1, 0) if has_next else None

        @block.sync
        def _(sp):
            def load_tile(q, g, buf):
                top, bottom = isinstance(q, int) and q == 0, isinstance(q, int) and q == BANDS - 1
                lo, hi = (1 if top else 0), (WR - 1 if bottom else WR)
                for cl in range(CL):
                    for b in range(BG):
                        dst = X[cl * WR + lo:cl * WR + hi, buf].rearrange("p c (b w) -> p c b w", b=BG)[:, :, b]
                        src = x_rows[bass.ds(g * BG + b, 1), cl]
                        sp.dma_start(dst, src[0, bass.ds(BR * q - 1 + lo, hi - lo)]).then_inc(x_loaded, 16)

            def store_tile(q, g, buf):
                for cl in range(CL):
                    for b in range(BG):
                        src = X[cl * WR + 1:cl * WR + 1 + BR, buf].rearrange("p c (b w) -> p c b w", b=BG)[:, :, b]
                        sp.dma_start(x2_rows[cl, bass.ds(q, 1), bass.ds(g * BG + b, 1)][0, 0], src).then_inc(x2_stored, 16)

            def store_stats(q, g):
                for s in range(2):
                    src = stat_out[1:1 + BR, s].rearrange("p (b w) -> p b w", b=BG)
                    sp.dma_start(stat2_rows[s, bass.ds(q, 1)][0, :, bass.ds(g * BG, BG)], src).then_inc(stat2_stored, 16)

            sp.wait_ge(x_cleared, 3)
            for cl in range(CL):
                src = weight[cl * CC:(cl + 1) * CC].rearrange("c o i j -> o (c i j)")
                sp.dma_start(wcol[cl * WR:(cl + 1) * WR].rearrange("p c k -> p (c k)"),
                             src.broadcast_to([WR, CC * TAPS * TAPS])).then_inc(w_loaded, 16)
            for n in range(XBUFS - 1):
                if n == 2:
                    sp.wait_ge(band_ready, 2)
                load_tile(0, n, n)
                sp.wait_ge(x_loaded, (n + 1) * LOAD)
                sp.sem_inc(tile_in, 1)

            def wait_then_address(sem, count):
                wait(sp, sem, count)
                sp.wait_ge(band_ready, 2)

            def step(t, q, g, load_q, load_g):
                def held(value):
                    return value if isinstance(value, int) else sp.snap(value)

                buf, load_buf = held(t % XBUFS), held((t + XBUFS - 1) % XBUFS)
                x2_count, stat2_count = held((t + 1) * SLOTS), held(t + 1)
                loaded_count, stored_count = held((t + XBUFS) * LOAD), held(t * LOAD)
                wait_then_address(x2_stored, stored_count)
                if load_q is not None:
                    load_tile(load_q, load_g, load_buf)
                wait_then_address(x2_ready, x2_count)
                store_tile(q, g, buf)
                if load_q is not None:
                    wait(sp, x_loaded, loaded_count)
                    sp.sem_inc(tile_in, 1)
                wait_then_address(stat2_ready, stat2_count)
                store_stats(q, g)

            def place(n):
                return (n // GROUPS, n % GROUPS) if n < TILES else (None, None)

            ahead = XBUFS - 1
            peeled = GROUPS - ahead
            for t in range(peeled):
                step(t, 0, t, *place(t + ahead))
            with sp.Fori(peeled, TILES - GROUPS - ahead) as t:
                t = sp.snap(t)
                step(t, t // GROUPS, t % GROUPS, (t + ahead) // GROUPS, (t + ahead) % GROUPS)
            with sp.Fori(TILES - GROUPS - ahead, TILES - ahead) as t:
                t = sp.snap(t)
                step(t, t // GROUPS, t % GROUPS, BANDS - 1, t - (TILES - GROUPS - ahead))
            for t in range(TILES - ahead, TILES):
                step(t, *place(t), None, None)
            sp.wait_ge(x2_stored, TILES * LOAD)
            sp.wait_ge(stat2_stored, TILES * 32)

        @block.gpsimd
        def _(pool):
            nc.gpsimd.memset(X[:, 2:4], 0.0).then_inc(masks_ready, 1)
            nc.gpsimd.memset(X[:, 4:XBUFS], 0.0).then_inc(x_cleared, 1)
            pool.wait_ge(masks_ready, 1)
            nc.gpsimd.memset(newton[:, 0:1], 0.0).then_inc(x_cleared, 1)
            step = 1
            for dy in range(TAPS):
                pool.wait_ge(masks_ready, step)
                nc.gpsimd.affine_select(out=diag[:, dy], in_=diag[:, dy], compare_op=ALU.not_equal, fill=1.0,
                                        base=1 - dy, pattern=[[-1, 128]], channel_multiplier=1).then_inc(masks_ready, 1)
                step += 1
                for base, cm, pat in ((0, 1, [[-WR, CL], [0, WR]]), (WR - 1, -1, [[WR, CL], [0, WR]])):
                    pool.wait_ge(masks_ready, step)
                    nc.gpsimd.affine_select(out=diag[:, dy].rearrange("p (c r) -> p c r", r=WR),
                                            in_=diag[:, dy].rearrange("p (c r) -> p c r", r=WR),
                                            compare_op=ALU.is_ge, fill=0.0, base=base, pattern=pat,
                                            channel_multiplier=cm).then_inc(masks_ready, 1)
                    step += 1
                for ro in (0, WR - 1):
                    pool.wait_ge(masks_ready, step)
                    nc.gpsimd.memset(diag[:, dy].rearrange("p (c r) -> p c r", r=WR)[:, :, ro], 0.0).then_inc(masks_ready, 1)
                    step += 1
            nc.gpsimd.memset(same_row[:, :], 0.0).then_inc(masks_ready, 1)
            nc.gpsimd.memset(row_mask[:, :], 1.0).then_inc(masks_ready, 1)
            nc.gpsimd.memset(eps1[:, :], LN1_EPS).then_inc(masks_ready, 1)
            step += 3
            for k in range(1 - CL, CL):
                pool.wait_ge(masks_ready, step)
                nc.gpsimd.affine_select(out=same_row[:, :], in_=same_row[:, :], compare_op=ALU.not_equal, fill=1.0 / CH,
                                        base=k * WR, pattern=[[-1, 128]], channel_multiplier=1).then_inc(masks_ready, 1)
                step += 1
            for cl in range(CL):
                for q, r in ((0, 0), (BANDS - 1, WR - 1)):
                    pool.wait_ge(masks_ready, step)
                    nc.gpsimd.affine_select(out=row_mask[:, q:q + 1], in_=row_mask[:, q:q + 1], compare_op=ALU.not_equal,
                                            fill=0.0, base=-(cl * WR + r), pattern=[[0, 1]],
                                            channel_multiplier=1).then_inc(masks_ready, 1)
                    step += 1
            pool.wait_ge(masks_ready, step)
            for ring in (xn_hi, xn_lo, xn_sg):
                for side in (0, PITCH - 1):
                    nc.gpsimd.memset(ring[:, :, :, :, side].bitcast(F32), 0.0).then_inc(pads_zero, 1)

            def mean_of(t):
                return mean1[:, t % XBUFS].unsqueeze(1).broadcast_to([128, SC, TN])

            def center(t, k):
                if k == 0:
                    wait(pool, mean1_ready, t + 1)
                part = X[:, t % XBUFS, SC * k:SC * (k + 1)]
                nc.gpsimd.tensor_tensor(part, part, mean_of(t), ALU.subtract).then_inc(centered, 1)

            def low_part(t, k):
                n = t * SLOTS + k
                wait(pool, hi_ready, n + 1)
                wait(pool, conv_done, BANKS * (n - 1))
                for c in range(SC):
                    i = nc.gpsimd.tensor_tensor(xn_lo[:, k % 2, c, :, 1:1 + WD], xn[:, k % 2, c].rearrange("p (b w) -> p b w", b=BG),
                                                xn_hi[:, k % 2, c, :, 1:1 + WD].bitcast(F32), ALU.subtract)
                i.then_inc(lo_ready, 1)

            def add_mean(t, k):
                n = t * SLOTS + k
                wait(pool, d_added, n + 1)
                wait(pool, sq2_ready, n + 1)
                part = X[:, t % XBUFS, SC * k:SC * (k + 1)]
                nc.gpsimd.tensor_tensor(part, part, mean_of(t), ALU.add).then_inc(x2_ready, 1)

            def tile(t, has_prev, has_next, has_next2):
                for k in range(SLOTS):
                    for work, at in ((add_mean, before(t, k, 2, has_prev)),
                                     (low_part, following(t, k, has_next)),
                                     (center, lead_of(t, k, has_next, has_next2, LEAD + 1))):
                        if at is not None:
                            work(*at)

            for k in range(SLOTS):
                center(0, k)
            for k in range(LEAD + 1):
                center(1, k)
            low_part(0, 0)
            tile(0, False, True, True)
            tile(1, True, True, True)
            with pool.Fori(2, TILES - 2) as t:
                tile(pool.snap(t), True, True, True)
            tile(TILES - 2, True, True, False)
            tile(TILES - 1, True, False, False)
            add_mean(TILES - 1, SLOTS - 2)
            add_mean(TILES - 1, SLOTS - 1)

        @block.scalar
        def _(act):
            act.wait_ge(full_ready, 1)
            nc.scalar.activation(band_sg[:, :, :, :].rearrange("p c d m -> p (c d m)"),
                                 full.rearrange("p c d m -> p (c d m)"), ACT.Sign).then_inc(band_ready, 1)

            def copy_mean(t):
                wait(act, mean1_summed, t + 1)
                wait(act, x2_ready, (t - 3) * SLOTS + 1)
                nc.scalar.activation(mean1[:, t % XBUFS], mean_sum, ACT.Copy).then_inc(mean1_ready, 1)

            def square1(t, k):
                n = t * SLOTS + k
                wait(act, centered, n + 1)
                wait(act, sq1_added, n)
                nc.scalar.activation(sq[:, :, 0:BC * TN], X[:, t % XBUFS, SC * k:SC * (k + 1)].rearrange(
                    "p (b c) n -> p b (c n)", b=BANKS), ACT.Square).then_inc(sq1_ready, 1)

            def seed(t):
                wait(act, var1_summed, t + 1)
                nc.scalar.activation(var_sum, var_sum, ACT.Identity, bias=eps1[:, 0:1]).then_inc(var1_eps, 1)
                wait(act, var1_eps, t + 1)
                nc.scalar.activation(guess[:, :], var_sum, ACT.Abs_reciprocal_sqrt).then_inc(seed_ready, 1)
                wait(act, seed_ready, 2 * t + 1)
                nc.scalar.activation(newton[:, :], guess[:, :], ACT.Square).then_inc(seed_ready, 1)

            def high_part(t, k):
                n = t * SLOTS + k
                wait(act, xn_ready, n + 1)
                wait(act, conv_done, BANKS * (n - 1))
                for c in range(SC):
                    i = nc.scalar.activation(xn_hi[:, k % 2, c, :, 1:1 + WD], xn[:, k % 2, c].rearrange("p (b w) -> p b w", b=BG), ACT.Copy)
                i.then_inc(hi_ready, 1)

            def signs(t, k):
                for c in range(SC):
                    i = nc.scalar.activation(xn_sg[:, k % 2, c, :, 1:1 + WD], xn[:, k % 2, c].rearrange("p (b w) -> p b w", b=BG), ACT.Sign)
                i.then_inc(sg_ready, 1)

            def square2(t, k):
                n = t * SLOTS + k
                wait(act, d_ready, BANKS * (n + 1))
                wait(act, sq2_added, n)
                nc.scalar.activation(sq2b[:, :, 0:BC * TN], X[:, t % XBUFS, SC * k:SC * (k + 1)].rearrange(
                    "p (b c) n -> p b (c n)", b=BANKS), ACT.Square).then_inc(sq2_ready, 1)

            def copy_stats(t):
                wait(act, stat2_summed, t + 1)
                wait(act, var1_summed, min(t + 3, TILES) if isinstance(t, int) else t + 3)
                wait(act, stat2_stored, 32 * t)
                nc.scalar.activation(stat_out[:, :, :], stats2_sum[0:WR], ACT.Copy).then_inc(stat2_ready, 1)

            def tile(t, has_prev, has_next, has_next2):
                for k in range(SLOTS):
                    if k == 1 and has_next2:
                        copy_mean(t + 2)
                    if lead_of(t, k, has_next, has_next2) is not None:
                        square1(*lead_of(t, k, has_next, has_next2))
                    if following(t, k, has_next) is not None:
                        high_part(*following(t, k, has_next))
                        signs(*following(t, k, has_next))
                    if k == 2 and has_prev:
                        copy_stats(t - 1)
                    if k == 2 and has_next:
                        seed(t + 1)
                    if before(t, k, 1, has_prev) is not None:
                        square2(*before(t, k, 1, has_prev))

            copy_mean(0)
            for k in range(SLOTS):
                square1(0, k)
            copy_mean(1)
            seed(0)
            for k in range(LEAD):
                square1(1, k)
            high_part(0, 0)
            signs(0, 0)
            tile(0, False, True, True)
            tile(1, True, True, True)
            with act.Fori(2, TILES - 2) as t:
                tile(act.snap(t), True, True, True)
            tile(TILES - 2, True, True, False)
            tile(TILES - 1, True, False, False)
            square2(TILES - 1, SLOTS - 1)
            copy_stats(TILES - 1)

        @block.vector
        def _(dve):
            nc.vector.memset(X[:, 0:2], 0.0).then_inc(x_cleared, 1)
            dve.wait_ge(w_loaded, 16 * CL)
            dve.wait_ge(masks_ready, 1 + 5 * TAPS)
            n = 0
            for cc in range(CC):
                for dx in range(TAPS):
                    for dy in range(TAPS):
                        w1 = wcol[:, cc, dy * TAPS + dx:dy * TAPS + dx + 1]
                        if dy == 0:
                            i = nc.vector.tensor_scalar(full[:, cc, dx], diag[:, dy], w1, None, ALU.mult)
                        else:
                            dve.wait_ge(rstd_step, n)
                            i = nc.vector.scalar_tensor_tensor(full[:, cc, dx], diag[:, dy], w1, full[:, cc, dx],
                                                               ALU.mult, ALU.add)
                        i.then_inc(rstd_step, 1)
                        n += 1
            base = n
            dve.wait_ge(rstd_step, base)
            nc.vector.tensor_copy(band_hi[:, :, :, :].rearrange("p c d m -> p (c d m)"),
                                  full.rearrange("p c d m -> p (c d m)")).then_inc(full_ready, 1)
            dve.wait_ge(full_ready, 1)
            nc.vector.tensor_tensor(band_lo[:, :, :, :].rearrange("p c d m -> p (c d m)"),
                                    full.rearrange("p c d m -> p (c d m)"),
                                    band_hi[:, :, :, :].rearrange("p c d m -> p (c d m)").bitcast(F32),
                                    ALU.subtract).then_inc(band_ready, 1)
            dve.wait_ge(masks_ready, 1 + 5 * TAPS + 3 + 2 * CL - 1 + 2 * CL)

            def banks(tensor):
                return tensor.rearrange("p (b c) n -> p b (c n)", b=BANKS)

            def add_square1(t, k):
                n = t * SLOTS + k
                wait(dve, sq1_ready, n + 1)
                if k == 0:
                    wait(dve, var1_summed, t - 1)
                    nc.vector.tensor_copy(banks(acc_sq1[:, t % 2]), sq[:, :, 0:BC * TN]).then_inc(sq1_added, 1)
                else:
                    wait(dve, sq1_added, n)
                    nc.vector.tensor_tensor(banks(acc_sq1[:, t % 2]), banks(acc_sq1[:, t % 2]), sq[:, :, 0:BC * TN],
                                            ALU.add).then_inc(sq1_added, 1)

            def finish_rstd(t, q):
                wait(dve, seed_ready, 2 * t + 2)
                nc.vector.tensor_tensor(newton[:, :], newton[:, :], var_sum, ALU.mult).then_inc(rstd_step, 1)
                wait(dve, rstd_step, base + 2 * t + 1)
                nc.vector.tensor_scalar(newton[:, :], newton[:, :], -0.5, 1.5, ALU.mult, ALU.add).then_inc(rstd_step, 1)
                wait(dve, rstd_step, base + 2 * t + 2)
                nc.vector.scalar_tensor_tensor(rstd1[:, t % 2], guess[:, :], row_mask[:, bass.ds(q, 1)], newton[:, :],
                                               ALU.mult, ALU.mult).then_inc(rstd_ready, 1)

            def normalize(t, k):
                n = t * SLOTS + k
                wait(dve, rstd_ready, t + 1)
                wait(dve, sg_ready, n - 1)
                wait(dve, lo_ready, n - 1)
                nc.vector.tensor_tensor(xn[:, k % 2], X[:, t % XBUFS, SC * k:SC * (k + 1)],
                                        rstd1[:, t % 2].unsqueeze(1).broadcast_to([128, SC, TN]), ALU.mult).then_inc(xn_ready, 1)

            def add_conv(t, k, bank):
                n = BANKS * (t * SLOTS + k) + bank
                part = X[:, t % XBUFS, SC * k + BC * bank:SC * k + BC * (bank + 1)].rearrange("p c n -> p (c n)")
                wait(dve, conv_done, n + 1)
                nc.vector.tensor_tensor(part, part, conv[:, bank, 0:BC * TN], ALU.add).then_inc(d_ready, 1)

            def sum_d(t, k):
                n = t * SLOTS + k
                part = X[:, t % XBUFS, SC * k:SC * (k + 1)]
                wait(dve, d_ready, BANKS * (n + 1))
                if k == 0:
                    wait(dve, stat2_summed, t - 1)
                    nc.vector.tensor_scalar(acc_d[:, t % 2], part, 1.0, None, ALU.mult).then_inc(d_added, 1)
                else:
                    wait(dve, d_added, n)
                    nc.vector.tensor_tensor(acc_d[:, t % 2], acc_d[:, t % 2], part, ALU.add).then_inc(d_added, 1)

            def add_square2(t, k):
                n = t * SLOTS + k
                wait(dve, sq2_ready, n + 1)
                if k == 0:
                    wait(dve, stat2_summed, t - 1)
                    nc.vector.tensor_copy(banks(acc_sq2[:, t % 2]), sq2b[:, :, 0:BC * TN]).then_inc(sq2_added, 1)
                else:
                    wait(dve, sq2_added, n)
                    nc.vector.tensor_tensor(banks(acc_sq2[:, t % 2]), banks(acc_sq2[:, t % 2]), sq2b[:, :, 0:BC * TN],
                                            ALU.add).then_inc(sq2_added, 1)

            def tile(t, q_next, has_prev, has_next, has_next2):
                for k in range(SLOTS):
                    ahead, stat = following(t, k, has_next), lead_of(t, k, has_next, has_next2)
                    last, last2 = before(t, k, 1, has_prev), before(t, k, 2, has_prev)
                    if ahead is not None:
                        normalize(*ahead)
                    if last is not None:
                        add_conv(*last, 1)
                        sum_d(*last)
                    if last2 is not None:
                        add_square2(*last2)
                    if stat is not None:
                        add_square1(*stat)
                    add_conv(t, k, 0)
                    if k == 2 and has_next:
                        finish_rstd(t + 1, q_next)

            for k in range(SLOTS):
                add_square1(0, k)
            finish_rstd(0, 0)
            for k in range(LEAD):
                add_square1(1, k)
            normalize(0, 0)
            tile(0, 0, False, True, True)
            tile(1, 0, True, True, True)
            with dve.Fori(2, TILES - 2) as t:
                t = dve.snap(t)
                tile(t, dve.snap((t + 1) // GROUPS), True, True, True)
            tile(TILES - 2, BANDS - 1, True, True, False)
            tile(TILES - 1, None, True, False, False)
            add_conv(TILES - 1, SLOTS - 1, 1)
            sum_d(TILES - 1, SLOTS - 1)
            add_square2(TILES - 1, SLOTS - 2)
            add_square2(TILES - 1, SLOTS - 1)

        @block.tensor
        def _(pe):
            pe.wait_ge(masks_ready, 1 + 5 * TAPS + 3 + 2 * CL - 1)

            MEAN_PARTS = (0, 4, 10, CC)

            def sum_mean(t, part):
                if part == 0:
                    wait(pe, tile_in, t + 1)
                    wait(pe, mean1_ready, t)
                    wait(pe, stat2_ready, t - 3)
                for c in range(MEAN_PARTS[part], MEAN_PARTS[part + 1]):
                    i = nc.tensor.matmul(mean_sum, same_row[:, :], X[:, t % XBUFS, c], start=c == 0, stop=c == CC - 1)
                if part == len(MEAN_PARTS) - 2:
                    i.then_inc(mean1_summed, 1)

            def sum_var(t):
                wait(pe, sq1_added, (t + 1) * SLOTS)
                wait(pe, rstd_ready, t)
                wait(pe, stat2_ready, t - 2)
                for c in range(SC):
                    i = nc.tensor.matmul(var_sum, same_row[:, :], acc_sq1[:, t % 2, c], start=c == 0, stop=c == SC - 1)
                i.then_inc(var1_summed, 1)

            def sum_stats2(t):
                wait(pe, sq2_added, (t + 1) * SLOTS)
                wait(pe, d_added, (t + 1) * SLOTS)
                wait(pe, stat2_ready, t)
                wait(pe, mean1_ready, min(t + 4, TILES) if isinstance(t, int) else t + 4)
                wait(pe, rstd_ready, min(t + 2, TILES) if isinstance(t, int) else t + 2)
                for c in range(SC):
                    nc.tensor.matmul(stats2_sum[:, 0], same_row[:, :], acc_d[:, t % 2, c], start=c == 0, stop=c == SC - 1)
                for c in range(SC):
                    i = nc.tensor.matmul(stats2_sum[:, 1], same_row[:, :], acc_sq2[:, t % 2, c], start=c == 0, stop=c == SC - 1)
                i.then_inc(stat2_summed, 1)

            def convolve(t, k):
                n = t * SLOTS + k
                wait(pe, sg_ready, n + 1)
                wait(pe, lo_ready, n + 1)
                for c in range(SC):
                    bank, at = c // BC, c % BC * TN
                    if c % BC == 0:
                        wait(pe, d_ready, BANKS * (n - 1) + bank + 1)
                    todo = [(m, ring, dx) for dx in range(TAPS)
                            for m, ring in ((band_sg, xn_hi), (band_sg, xn_lo), (band_hi, xn_sg), (band_lo, xn_sg))]
                    for j, (m, ring, dx) in enumerate(todo):
                        i = nc.tensor.matmul(conv[:, bank, at:at + TN], m[:, SC * k + c, dx], ring[:, k % 2, c, :, dx:dx + WD],
                                             start=j == 0, stop=j == len(todo) - 1)
                    if c % BC == BC - 1:
                        i.then_inc(conv_done, 1)

            def tile(t, has_prev, has_next, has_next2, has_next3):
                for k in range(SLOTS):
                    convolve(t, k)
                    if k == 0 and has_next2:
                        sum_mean(t + 2, 2)
                    if k == 1 and has_prev:
                        sum_stats2(t - 1)
                    if k == 1 and has_next:
                        sum_var(t + 1)
                    if k >= 2 and has_next3:
                        sum_mean(t + 3, k - 2)

            for t in range(3):
                for part in range(3 if t < 2 else 2):
                    sum_mean(t, part)
                if t == 0:
                    sum_var(0)
            pe.wait_ge(band_ready, 2)
            pe.wait_ge(full_ready, 1)
            pe.wait_ge(pads_zero, 6)
            tile(0, False, True, True, True)
            tile(1, True, True, True, True)
            with pe.Fori(2, TILES - 3) as t:
                tile(pe.snap(t), True, True, True, True)
            tile(TILES - 3, True, True, True, False)
            tile(TILES - 2, True, True, False, False)
            tile(TILES - 1, True, False, False, False)
            sum_stats2(TILES - 1)


STEPS = 8
BLOCKS = WD // STEPS
QUAD = 4
IMG_GROUPS = 2
IMGS = NB // IMG_GROUPS
COLS = IMGS * BANDS
PARTS = 3
HALF = BLOCKS // 2
WINDOW_BUFS = 3
TOLERANCE = 2.0 ** -22


def rstd_phase(nc, stat2, rparts):
    with ExitStack() as ctx:
        def sb(name, shape, dt=F32):
            return ctx.enter_context(nc.sbuf_tensor(name, shape, dt))

        def sem(name):
            return ctx.enter_context(nc.semaphore(name))

        moments = sb("moments", [COLS, 2, IMG_GROUPS, BR, WD])
        rstd = sb("rstd", [COLS, IMG_GROUPS, BR, WD])
        work = sb("work", [COLS, IMG_GROUPS, BR, WD])
        ident = sb("ident_r", [128, 128])
        left = sb("left", [WD, BR * IMG_GROUPS, COLS])
        part = [sb(f"part{i}", [WD, BR * IMG_GROUPS, COLS], BF16) for i in range(PARTS)]
        per_bank = 512 // COLS
        banks = BR * IMG_GROUPS // per_bank
        turned = ctx.enter_context(nc.psum_tensor("turned", [WD, banks, per_bank, COLS], F32))
        loaded, ident_ready, squared, var_ready, seeded = (sem(n) for n in ("loaded", "ident_ready", "squared", "var_ready", "seeded"))
        step, rstd_ready, turned_ready, left_ready, parts_stored = (sem(n) for n in ("step", "rstd_done", "turned_ready", "left_ready", "parts_stored"))
        part_ready = sem("part_ready")
        block = ctx.enter_context(nc.Block())
        flat = lambda t: t.rearrange("p g r w -> p (g r w)")

        @block.sync
        def _(sp):
            src = stat2.rearrange("s r (g b) q w -> s g (b q) r w", g=IMG_GROUPS)
            for s in range(2):
                for g in range(IMG_GROUPS):
                    sp.dma_start(moments[:, s, g], src[s, g]).then_inc(loaded, 16)
            dst = rparts.rearrange("r g p j s c -> p (j s) (r g) c")
            for i in range(PARTS):
                sp.wait_ge(part_ready, 1 + i)
                sp.dma_start(dst[i], part[i][:, :, :]).then_inc(parts_stored, 16)
            sp.wait_ge(parts_stored, 16 * PARTS)

        @block.gpsimd
        def _(pool):
            nc.gpsimd.memset(ident[:, :], 0.0).then_inc(ident_ready, 1)
            pool.wait_ge(ident_ready, 1)
            nc.gpsimd.affine_select(out=ident[:, :], in_=ident[:, :], compare_op=ALU.not_equal, fill=1.0, base=0,
                                    pattern=[[-1, 128]], channel_multiplier=1).then_inc(ident_ready, 1)

        @block.scalar
        def _(act):
            act.wait_ge(loaded, 16 * 4)
            nc.scalar.activation(flat(work[:, :, :, :]), flat(moments[:, 0]), ACT.Square).then_inc(squared, 1)
            act.wait_ge(var_ready, 1)
            nc.scalar.activation(flat(rstd[:, :, :, :]), flat(moments[:, 1]), ACT.Abs_reciprocal_sqrt).then_inc(seeded, 1)
            act.wait_ge(seeded, 1)
            nc.scalar.activation(flat(work[:, :, :, :]), flat(rstd[:, :, :, :]), ACT.Square).then_inc(seeded, 1)

        @block.vector
        def _(dve):
            dve.wait_ge(squared, 1)
            nc.vector.scalar_tensor_tensor(flat(moments[:, 1]), flat(moments[:, 1]), LN2_EPS, flat(work[:, :, :, :]),
                                           ALU.add, ALU.subtract).then_inc(var_ready, 1)
            dve.wait_ge(seeded, 2)
            nc.vector.tensor_tensor(flat(work[:, :, :, :]), flat(work[:, :, :, :]), flat(moments[:, 1]), ALU.mult).then_inc(step, 1)
            dve.wait_ge(step, 1)
            nc.vector.tensor_scalar(flat(work[:, :, :, :]), flat(work[:, :, :, :]), -0.5, 1.5, ALU.mult, ALU.add).then_inc(step, 1)
            dve.wait_ge(step, 2)
            nc.vector.tensor_tensor(flat(rstd[:, :, :, :]), flat(rstd[:, :, :, :]), flat(work[:, :, :, :]), ALU.mult).then_inc(rstd_ready, 1)
            dve.wait_ge(turned_ready, 1)
            rows = left[:, :, :].rearrange("p n c -> p (n c)")
            nc.vector.tensor_copy(left[:, :, :].rearrange("p (k n) c -> p k (n c)", k=banks),
                                  turned[:, :, :, :].rearrange("p k n c -> p k (n c)")).then_inc(left_ready, 1)
            for i in range(PARTS):
                dve.wait_ge(left_ready, 1 + i)
                to = part[i][:, :, :].rearrange("p n c -> p (n c)")
                nc.vector.tensor_copy(to, rows).then_inc(part_ready, 1)
                if i < PARTS - 1:
                    dve.wait_ge(part_ready, 1 + i)
                    nc.vector.tensor_tensor(rows, rows, to, ALU.subtract).then_inc(left_ready, 1)

        @block.tensor
        def _(pe):
            pe.wait_ge(ident_ready, 2)
            pe.wait_ge(rstd_ready, 1)
            for n in range(BR * IMG_GROUPS):
                r, g = n // IMG_GROUPS, n % IMG_GROUPS
                i = nc.tensor.transpose(turned[:, n // per_bank, n % per_bank], rstd[:, g, r], ident[:, :])
            i.then_inc(turned_ready, 1)



def window_loader(x2, rparts, X, R):
    x2_win = x2.rearrange("c r (g b) q w -> r g c (b q) w", g=IMG_GROUPS)
    r_win = rparts.rearrange("r g p j s c -> r g p s j c")

    def load(sp, row, g, buf, done):
        sp.dma_start(X[:, buf], x2_win[bass.ds(row, 1), g][0]).then_inc(done, 16)
        for p in range(PARTS):
            sp.dma_start(R[p * STEPS:(p + 1) * STEPS, buf], r_win[bass.ds(row, 1), g, p][0]).then_inc(done, 16)

    return load, x2_win, r_win


WINDOW_INC = 16 * (1 + PARTS)


def pool_constants(nc, pool, R, pick, pick_ready):
    nc.gpsimd.memset(R.rearrange("p k j c -> p (k j c)"), 0.0).then_inc(pick_ready, 1)
    nc.gpsimd.memset(pick.rearrange("p s m -> p (s m)"), 0.0).then_inc(pick_ready, 1)
    for part in range(PARTS):
        pool.wait_ge(pick_ready, 2 + part)
        nc.gpsimd.affine_select(out=pick, in_=pick, compare_op=ALU.not_equal, fill=1.0, base=-part * STEPS,
                                pattern=[[-1, STEPS], [0, 128]], channel_multiplier=1).then_inc(pick_ready, 1)


PICK_READY = 2 + PARTS


def statistics_phase(nc, x2, rparts, W, V, gamma, beta, wT, vT, bias_q):
    with ExitStack() as ctx:
        def sb(name, shape, dt=F32):
            return ctx.enter_context(nc.sbuf_tensor(name, shape, dt))

        def sem(name):
            return ctx.enter_context(nc.semaphore(name))

        quads = WD // QUAD
        total = BR * IMG_GROUPS * quads
        X = sb("X_stat", [128, IMG_GROUPS, COLS, WD])
        R = sb("R_stat", [128, IMG_GROUPS, BLOCKS, COLS], BF16)
        T = sb("T_stat", [128, 2, QUAD, COLS])
        pick = sb("pick_stat", [128, STEPS, 128], BF16)
        parts = sb("bn_parts", [128, total * 6])
        w_in, v_in, ident = sb("w_in", [128, 128]), sb("v_in", [128, 128]), sb("ident", [128, 128])
        small = sb("small", [128, 8])
        gam, bet, row_mean, scale, eps = (small[:, i:i + 1] for i in range(5))
        moments = small[:, 5:7]
        RB = ctx.enter_context(nc.psum_tensor("RB_stat", [128, 2, QUAD, COLS], F32))
        Q = ctx.enter_context(nc.psum_tensor("Q", [128, 2, QUAD, COLS], F32))
        turned = ctx.enter_context(nc.psum_tensor("turned_w", [128, 3, 128], F32))

        params_in, pick_ready, ident_ready = sem("params_in"), sem("pick_ready"), sem("ident_ready_s")
        w_in_x = [sem(f"window_in{g}") for g in range(IMG_GROUPS)]
        spread_done, scaled, projected, measured = sem("spread_done"), sem("scaled"), sem("projected"), sem("measured")
        w_centered, turned_ready, wT_ready, vT_ready = sem("w_centered"), sem("turned_w_ready"), sem("wT_ready"), sem("vT_ready")
        bn_step, std_ready = sem("bn_step"), sem("std_ready")
        load, _, _ = window_loader(x2, rparts, X, R)
        block = ctx.enter_context(nc.Block())

        def run_windows(eng, body):
            body(0, 0, 0, True)
            with eng.Fori(1, BLOCKS) as j:
                body(0, 0, eng.snap(j), False)
            body(0, 1, 0, False)
            with eng.Fori(1, BLOCKS) as j:
                body(0, 1, eng.snap(j), False)
            with eng.Fori(1, BR) as row:
                row = eng.snap(row)
                for g in range(IMG_GROUPS):
                    body(row, g, 0, False)
                    with eng.Fori(1, BLOCKS) as j:
                        body(row, g, eng.snap(j), False)

        def quad_index(row, g, j, i):
            return (row * IMG_GROUPS + g) * quads + 2 * j + i

        @block.sync
        def _(sp):
            for dst, src in ((w_in[:, :], W), (v_in[:, :], V), (gam, gamma.unsqueeze(1)), (bet, beta.unsqueeze(1))):
                sp.dma_start(dst, src).then_inc(params_in, 16)
            sp.wait_ge(pick_ready, 1)
            for g in range(IMG_GROUPS):
                load(sp, 0, g, g, w_in_x[g])
            with sp.Fori(1, BR) as row:
                row = sp.snap(row)
                for g in range(IMG_GROUPS):
                    through = sp.snap(quad_index(row - 1, g, BLOCKS, 0))
                    sp.wait_ge(scaled, through)
                    sp.wait_ge(params_in, 64)
                    load(sp, row, g, g, w_in_x[g])

        @block.gpsimd
        def _(pool):
            pool_constants(nc, pool, R[:, :, :, :], pick[:, :, :], pick_ready)
            nc.gpsimd.memset(ident[:, :], 0.0).then_inc(ident_ready, 1)
            pool.wait_ge(ident_ready, 1)
            nc.gpsimd.affine_select(out=ident[:, :], in_=ident[:, :], compare_op=ALU.not_equal, fill=1.0, base=0,
                                    pattern=[[-1, 128]], channel_multiplier=1).then_inc(ident_ready, 1)
            nc.gpsimd.memset(eps, BN_EPS).then_inc(ident_ready, 1)

        @block.scalar
        def _(act):
            act.wait_ge(bn_step, 1)
            act.wait_ge(ident_ready, 3)
            nc.scalar.activation(scale, moments[:, 1:2], ACT.Sqrt, bias=eps).then_inc(std_ready, 1)

        @block.vector
        def _(dve):
            dve.wait_ge(params_in, 64)
            nc.vector.tensor_reduce(row_mean, w_in[:, :], axis=AX.X, op=ALU.add).then_inc(w_centered, 1)
            dve.wait_ge(w_centered, 1)
            nc.vector.tensor_scalar(row_mean, row_mean, 1.0 / CH, None, ALU.mult).then_inc(w_centered, 1)
            dve.wait_ge(w_centered, 2)
            nc.vector.tensor_scalar(w_in[:, :], w_in[:, :], row_mean, None, ALU.subtract).then_inc(w_centered, 1)
            dve.wait_ge(turned_ready, 1)
            nc.vector.tensor_copy(wT, turned[:, 0]).then_inc(wT_ready, 1)
            nc.vector.tensor_copy(vT, turned[:, 1]).then_inc(vT_ready, 1)

            def body(row, g, j, first):
                for i in range(2):
                    n = quad_index(row, g, j, i)
                    if isinstance(j, int) and i == 0:
                        wait(dve, w_in_x[g], (row + 1) * WINDOW_INC)
                    wait(dve, spread_done, n + 1)
                    wait(dve, projected, n - 1)
                    src = X[:, g, :, bass.ds(j * STEPS + i * QUAD, QUAD)].rearrange("p c s -> p s c")
                    nc.vector.tensor_tensor(T[:, i], src, RB[:, i], ALU.mult).then_inc(scaled, 1)
                    if not first:
                        nc.vector.bn_stats(parts[:, bass.ds(6 * (n - 2), 6)], Q[:, i].rearrange("p s c -> p (s c)")).then_inc(measured, 1)

            run_windows(dve, body)
            for n in (total - 2, total - 1):
                dve.wait_ge(projected, n + 1)
                nc.vector.bn_stats(parts[:, 6 * n:6 * n + 6], Q[:, n % 2].rearrange("p s c -> p (s c)")).then_inc(measured, 1)
            dve.wait_ge(measured, total)
            nc.vector.bn_aggr(moments, parts[:, :]).then_inc(bn_step, 1)
            dve.wait_ge(std_ready, 1)
            nc.vector.reciprocal(scale, scale).then_inc(bn_step, 1)
            dve.wait_ge(bn_step, 2)
            nc.vector.tensor_tensor(scale, scale, gam, ALU.mult).then_inc(bn_step, 1)
            dve.wait_ge(bn_step, 3)
            nc.vector.tensor_tensor(row_mean, moments[:, 0:1], scale, ALU.mult).then_inc(bn_step, 1)
            nc.vector.tensor_scalar(w_in[:, :], w_in[:, :], scale, None, ALU.mult).then_inc(w_centered, 1)
            dve.wait_ge(bn_step, 4)
            nc.vector.tensor_tensor(bias_q, bet, row_mean, ALU.subtract).then_inc(bn_step, 1)
            dve.wait_ge(turned_ready, 2)
            nc.vector.tensor_copy(wT, turned[:, 2]).then_inc(wT_ready, 1)
            dve.wait_ge(wT_ready, 2)
            dve.wait_ge(bn_step, 5)

        @block.tensor
        def _(pe):
            pe.wait_ge(ident_ready, 2)
            pe.wait_ge(w_centered, 3)
            nc.tensor.transpose(turned[:, 0], w_in[:, :], ident[:, :])
            nc.tensor.transpose(turned[:, 1], v_in[:, :], ident[:, :]).then_inc(turned_ready, 1)
            pe.wait_ge(pick_ready, PICK_READY)
            pe.wait_ge(wT_ready, 1)

            def project(i, n):
                nc.tensor.matmul(Q[:, i].rearrange("p s c -> p (s c)"), wT, T[:, i].rearrange("p s c -> p (s c)"),
                                 start=True, stop=True).then_inc(projected, 1)

            def body(row, g, j, first):
                for i in range(2):
                    n = quad_index(row, g, j, i)
                    if isinstance(j, int) and i == 0:
                        wait(pe, w_in_x[g], (row + 1) * WINDOW_INC)
                    wait(pe, scaled, n - 1)
                    for s in range(QUAD):
                        x = nc.tensor.matmul(RB[:, i, s], pick[:, QUAD * i + s], R[:, g, j], start=s == 0, stop=s == QUAD - 1)
                    x.then_inc(spread_done, 1)
                    if first and i == 0:
                        continue
                    wait(pe, scaled, n)
                    wait(pe, measured, n - 2)
                    project(1 - i, n - 1)

            run_windows(pe, body)
            pe.wait_ge(scaled, total)
            pe.wait_ge(measured, total - 2)
            project(1, total - 1)
            pe.wait_ge(w_centered, 4)
            nc.tensor.transpose(turned[:, 2], w_in[:, :], ident[:, :]).then_inc(turned_ready, 1)


def scan_phase(nc, x2, rparts, wT, vT, bias_q, out):
    with ExitStack() as ctx:
        def sb(name, shape, dt=F32):
            return ctx.enter_context(nc.sbuf_tensor(name, shape, dt))

        def sem(name):
            return ctx.enter_context(nc.semaphore(name))

        X = sb("X_scan", [128, WINDOW_BUFS, COLS, WD])
        R = sb("R_scan", [128, WINDOW_BUFS, BLOCKS, COLS], BF16)
        T = sb("T_scan", [128, IMG_GROUPS, 2, QUAD, COLS])
        Y = sb("Y", [128, IMG_GROUPS, STEPS, COLS])
        pick = sb("pick_scan", [128, STEPS, 128], BF16)
        y_warm = sb("y_warm", [128, IMG_GROUPS, COLS])
        small = sb("small_scan", [128, 4])
        ones, agreed = small[:, 0:1], small[:, 1:3]
        verdict = sb("verdict", [1, 1], I32)
        Z = ctx.enter_context(nc.psum_tensor("Z", [128, IMG_GROUPS, 2, QUAD, COLS], F32))
        RB = ctx.enter_context(nc.psum_tensor("RB_scan", [128, IMG_GROUPS, 2, QUAD, COLS], F32))

        pick_ready, y_zero = sem("pick_ready_c"), sem("y_zero")
        both = range(IMG_GROUPS)
        window_in, spread_done, scaled, summed, y_ready, added = (
            [sem(f"{name}{g}") for g in both] for name in ("win_in", "spread", "scaled_c", "summed", "y_ready", "added"))
        restarted, out_stored = sem("restarted"), sem("out_stored")
        warm_kept, check_step, check_summed, verdict_in = sem("warm_kept"), sem("check_step"), sem("check_summed"), sem("verdict_in")
        q_in, q_spread, q_scaled, q_summed, q_y, q_added, q_out = (
            sem(n) for n in ("q_in", "q_spread", "q_scaled", "q_summed", "q_y", "q_added", "q_out"))
        load, x2_win, r_win = window_loader(x2, rparts, X, R)
        out_win = out.rearrange("b c (q r) w -> r b c q w", r=BR)
        block = ctx.enter_context(nc.Block())

        UNITS = 2 * BR + 2

        def alive(u):
            return tuple(g for g in both if g <= u <= UNITS - 2 + g)

        def run_units(eng, unit):
            for u in (0, 1):
                unit(u, u % 2, alive(u), alive(u + 1))
            with eng.Fori(1, BR) as k:
                k = eng.snap(k)
                unit(eng.snap(2 * k), 0, (0, 1), (0, 1))
                unit(eng.snap(2 * k + 1), 1, (0, 1), (0, 1))
            for u in (UNITS - 2, UNITS - 1):
                unit(u, u % 2, alive(u), alive(u + 1))

        def run_bodies(eng, u, parity, groups, then, body, before_last=None):
            def place(u, parity, g, b):
                window = (u + 1 - g) // 2
                return (IMG_GROUPS * window + g) % WINDOW_BUFS, (parity + 1 - g) % 2 * HALF + b

            def one(b, last):
                m = {g: (u - g) * HALF + b for g in sorted({*groups, *(then if last else ())})}
                now = {g: place(u, parity, g, b) for g in groups}
                if last:
                    after = {g: place(u + 1, 1 - parity, g, 0) for g in then}
                else:
                    after = {g: place(u, parity, g, b + 1) for g in groups}
                body(m, now, after)

            with eng.Fori(0, HALF - 1) as b:
                one(eng.snap(b), False)
            if before_last is not None:
                before_last()
            one(HALF - 1, True)

        def wait_window(eng, u, parity, then):
            if parity in then:
                wait(eng, window_in[parity], WINDOW_INC + WINDOW_INC * ((u + 2 - parity) // 2))
            if isinstance(u, int) and u == 0:
                wait(eng, window_in[1], WINDOW_INC)


        x_row = X[:, 0, 0:NB]
        t_seq = T[:, 0, 0].rearrange("p s c -> p (s c)")[:, 0:STEPS * NB].rearrange("p (s b) -> p s b", b=NB)
        y_seq = Y[:, 0].rearrange("p s c -> p (s c)")[:, 0:STEPS * NB].rearrange("p (s b) -> p s b", b=NB)
        z_seq = Z[:, 0, 0].rearrange("p s c -> p (s c)")[:, 0:STEPS * NB].rearrange("p (s b) -> p s b", b=NB)
        r_seq = RB[:, 0, 0].rearrange("p s c -> p (s c)")[:, 0:STEPS * NB].rearrange("p (s b) -> p s b", b=NB)
        ROW_INC = 16 * (1 + IMG_GROUPS * PARTS)

        def rows_in_time(eng, row_of, body):
            with eng.Fori(0, BANDS) as q:
                q = eng.snap(q)
                with eng.Fori(0, BR) as r:
                    r = eng.snap(r)
                    n = eng.snap(q * BR + r)
                    row_of(n, q, r)
                    if body is not None:
                        with eng.Fori(0, BLOCKS) as j:
                            j = eng.snap(j)
                            body(eng.snap(n * BLOCKS + j), n, q, j)

        def one_by_one_sync(sp):
            src = x2.rearrange("c r b q w -> r q c b w")
            dst = out.rearrange("b c (q r) w -> q r c b w", r=BR)

            def row(n, q, r):
                before, through = sp.snap(n * 16 + 16), sp.snap((n + 1) * BLOCKS + 1)
                sp.wait_ge(q_out, before)
                sp.wait_ge(pick_ready, 1)
                sp.dma_start(x_row, src[bass.ds(r, 1), bass.ds(q, 1)][0, 0]).then_inc(q_in, 16)
                for g in both:
                    for p in range(PARTS):
                        sp.dma_start(R[p * STEPS:(p + 1) * STEPS, g], r_win[bass.ds(r, 1), g, p][0]).then_inc(q_in, 16)
                sp.wait_ge(q_added, through)
                sp.wait_ge(pick_ready, 1)
                sp.dma_start(dst[bass.ds(q, 1), bass.ds(r, 1)][0, 0], x_row).then_inc(q_out, 16)

            sp.dma_start(R[0:1, 2, 0], R[0:1, 1, 0]).then_inc(q_out, 16)
            rows_in_time(sp, row, None)
            sp.wait_ge(q_out, (HT + 1) * 16)

        def one_by_one_scalar(act):
            def body(m, n, q, j):
                for s in range(STEPS):
                    if s == 0:
                        act.wait_ge(q_added, m + 1)
                    act.wait_ge(q_summed, m * STEPS + s + 1)
                    nc.scalar.activation(y_seq[:, s], z_seq[:, s], ACT.Sigmoid, bias=bias_q).then_inc(q_y, 1)
            rows_in_time(act, lambda n, q, r: None, body)

        def one_by_one_vector(dve):
            nc.vector.memset(y_seq[:, STEPS - 1], 0.0).then_inc(q_y, 1)
            nc.vector.memset(small[:, 3:4], 0.0).then_inc(q_added, 1)

            def body(m, n, q, j):
                part = x_row[:, :, bass.ds(j * STEPS, STEPS)]
                dve.wait_ge(q_in, (n + 1) * ROW_INC)
                dve.wait_ge(q_spread, m + 1)
                nc.vector.tensor_tensor(t_seq, part.rearrange("p b s -> p s b"), r_seq, ALU.mult).then_inc(q_scaled, 1)
                dve.wait_ge(q_y, (m + 1) * STEPS + 1)
                nc.vector.tensor_tensor(part, part, y_seq.rearrange("p s b -> p b s"), ALU.add).then_inc(q_added, 1)
            rows_in_time(dve, lambda n, q, r: None, body)

        def one_by_one_tensor(pe):
            def body(m, n, q, j):
                pe.wait_ge(q_in, (n + 1) * ROW_INC)
                pe.wait_ge(q_added, m + 1)
                for s in range(STEPS):
                    for g in both:
                        of_band = R[:, g, bass.ds(j, 1)][:, 0].rearrange("p (b q) -> p q b", q=BANDS)[:, bass.ds(q, 1)][:, 0]
                        x = nc.tensor.matmul(r_seq[:, s, g * IMGS:(g + 1) * IMGS], pick[:, s], of_band, start=True, stop=True)
                x.then_inc(q_spread, 1)
                pe.wait_ge(q_scaled, m + 1)
                nc.tensor.matmul(z_seq.rearrange("p s b -> p (s b)"), wT, t_seq.rearrange("p s b -> p (s b)"),
                                 start=True, stop=False, skip_group_check=True)
                for s in range(STEPS):
                    pe.wait_ge(q_y, m * STEPS + s + 1)
                    nc.tensor.matmul(z_seq[:, s], vT, y_seq[:, (s - 1) % STEPS], start=False, stop=True,
                                     skip_group_check=True).then_inc(q_summed, 1)
            rows_in_time(pe, lambda n, q, r: None, body)

        @block.sync
        def _(sp):
            sp.wait_ge(pick_ready, 1)
            for g in both:
                src, half = x2_win[BR - 1, g], WD // 2
                sp.dma_start(X[:, g, 1:COLS, half:WD], src[:, 0:COLS - 1, half:WD]).then_inc(window_in[g], 16)
                for p in range(PARTS):
                    r, rows = r_win[BR - 1, g, p], slice(p * STEPS, (p + 1) * STEPS)
                    sp.dma_start(R[rows, g, HALF:BLOCKS, 1:COLS], r[:, HALF:BLOCKS, 0:COLS - 1]).then_inc(window_in[g], 16)
            sp.wait_ge(scaled[0], 1)
            load(sp, 0, 0, 2, window_in[0])

            def window_through(w, g, refill):
                held = (lambda v: v) if isinstance(w, int) else sp.snap
                buf = held((IMG_GROUPS * w + g) % WINDOW_BUFS)
                through, stored = held(2 * (HALF + BLOCKS * w)), held((IMG_GROUPS * w + g - 1) * IMGS * 16)
                sp.wait_ge(added[g], through)
                sp.wait_ge(pick_ready, 1)
                if not isinstance(w, int) or w > 0:
                    for b in range(IMGS):
                        src = X[:, bass.ds(buf, 1), b * BANDS:(b + 1) * BANDS][:, 0]
                        sp.dma_start(out_win[bass.ds(w - 1, 1), g * IMGS + b][0], src).then_inc(out_stored, 16)
                if refill:
                    wait(sp, out_stored, stored)
                    sp.wait_ge(pick_ready, 1)
                    load(sp, w + g, 1 - g, buf, window_in[1 - g])

            window_through(0, 0, True)
            window_through(0, 1, True)
            with sp.Fori(1, BR - 1) as w:
                w = sp.snap(w)
                for g in both:
                    window_through(w, g, True)
            for w in (BR - 1, BR):
                for g in both:
                    window_through(w, g, w == BR - 1 and g == 0)
            sp.wait_ge(out_stored, BR * NB * 16)
            sp.wait_ge(verdict_in, 1)
            bad = sp.value_load(verdict[0:1, 0:1], min_val=0, max_val=1 << 20)
            with sp.If(bad > 0):
                one_by_one_sync(sp)
            sp.wait_ge(verdict_in, 1)

        @block.gpsimd
        def _(pool):
            pool_constants(nc, pool, R[:, :, :, :], pick[:, :, :], pick_ready)
            nc.gpsimd.memset(Y[:, :, STEPS - 1], 0.0).then_inc(y_zero, 1)
            nc.gpsimd.memset(ones, 1.0).then_inc(y_zero, 1)
            nc.gpsimd.memset(X[:, 0:IMG_GROUPS, 0, WD // 2:WD], 0.0).then_inc(y_zero, 1)

        @block.scalar
        def _(act):
            def body(m, now, after):
                for s in range(STEPS):
                    for g in now:
                        if s % QUAD == 0:
                            wait(act, added[g], 2 * m[g] + s // QUAD - 1)
                        wait(act, summed[g], m[g] * STEPS + s + 1)
                        nc.scalar.activation(Y[:, g, s], Z[:, g, s // QUAD, s % QUAD], ACT.Sigmoid, bias=bias_q).then_inc(y_ready[g], 1)

            def unit(u, parity, groups, then):
                with_first = isinstance(u, int) and u < IMG_GROUPS
                if with_first:
                    m = {g: (u - g) * HALF for g in groups}
                    body(m, groups, ())
                    with act.Fori(1, HALF) as b:
                        b = act.snap(b)
                        body({g: (u - g) * HALF + b for g in groups}, groups, ())
                else:
                    with act.Fori(0, HALF) as b:
                        b = act.snap(b)
                        body({g: (u - g) * HALF + b for g in groups}, groups, ())

            run_units(act, unit)
            act.wait_ge(verdict_in, 1)
            bad = act.value_load(verdict[0:1, 0:1], min_val=0, max_val=1 << 20)
            with act.If(bad > 0):
                one_by_one_scalar(act)
            act.wait_ge(verdict_in, 1)

        @block.vector
        def _(dve):
            def scale(g, m_next, place, i):
                buf, j = place
                wait(dve, spread_done[g], 2 * m_next + i + 1)
                src = X[:, buf, :, bass.ds(j * STEPS + i * QUAD, QUAD)].rearrange("p c s -> p s c")
                nc.vector.tensor_tensor(T[:, g, i], src, RB[:, g, i], ALU.mult).then_inc(scaled[g], 1)

            def add_states(g, m, place, i):
                buf, j = place
                wait(dve, y_ready[g], m * STEPS + (i + 1) * QUAD)
                part = X[:, buf, :, bass.ds(j * STEPS + i * QUAD, QUAD)]
                nc.vector.tensor_tensor(part, part, Y[:, g, i * QUAD:(i + 1) * QUAD].rearrange("p s c -> p c s"),
                                        ALU.add).then_inc(added[g], 1)

            def body(m, now, after):
                for i in range(2):
                    for g in after:
                        scale(g, m[g] + 1, after[g], i)
                    for g in now:
                        add_states(g, m[g], now[g], i)

            def unit(u, parity, groups, then):
                run_bodies(dve, u, parity, groups, then, body, lambda: wait_window(dve, u, parity, then))
                if isinstance(u, int) and u < IMG_GROUPS:
                    last = Y[:, u, STEPS - 1]
                    nc.vector.tensor_copy(y_warm[:, u], last).then_inc(warm_kept, 1)
                    dve.wait_ge(warm_kept, u + 1)
                    nc.vector.memset(last.rearrange("p (b q) -> p b q", q=BANDS)[:, :, 0:1], 0.0).then_inc(restarted, 1)

            dve.wait_ge(y_zero, 3)
            dve.wait_ge(window_in[0], WINDOW_INC)
            body({0: -1}, {}, {0: (0, HALF)})
            run_units(dve, unit)

            diff = T[:, 0].rearrange("p k s c -> p (k s c)")[:, 0:IMG_GROUPS * IMGS * (BANDS - 1)].rearrange(
                "p (g b q) -> p g b q", g=IMG_GROUPS, b=IMGS)
            for g in both:
                nc.vector.tensor_tensor(diff[:, g], Y[:, g, STEPS - 1].rearrange("p (b q) -> p b q", q=BANDS)[:, :, 0:BANDS - 1],
                                        y_warm[:, g].rearrange("p (b q) -> p b q", q=BANDS)[:, :, 1:BANDS],
                                        ALU.subtract).then_inc(check_step, 1)
            dve.wait_ge(check_step, 2)
            flat = diff.rearrange("p g b q -> p (g b q)")
            nc.vector.tensor_tensor(flat, flat, flat, ALU.mult).then_inc(check_step, 1)
            dve.wait_ge(check_step, 3)
            nc.vector.tensor_scalar(flat, flat, TOLERANCE * TOLERANCE, None, ALU.is_le).then_inc(check_step, 1)
            dve.wait_ge(check_step, 4)
            nc.vector.tensor_reduce(agreed[:, 0:1], flat, axis=AX.X, op=ALU.add).then_inc(check_step, 1)
            dve.wait_ge(check_summed, 1)
            count = float(CH * NB * (BANDS - 1))
            nc.vector.tensor_scalar(verdict[0:1, 0:1], RB[0:1, 0, 0, 0, 0:1], -1.0, count, ALU.mult, ALU.add).then_inc(verdict_in, 1)
            dve.wait_ge(verdict_in, 1)
            bad = dve.value_load(verdict[0:1, 0:1], min_val=0, max_val=1 << 20)
            with dve.If(bad > 0):
                one_by_one_vector(dve)
            dve.wait_ge(verdict_in, 1)

        @block.tensor
        def _(pe):
            def spread(g, place, i, half):
                buf, j = place
                for s in (2 * half, 2 * half + 1):
                    x = nc.tensor.matmul(RB[:, g, i, s], pick[:, QUAD * i + s], R[:, buf, j], start=s == 0, stop=s == QUAD - 1)
                if half == 1:
                    x.then_inc(spread_done[g], 1)

            def project(g, quad, i, half):
                if half == 0:
                    wait(pe, scaled[g], quad + 1)
                two = slice(2 * half, 2 * half + 2)
                nc.tensor.matmul(Z[:, g, i, two].rearrange("p s c -> p (s c)"), wT, T[:, g, i, two].rearrange("p s c -> p (s c)"),
                                 start=half == 0, stop=False, skip_group_check=True)

            def recur(g, m, s):
                wait(pe, y_ready[g], m * STEPS + s)
                nc.tensor.matmul(Z[:, g, s // QUAD, s % QUAD], vT, Y[:, g, (s - 1) % STEPS], start=False, stop=True,
                                 skip_group_check=True).then_inc(summed[g], 1)

            def body(m, now, after):
                for s in range(STEPS):
                    for g in now:
                        recur(g, m[g], s)
                    i, g, half = s // QUAD, s % QUAD // 2, s % 2
                    if (g in now) if i == 0 else (g in after):
                        project(g, 2 * m[g] + i + 1, 1 - i, half)
                    if g in after:
                        spread(g, after[g], i, half)

            def unit(u, parity, groups, then):
                run_bodies(pe, u, parity, groups, then, body, lambda: wait_window(pe, u, parity, then))
                if isinstance(u, int) and u < IMG_GROUPS:
                    pe.wait_ge(restarted, u + 1)

            pe.wait_ge(pick_ready, PICK_READY)
            pe.wait_ge(y_zero, 2)
            pe.wait_ge(window_in[0], WINDOW_INC)
            body({0: -1}, {}, {0: (0, HALF)})
            run_units(pe, unit)
            pe.wait_ge(check_step, 5)
            nc.tensor.matmul(RB[0:1, 0, 0, 0, 0:1], agreed[:, 0:1], ones, start=True, stop=True).then_inc(check_summed, 1)
            pe.wait_ge(verdict_in, 1)
            bad = pe.value_load(verdict[0:1, 0:1], min_val=0, max_val=1 << 20)
            with pe.If(bad > 0):
                one_by_one_tensor(pe)
            pe.wait_ge(verdict_in, 1)


def build(nc, x, conv_weight, W, V, gamma, beta, out):
    x2 = nc.dram_tensor("x2", (CH, BR, NB, BANDS, WD), F32, kind="Internal").ap()
    stat2 = nc.dram_tensor("stat2", (2, BR, NB, BANDS, WD), F32, kind="Internal").ap()
    rparts = nc.dram_tensor("rparts", (BR, IMG_GROUPS, PARTS, BLOCKS, STEPS, COLS), BF16, kind="Internal").ap()
    conv_phase(nc, x, conv_weight, x2, stat2)
    rstd_phase(nc, stat2, rparts)
    with ExitStack() as ctx:
        weights = ctx.enter_context(nc.sbuf_tensor("weights", [128, 2, 128], F32))
        bias = ctx.enter_context(nc.sbuf_tensor("bias", [128, 1], F32))
        statistics_phase(nc, x2, rparts, W, V, gamma, beta, weights[:, 0], weights[:, 1], bias[:, 0:1])
        scan_phase(nc, x2, rparts, weights[:, 0], weights[:, 1], bias[:, 0:1], out)


_INS = ['x', 'L0_conv_weight', 'L0_ffn_W', 'L0_ffn_V', 'L0_ffn_gamma', 'L0_ffn_beta']
_OUTS = [((NB, CH, HT, WD), 'float32')]


def kernel(**inputs):
    import numpy as _np
    import concourse.bacc as _bacc
    from concourse import mybir as _mybir
    from concourse.bass_utils import run_bass_kernel_spmd as _run
    nc = _bacc.Bacc("TRN2", target_bir_lowering=False, num_devices=1)
    arrays, args = {}, []
    for name in _INS:
        a = _np.ascontiguousarray(inputs[name])
        arrays[f"in_{name}_dram"] = a
        args.append(nc.dram_tensor(f"in_{name}_dram", a.shape, _mybir.dt.from_np(a.dtype), kind="ExternalInput").ap())
    for i, (shape, dtype) in enumerate(_OUTS):
        dt = _mybir.dt.from_np(_np.dtype(dtype))
        args.append(nc.dram_tensor(f"out_{i}_dram", shape, dt, kind="ExternalOutput").ap())
    build(nc, *args)
    r = _run(nc, [arrays], core_ids=[0])
    return r.results[0]["out_0_dram"]
```

```python
from contextlib import ExitStack

import concourse.bass as bass
from concourse import mybir

F32 = mybir.dt.float32
F32R = mybir.dt.float32r
BF16 = mybir.dt.bfloat16
I32 = mybir.dt.int32
ACT = mybir.ActivationFunctionType
ALU = mybir.AluOpType
AX = mybir.AxisListType

NB, CH, HT, WD = 32, 128, 112, 112
TAPS = 3

CL, WR = 8, 16
CC = CH // CL
BR = WR - 2
BANDS = HT // BR
BG = 2
GROUPS = NB // BG
TILES = BANDS * GROUPS
TN = BG * WD
SC = 4
SLOTS = CC // SC
BC = 2
BANKS = SC // BC
PITCH = WD + 2
LEAD = 2
XBUFS = 5
LN1_EPS, LN2_EPS, BN_EPS = 1e-6, 1e-5, 1e-5


def wait(eng, sem, count):
    if isinstance(count, int) and count <= 0:
        return
    eng.wait_ge(sem, count)


def conv_phase(nc, x, weight, x2, stat2):
    with ExitStack() as ctx:
        def sb(name, shape, dt=F32):
            return ctx.enter_context(nc.sbuf_tensor(name, shape, dt))

        def ps(name, shape, dt=F32):
            return ctx.enter_context(nc.psum_tensor(name, shape, dt))

        def sem(name):
            return ctx.enter_context(nc.semaphore(name))

        X = sb("X", [128, XBUFS, CC, TN])
        band_hi = sb("band_hi", [128, CC, TAPS, 128], F32R)
        band_lo = sb("band_lo", [128, CC, TAPS, 128], F32R)
        band_sg = sb("band_sg", [128, CC, TAPS, 128], F32R)
        xn = sb("xn", [128, 2, SC, TN])
        xn_hi = sb("xn_hi", [128, 2, SC, BG, PITCH], F32R)
        xn_lo = sb("xn_lo", [128, 2, SC, BG, PITCH], F32R)
        xn_sg = sb("xn_sg", [128, 2, SC, BG, PITCH], F32R)
        acc_sq1 = sb("acc_sq1", [128, 2, SC, TN])
        x_sum = sb("x_sum", [128, SC, TN])
        acc2 = sb("acc2", [128, 2, 2, SC, TN])
        acc_d = acc2[:, :, 0]
        acc_sq2 = acc2[:, :, 1]
        mean1 = sb("mean1", [128, XBUFS, TN])
        rstd1 = sb("rstd1", [128, 2, TN])
        guess = sb("guess", [128, TN])
        newton = sb("newton", [128, TN])
        stat_out = sb("stat_out", [WR, 2, TN])
        same_row = sb("same_row", [128, 128])
        masks = sb("masks", [128, BANDS + 1])
        row_mask = masks[:, 0:BANDS]
        eps1 = masks[:, BANDS:BANDS + 1]
        conv = ps("conv", [128, BANKS, 512])
        sq = ps("sq", [128, BANKS, 512])
        sq2b = ps("sq2b", [128, BANKS, 512])
        stats = ps("stats", [128, 2, 2, 256])
        mean_sum, var_sum, stats2_sum = stats[:, 0, 0, 0:TN], stats[:, 1, 0, 0:TN], stats[:, :, 1, 0:TN]
        spare = X[:, 2:XBUFS].rearrange("p x c n -> p (x c n)")
        diag = spare[:, 0:TAPS * 128].rearrange("p (d m) -> p d m", m=128)
        wcol = spare[:, TAPS * 128:TAPS * 128 + CC * TAPS * TAPS].rearrange("p (c k) -> p c k", c=CC)
        full_at = CC * TN
        full = spare[:, full_at:full_at + CC * TAPS * 128].rearrange("p (c d m) -> p c d m", c=CC, d=TAPS)

        x_loaded, x2_stored = sem("x_loaded"), sem("x2_stored")
        w_loaded, masks_ready, full_ready = sem("w_loaded"), sem("masks_ready"), sem("full_ready")
        band_ready, pads_zero = sem("band_ready"), sem("pads_zero")
        x_cleared, tile_in = sem("x_cleared"), sem("tile_in")
        mean1_summed, mean1_ready = sem("mean1_summed"), sem("mean1_ready")
        centered, sq1_ready, sq1_added = sem("centered"), sem("sq1_ready"), sem("sq1_added")
        var1_summed, seed_ready, rstd_step, rstd_ready = sem("var1_summed"), sem("seed_ready"), sem("rstd_step"), sem("rstd_ready")
        var1_eps = sem("var1_eps")
        xn_ready, hi_ready, sg_ready, lo_ready = sem("xn_ready"), sem("hi_ready"), sem("sg_ready"), sem("lo_ready")
        conv_done, d_ready, d_added = sem("conv_done"), sem("d_ready"), sem("d_added")
        sq2_ready, sq2_added, x2_ready = sem("sq2_ready"), sem("sq2_added"), sem("x2_ready")
        stat2_summed, stat2_ready, stat2_stored = sem("stat2_summed"), sem("stat2_ready"), sem("stat2_stored")
        x_folded = sem("x_folded")
        sq1_folded, stats2_folded = sem("sq1_folded"), sem("stats2_folded")

        block = ctx.enter_context(nc.Block())
        LOAD = 16 * CL * BG
        x_rows = x.rearrange("b (cl cc) h w -> b cl h cc w", cc=CC)
        x2_rows = x2.rearrange("(cl cc) b (q r w) -> cl q b r cc w", cc=CC, r=BR, w=WD)
        stat2_rows = stat2.rearrange("s b (q r w) -> s q r b w", r=BR, w=WD)
        flat = lambda t: t.rearrange("p a b -> p (a b)")

        def padded(ring, k):
            return ring[:, k % 2].rearrange("p c b w -> p (c b) w")[:, :, 1:1 + WD]

        def lines(k):
            return xn[:, k % 2].rearrange("p c (b w) -> p (c b) w", b=BG)

        def lead_of(t, k, has_next, has_next2, lead=LEAD):
            s = k + lead
            if s < SLOTS:
                return (t + 1, s) if has_next else None
            return (t + 2, s - SLOTS) if has_next2 else None

        def before(t, k, by, has_prev):
            if k >= by:
                return t, k - by
            return (t - 1, SLOTS + k - by) if has_prev else None

        def following(t, k, has_next):
            if k + 1 < SLOTS:
                return t, k + 1
            return (t + 1, 0) if has_next else None

        @block.sync
        def _(sp):
            def load_tile(q, g, buf):
                top, bottom = isinstance(q, int) and q == 0, isinstance(q, int) and q == BANDS - 1
                lo, hi = (1 if top else 0), (WR - 1 if bottom else WR)
                for cl in range(CL):
                    for b in range(BG):
                        dst = X[cl * WR + lo:cl * WR + hi, buf].rearrange("p c (b w) -> p c b w", b=BG)[:, :, b]
                        src = x_rows[bass.ds(g * BG + b, 1), cl]
                        sp.dma_start(dst, src[0, bass.ds(BR * q - 1 + lo, hi - lo)]).then_inc(x_loaded, 16)

            def store_tile(q, g, buf):
                for cl in range(CL):
                    for b in range(BG):
                        src = X[cl * WR + 1:cl * WR + 1 + BR, buf].rearrange("p c (b w) -> p c b w", b=BG)[:, :, b]
                        sp.dma_start(x2_rows[cl, bass.ds(q, 1), bass.ds(g * BG + b, 1)][0, 0], src).then_inc(x2_stored, 16)

            def store_stats(q, g):
                for s in range(2):
                    src = stat_out[1:1 + BR, s].rearrange("p (b w) -> p b w", b=BG)
                    sp.dma_start(stat2_rows[s, bass.ds(q, 1)][0, :, bass.ds(g * BG, BG)], src).then_inc(stat2_stored, 16)

            sp.wait_ge(x_cleared, 3)
            for cl in range(CL):
                src = weight[cl * CC:(cl + 1) * CC].rearrange("c o i j -> o (c i j)")
                sp.dma_start(wcol[cl * WR:(cl + 1) * WR].rearrange("p c k -> p (c k)"),
                             src.broadcast_to([WR, CC * TAPS * TAPS])).then_inc(w_loaded, 16)
            for n in range(XBUFS - 1):
                if n == 2:
                    sp.wait_ge(band_ready, 2)
                load_tile(0, n, n)
                sp.wait_ge(x_loaded, (n + 1) * LOAD)
                sp.sem_inc(tile_in, 1)

            def wait_then_address(sem, count):
                wait(sp, sem, count)
                sp.wait_ge(band_ready, 2)

            def step(t, q, g, load_q, load_g):
                def held(value):
                    return value if isinstance(value, int) else sp.snap(value)

                buf, load_buf = held(t % XBUFS), held((t + XBUFS - 1) % XBUFS)
                x2_count, stat2_count = held((t + 1) * SLOTS), held(t + 1)
                loaded_count, stored_count = held((t + XBUFS) * LOAD), held(t * LOAD)
                wait_then_address(x2_stored, stored_count)
                if load_q is not None:
                    load_tile(load_q, load_g, load_buf)
                wait_then_address(x2_ready, x2_count)
                store_tile(q, g, buf)
                if load_q is not None:
                    wait(sp, x_loaded, loaded_count)
                    sp.sem_inc(tile_in, 1)
                wait_then_address(stat2_ready, stat2_count)
                store_stats(q, g)

            def place(n):
                return (n // GROUPS, n % GROUPS) if n < TILES else (None, None)

            ahead = XBUFS - 1
            peeled = GROUPS - ahead
            for t in range(peeled):
                step(t, 0, t, *place(t + ahead))
            with sp.Fori(peeled, TILES - GROUPS - ahead) as t:
                t = sp.snap(t)
                step(t, t // GROUPS, t % GROUPS, (t + ahead) // GROUPS, (t + ahead) % GROUPS)
            with sp.Fori(TILES - GROUPS - ahead, TILES - ahead) as t:
                t = sp.snap(t)
                step(t, t // GROUPS, t % GROUPS, BANDS - 1, t - (TILES - GROUPS - ahead))
            for t in range(TILES - ahead, TILES):
                step(t, *place(t), None, None)
            sp.wait_ge(x2_stored, TILES * LOAD)
            sp.wait_ge(stat2_stored, TILES * 32)

        @block.gpsimd
        def _(pool):
            nc.gpsimd.memset(X[:, 2:4], 0.0).then_inc(masks_ready, 1)
            nc.gpsimd.memset(X[:, 4:XBUFS], 0.0).then_inc(x_cleared, 1)
            pool.wait_ge(masks_ready, 1)
            nc.gpsimd.memset(newton[:, 0:1], 0.0).then_inc(x_cleared, 1)
            step = 1
            for dy in range(TAPS):
                pool.wait_ge(masks_ready, step)
                nc.gpsimd.affine_select(out=diag[:, dy], in_=diag[:, dy], compare_op=ALU.not_equal, fill=1.0,
                                        base=1 - dy, pattern=[[-1, 128]], channel_multiplier=1).then_inc(masks_ready, 1)
                step += 1
                for base, cm, pat in ((0, 1, [[-WR, CL], [0, WR]]), (WR - 1, -1, [[WR, CL], [0, WR]])):
                    pool.wait_ge(masks_ready, step)
                    nc.gpsimd.affine_select(out=diag[:, dy].rearrange("p (c r) -> p c r", r=WR),
                                            in_=diag[:, dy].rearrange("p (c r) -> p c r", r=WR),
                                            compare_op=ALU.is_ge, fill=0.0, base=base, pattern=pat,
                                            channel_multiplier=cm).then_inc(masks_ready, 1)
                    step += 1
                for ro in (0, WR - 1):
                    pool.wait_ge(masks_ready, step)
                    nc.gpsimd.memset(diag[:, dy].rearrange("p (c r) -> p c r", r=WR)[:, :, ro], 0.0).then_inc(masks_ready, 1)
                    step += 1
            nc.gpsimd.memset(same_row[:, :], 0.0).then_inc(masks_ready, 1)
            nc.gpsimd.memset(row_mask[:, :], 1.0).then_inc(masks_ready, 1)
            nc.gpsimd.memset(eps1[:, :], LN1_EPS).then_inc(masks_ready, 1)
            step += 3
            for k in range(1 - CL, CL):
                pool.wait_ge(masks_ready, step)
                nc.gpsimd.affine_select(out=same_row[:, :], in_=same_row[:, :], compare_op=ALU.not_equal, fill=1.0 / CH,
                                        base=k * WR, pattern=[[-1, 128]], channel_multiplier=1).then_inc(masks_ready, 1)
                step += 1
            for cl in range(CL):
                for q, r in ((0, 0), (BANDS - 1, WR - 1)):
                    pool.wait_ge(masks_ready, step)
                    nc.gpsimd.affine_select(out=row_mask[:, q:q + 1], in_=row_mask[:, q:q + 1], compare_op=ALU.not_equal,
                                            fill=0.0, base=-(cl * WR + r), pattern=[[0, 1]],
                                            channel_multiplier=1).then_inc(masks_ready, 1)
                    step += 1
            pool.wait_ge(masks_ready, step)
            for ring in (xn_hi, xn_lo, xn_sg):
                for side in (0, PITCH - 1):
                    nc.gpsimd.memset(ring[:, :, :, :, side].bitcast(F32), 0.0).then_inc(pads_zero, 1)

            def mean_of(t):
                return mean1[:, t % XBUFS].unsqueeze(1).broadcast_to([128, SC, TN])

            def center(t, k):
                if k == 0:
                    wait(pool, mean1_ready, t + 1)
                part = X[:, t % XBUFS, SC * k:SC * (k + 1)]
                nc.gpsimd.tensor_tensor(part, part, mean_of(t), ALU.subtract).then_inc(centered, 1)

            def low_part(t, k):
                n = t * SLOTS + k
                wait(pool, hi_ready, n + 1)
                wait(pool, conv_done, BANKS * (n - 1))
                nc.gpsimd.tensor_tensor(padded(xn_lo, k), lines(k), padded(xn_hi, k).bitcast(F32), ALU.subtract).then_inc(lo_ready, 1)

            def add_mean(t, k):
                n = t * SLOTS + k
                wait(pool, d_added, n + 1)
                wait(pool, sq2_ready, n + 1)
                part = X[:, t % XBUFS, SC * k:SC * (k + 1)]
                nc.gpsimd.tensor_tensor(part, part, mean_of(t), ALU.add).then_inc(x2_ready, 1)

            def tile(t, has_prev, has_next, has_next2):
                for k in range(SLOTS):
                    for work, at in ((add_mean, before(t, k, 2, has_prev)),
                                     (low_part, following(t, k, has_next)),
                                     (center, lead_of(t, k, has_next, has_next2, LEAD + 1))):
                        if at is not None:
                            work(*at)

            for k in range(SLOTS):
                center(0, k)
            for k in range(LEAD + 1):
                center(1, k)
            low_part(0, 0)
            tile(0, False, True, True)
            tile(1, True, True, True)
            with pool.Fori(2, TILES - 2) as t:
                tile(pool.snap(t), True, True, True)
            tile(TILES - 2, True, True, False)
            tile(TILES - 1, True, False, False)
            add_mean(TILES - 1, SLOTS - 2)
            add_mean(TILES - 1, SLOTS - 1)

        @block.scalar
        def _(act):
            act.wait_ge(full_ready, 1)
            nc.scalar.activation(band_sg[:, :, :, :].rearrange("p c d m -> p (c d m)"),
                                 full.rearrange("p c d m -> p (c d m)"), ACT.Sign).then_inc(band_ready, 1)

            def copy_mean(t):
                wait(act, mean1_summed, t + 1)
                wait(act, x2_ready, (t - 3) * SLOTS + 1)
                nc.scalar.activation(mean1[:, t % XBUFS], mean_sum, ACT.Copy).then_inc(mean1_ready, 1)

            def square1(t, k):
                n = t * SLOTS + k
                wait(act, centered, n + 1)
                wait(act, sq1_added, n)
                nc.scalar.activation(sq[:, :, 0:BC * TN], X[:, t % XBUFS, SC * k:SC * (k + 1)].rearrange(
                    "p (b c) n -> p b (c n)", b=BANKS), ACT.Square).then_inc(sq1_ready, 1)

            def seed(t):
                wait(act, var1_summed, t + 1)
                nc.scalar.activation(var_sum, var_sum, ACT.Identity, bias=eps1[:, 0:1]).then_inc(var1_eps, 1)
                wait(act, var1_eps, t + 1)
                nc.scalar.activation(guess[:, :], var_sum, ACT.Abs_reciprocal_sqrt).then_inc(seed_ready, 1)
                wait(act, seed_ready, 2 * t + 1)
                nc.scalar.activation(newton[:, :], guess[:, :], ACT.Square).then_inc(seed_ready, 1)

            def high_part(t, k):
                n = t * SLOTS + k
                wait(act, xn_ready, n + 1)
                wait(act, conv_done, BANKS * (n - 1))
                nc.scalar.activation(padded(xn_hi, k), lines(k), ACT.Copy).then_inc(hi_ready, 1)

            def signs(t, k):
                nc.scalar.activation(padded(xn_sg, k), lines(k), ACT.Sign).then_inc(sg_ready, 1)

            def square2(t, k):
                n = t * SLOTS + k
                wait(act, d_ready, BANKS * (n + 1))
                wait(act, sq2_added, n)
                nc.scalar.activation(sq2b[:, :, 0:BC * TN], X[:, t % XBUFS, SC * k:SC * (k + 1)].rearrange(
                    "p (b c) n -> p b (c n)", b=BANKS), ACT.Square).then_inc(sq2_ready, 1)

            def copy_stats(t):
                wait(act, stat2_summed, t + 1)
                wait(act, var1_summed, min(t + 3, TILES) if isinstance(t, int) else t + 3)
                wait(act, stat2_stored, 32 * t)
                nc.scalar.activation(stat_out[:, :, :], stats2_sum[0:WR], ACT.Copy).then_inc(stat2_ready, 1)

            def tile(t, has_prev, has_next, has_next2):
                for k in range(SLOTS):
                    if k == 1 and has_next2:
                        copy_mean(t + 2)
                    if lead_of(t, k, has_next, has_next2) is not None:
                        square1(*lead_of(t, k, has_next, has_next2))
                    if following(t, k, has_next) is not None:
                        high_part(*following(t, k, has_next))
                        signs(*following(t, k, has_next))
                    if k == 2 and has_prev:
                        copy_stats(t - 1)
                    if k == 2 and has_next:
                        seed(t + 1)
                    if before(t, k, 1, has_prev) is not None:
                        square2(*before(t, k, 1, has_prev))

            copy_mean(0)
            for k in range(SLOTS):
                square1(0, k)
            copy_mean(1)
            seed(0)
            for k in range(LEAD):
                square1(1, k)
            high_part(0, 0)
            signs(0, 0)
            tile(0, False, True, True)
            tile(1, True, True, True)
            with act.Fori(2, TILES - 2) as t:
                tile(act.snap(t), True, True, True)
            tile(TILES - 2, True, True, False)
            tile(TILES - 1, True, False, False)
            square2(TILES - 1, SLOTS - 1)
            copy_stats(TILES - 1)

        @block.vector
        def _(dve):
            nc.vector.memset(X[:, 0:2], 0.0).then_inc(x_cleared, 1)
            dve.wait_ge(w_loaded, 16 * CL)
            dve.wait_ge(masks_ready, 1 + 5 * TAPS)
            n = 0
            for cc in range(CC):
                for dx in range(TAPS):
                    for dy in range(TAPS):
                        w1 = wcol[:, cc, dy * TAPS + dx:dy * TAPS + dx + 1]
                        if dy == 0:
                            i = nc.vector.tensor_scalar(full[:, cc, dx], diag[:, dy], w1, None, ALU.mult)
                        else:
                            dve.wait_ge(rstd_step, n)
                            i = nc.vector.scalar_tensor_tensor(full[:, cc, dx], diag[:, dy], w1, full[:, cc, dx],
                                                               ALU.mult, ALU.add)
                        i.then_inc(rstd_step, 1)
                        n += 1
            base = n
            dve.wait_ge(rstd_step, base)
            nc.vector.tensor_copy(band_hi[:, :, :, :].rearrange("p c d m -> p (c d m)"),
                                  full.rearrange("p c d m -> p (c d m)")).then_inc(full_ready, 1)
            dve.wait_ge(full_ready, 1)
            nc.vector.tensor_tensor(band_lo[:, :, :, :].rearrange("p c d m -> p (c d m)"),
                                    full.rearrange("p c d m -> p (c d m)"),
                                    band_hi[:, :, :, :].rearrange("p c d m -> p (c d m)").bitcast(F32),
                                    ALU.subtract).then_inc(band_ready, 1)
            dve.wait_ge(masks_ready, 1 + 5 * TAPS + 3 + 2 * CL - 1 + 2 * CL)

            def banks(tensor):
                return tensor.rearrange("p (b c) n -> p b (c n)", b=BANKS)

            def add_square1(t, k):
                n = t * SLOTS + k
                wait(dve, sq1_ready, n + 1)
                if k == 0:
                    wait(dve, var1_summed, t - 1)
                    nc.vector.tensor_copy(banks(acc_sq1[:, t % 2]), sq[:, :, 0:BC * TN]).then_inc(sq1_added, 1)
                else:
                    wait(dve, sq1_added, n)
                    nc.vector.tensor_tensor(banks(acc_sq1[:, t % 2]), banks(acc_sq1[:, t % 2]), sq[:, :, 0:BC * TN],
                                            ALU.add).then_inc(sq1_added, 1)

            def finish_rstd(t, q):
                wait(dve, seed_ready, 2 * t + 2)
                nc.vector.tensor_tensor(newton[:, :], newton[:, :], var_sum, ALU.mult).then_inc(rstd_step, 1)
                wait(dve, rstd_step, base + 2 * t + 1)
                nc.vector.tensor_scalar(newton[:, :], newton[:, :], -0.5, 1.5, ALU.mult, ALU.add).then_inc(rstd_step, 1)
                wait(dve, rstd_step, base + 2 * t + 2)
                nc.vector.scalar_tensor_tensor(rstd1[:, t % 2], guess[:, :], row_mask[:, bass.ds(q, 1)], newton[:, :],
                                               ALU.mult, ALU.mult).then_inc(rstd_ready, 1)

            def normalize(t, k):
                n = t * SLOTS + k
                wait(dve, rstd_ready, t + 1)
                wait(dve, sg_ready, n - 1)
                wait(dve, lo_ready, n - 1)
                nc.vector.tensor_tensor(xn[:, k % 2], X[:, t % XBUFS, SC * k:SC * (k + 1)],
                                        rstd1[:, t % 2].unsqueeze(1).broadcast_to([128, SC, TN]), ALU.mult).then_inc(xn_ready, 1)

            def add_conv(t, k, bank):
                n = BANKS * (t * SLOTS + k) + bank
                part = X[:, t % XBUFS, SC * k + BC * bank:SC * k + BC * (bank + 1)].rearrange("p c n -> p (c n)")
                wait(dve, conv_done, n + 1)
                nc.vector.tensor_tensor(part, part, conv[:, bank, 0:BC * TN], ALU.add).then_inc(d_ready, 1)

            def sum_d(t, k):
                n = t * SLOTS + k
                part = X[:, t % XBUFS, SC * k:SC * (k + 1)]
                wait(dve, d_ready, BANKS * (n + 1))
                if k == 0:
                    wait(dve, stat2_summed, t - 1)
                    nc.vector.tensor_scalar(acc_d[:, t % 2], part, 1.0, None, ALU.mult).then_inc(d_added, 1)
                else:
                    wait(dve, d_added, n)
                    nc.vector.tensor_tensor(acc_d[:, t % 2], acc_d[:, t % 2], part, ALU.add).then_inc(d_added, 1)

            def add_square2(t, k):
                n = t * SLOTS + k
                wait(dve, sq2_ready, n + 1)
                if k == 0:
                    wait(dve, stat2_summed, t - 1)
                    nc.vector.tensor_copy(banks(acc_sq2[:, t % 2]), sq2b[:, :, 0:BC * TN]).then_inc(sq2_added, 1)
                else:
                    wait(dve, sq2_added, n)
                    nc.vector.tensor_tensor(banks(acc_sq2[:, t % 2]), banks(acc_sq2[:, t % 2]), sq2b[:, :, 0:BC * TN],
                                            ALU.add).then_inc(sq2_added, 1)

            def fold_x(t, go):
                x_slot = lambda k: X[:, t % XBUFS, SC * k:SC * (k + 1)]
                if go == 0:
                    wait(dve, tile_in, t + 1)
                    wait(dve, mean1_summed, t)
                    nc.vector.tensor_tensor(x_sum[:, :, :], x_slot(1), x_slot(2), ALU.add).then_inc(x_folded, 1)
                else:
                    wait(dve, x_folded, 2 * t + 1)
                    nc.vector.tensor_tensor(x_sum[:, :, :], x_sum[:, :, :], x_slot(3), ALU.add).then_inc(x_folded, 1)

            def fold_square1(t):
                acc = acc_sq1[:, t % 2]
                wait(dve, sq1_added, (t + 1) * SLOTS)
                nc.vector.tensor_tensor(acc[:, 0:SC // 2], acc[:, 0:SC // 2], acc[:, SC // 2:SC], ALU.add).then_inc(sq1_folded, 1)

            def fold_stats2(t):
                acc = acc2[:, t % 2]
                wait(dve, d_added, (t + 1) * SLOTS)
                wait(dve, sq2_added, (t + 1) * SLOTS)
                nc.vector.tensor_tensor(acc[:, :, 0:SC // 2].rearrange("p s c n -> p s (c n)"),
                                        acc[:, :, 0:SC // 2].rearrange("p s c n -> p s (c n)"),
                                        acc[:, :, SC // 2:SC].rearrange("p s c n -> p s (c n)"), ALU.add).then_inc(stats2_folded, 1)

            def tile(t, q_next, has_prev, has_next, has_next2, has_next3=True):
                for k in range(SLOTS):
                    ahead, stat = following(t, k, has_next), lead_of(t, k, has_next, has_next2)
                    last, last2 = before(t, k, 1, has_prev), before(t, k, 2, has_prev)
                    if ahead is not None:
                        normalize(*ahead)
                    if k == 0 and has_next2:
                        fold_x(t + 2, 1)
                    if last is not None:
                        add_conv(*last, 1)
                        sum_d(*last)
                    if last2 is not None:
                        add_square2(*last2)
                    if stat is not None:
                        add_square1(*stat)
                    if k == 1 and has_prev:
                        fold_stats2(t - 1)
                    if k == 1 and has_next:
                        fold_square1(t + 1)
                    if k == 3 and has_next3:
                        fold_x(t + 3, 0)
                    add_conv(t, k, 0)
                    if k == 2 and has_next:
                        finish_rstd(t + 1, q_next)

            for go in range(2):
                fold_x(0, go)
            for k in range(SLOTS):
                add_square1(0, k)
            fold_square1(0)
            for go in range(2):
                fold_x(1, go)
            finish_rstd(0, 0)
            for k in range(LEAD):
                add_square1(1, k)
            fold_x(2, 0)
            normalize(0, 0)
            tile(0, 0, False, True, True)
            tile(1, 0, True, True, True)
            with dve.Fori(2, TILES - 3) as t:
                t = dve.snap(t)
                tile(t, dve.snap((t + 1) // GROUPS), True, True, True)
            tile(TILES - 3, BANDS - 1, True, True, True, False)
            tile(TILES - 2, BANDS - 1, True, True, False, False)
            tile(TILES - 1, None, True, False, False, False)
            add_conv(TILES - 1, SLOTS - 1, 1)
            sum_d(TILES - 1, SLOTS - 1)
            add_square2(TILES - 1, SLOTS - 2)
            add_square2(TILES - 1, SLOTS - 1)
            fold_stats2(TILES - 1)

        @block.tensor
        def _(pe):
            pe.wait_ge(masks_ready, 1 + 5 * TAPS + 3 + 2 * CL - 1)

            def sum_mean(t, part):
                if part == 0:
                    wait(pe, tile_in, t + 1)
                    wait(pe, mean1_ready, t)
                    wait(pe, stat2_ready, t - 3)
                    for c in range(SC):
                        nc.tensor.matmul(mean_sum, same_row[:, :], X[:, t % XBUFS, c], start=c == 0, stop=False)
                else:
                    wait(pe, x_folded, 2 * t + 2)
                    for c in range(SC):
                        i = nc.tensor.matmul(mean_sum, same_row[:, :], x_sum[:, c], start=False, stop=c == SC - 1)
                    i.then_inc(mean1_summed, 1)

            def sum_var(t):
                wait(pe, sq1_folded, t + 1)
                wait(pe, rstd_ready, t)
                wait(pe, stat2_ready, t - 2)
                for c in range(SC // 2):
                    i = nc.tensor.matmul(var_sum, same_row[:, :], acc_sq1[:, t % 2, c], start=c == 0, stop=c == SC // 2 - 1)
                i.then_inc(var1_summed, 1)

            def sum_stats2(t):
                wait(pe, stats2_folded, t + 1)
                wait(pe, stat2_ready, t)
                wait(pe, mean1_ready, min(t + 4, TILES) if isinstance(t, int) else t + 4)
                wait(pe, rstd_ready, min(t + 2, TILES) if isinstance(t, int) else t + 2)
                for c in range(SC // 2):
                    nc.tensor.matmul(stats2_sum[:, 0], same_row[:, :], acc_d[:, t % 2, c], start=c == 0, stop=c == SC // 2 - 1)
                for c in range(SC // 2):
                    i = nc.tensor.matmul(stats2_sum[:, 1], same_row[:, :], acc_sq2[:, t % 2, c], start=c == 0, stop=c == SC // 2 - 1)
                i.then_inc(stat2_summed, 1)

            def convolve(t, k):
                n = t * SLOTS + k
                wait(pe, sg_ready, n + 1)
                wait(pe, lo_ready, n + 1)
                for c in range(SC):
                    bank, at = c // BC, c % BC * TN
                    if c % BC == 0:
                        wait(pe, d_ready, BANKS * (n - 1) + bank + 1)
                    todo = [(m, ring, dx) for dx in range(TAPS)
                            for m, ring in ((band_sg, xn_hi), (band_sg, xn_lo), (band_hi, xn_sg), (band_lo, xn_sg))]
                    for j, (m, ring, dx) in enumerate(todo):
                        i = nc.tensor.matmul(conv[:, bank, at:at + TN], m[:, SC * k + c, dx], ring[:, k % 2, c, :, dx:dx + WD],
                                             start=j == 0, stop=j == len(todo) - 1)
                    if c % BC == BC - 1:
                        i.then_inc(conv_done, 1)

            def tile(t, has_prev, has_next, has_next2, has_next3):
                for k in range(SLOTS):
                    convolve(t, k)
                    if k == 0 and has_next2:
                        sum_mean(t + 2, 1)
                    if k == 1 and has_prev:
                        sum_stats2(t - 1)
                    if k == 1 and has_next:
                        sum_var(t + 1)
                    if k == 2 and has_next3:
                        sum_mean(t + 3, 0)

            for t in range(3):
                for part in range(2 if t < 2 else 1):
                    sum_mean(t, part)
                if t == 0:
                    sum_var(0)
            pe.wait_ge(band_ready, 2)
            pe.wait_ge(full_ready, 1)
            pe.wait_ge(pads_zero, 6)
            tile(0, False, True, True, True)
            tile(1, True, True, True, True)
            with pe.Fori(2, TILES - 3) as t:
                tile(pe.snap(t), True, True, True, True)
            tile(TILES - 3, True, True, True, False)
            tile(TILES - 2, True, True, False, False)
            tile(TILES - 1, True, False, False, False)
            sum_stats2(TILES - 1)


CHUNKS = 7
WIN = 128
WINDOWS = HT * WD // (CHUNKS * WIN)
STEPS = 8
BLOCKS = WIN // STEPS
QUAD = 4
IMG_GROUPS = 2
IMGS = NB // IMG_GROUPS
COLS = IMGS * CHUNKS
PARTS = 3
HALF = BLOCKS // 2
WINDOW_BUFS = 3
TOLERANCE = 2.0 ** -22


def rstd_phase(nc, stat2, rparts):
    with ExitStack() as ctx:
        def sb(name, shape, dt=F32):
            return ctx.enter_context(nc.sbuf_tensor(name, shape, dt))

        def sem(name):
            return ctx.enter_context(nc.semaphore(name))

        moments = sb("moments", [COLS, 2, IMG_GROUPS, WINDOWS, WIN])
        rstd = sb("rstd", [COLS, IMG_GROUPS, WINDOWS, WIN])
        work = sb("work", [COLS, IMG_GROUPS, WINDOWS, WIN])
        ident = sb("ident_r", [128, 128])
        left = sb("left", [WIN, WINDOWS * IMG_GROUPS, COLS])
        part = [sb(f"part{i}", [WIN, WINDOWS * IMG_GROUPS, COLS], BF16) for i in range(PARTS)]
        per_bank = 512 // COLS
        banks = WINDOWS * IMG_GROUPS // per_bank
        turned = ctx.enter_context(nc.psum_tensor("turned", [WIN, banks, 512], F32))
        loaded, ident_ready, squared, var_ready, seeded = (sem(n) for n in ("loaded", "ident_ready", "squared", "var_ready", "seeded"))
        step, rstd_ready, turned_ready, left_ready, parts_stored = (sem(n) for n in ("step", "rstd_done", "turned_ready", "left_ready", "parts_stored"))
        part_ready = sem("part_ready")
        block = ctx.enter_context(nc.Block())
        flat = lambda t: t.rearrange("p g r w -> p (g r w)")

        @block.sync
        def _(sp):
            src = stat2.rearrange("s (g b) (q r w) -> s g (b q) r w", g=IMG_GROUPS, q=CHUNKS, w=WIN)
            for s in range(2):
                for g in range(IMG_GROUPS):
                    sp.dma_start(moments[:, s, g], src[s, g]).then_inc(loaded, 16)
            dst = rparts.rearrange("r g p j s c -> p (j s) (r g) c")
            for i in range(PARTS):
                sp.wait_ge(part_ready, 1 + i)
                sp.dma_start(dst[i], part[i][:, :, :]).then_inc(parts_stored, 16)
            sp.wait_ge(parts_stored, 16 * PARTS)

        @block.gpsimd
        def _(pool):
            nc.gpsimd.memset(ident[:, :], 0.0).then_inc(ident_ready, 1)
            pool.wait_ge(ident_ready, 1)
            nc.gpsimd.affine_select(out=ident[:, :], in_=ident[:, :], compare_op=ALU.not_equal, fill=1.0, base=0,
                                    pattern=[[-1, 128]], channel_multiplier=1).then_inc(ident_ready, 1)

        @block.scalar
        def _(act):
            act.wait_ge(loaded, 16 * 4)
            nc.scalar.activation(flat(work[:, :, :, :]), flat(moments[:, 0]), ACT.Square).then_inc(squared, 1)
            act.wait_ge(var_ready, 1)
            nc.scalar.activation(flat(rstd[:, :, :, :]), flat(moments[:, 1]), ACT.Abs_reciprocal_sqrt).then_inc(seeded, 1)
            act.wait_ge(seeded, 1)
            nc.scalar.activation(flat(work[:, :, :, :]), flat(rstd[:, :, :, :]), ACT.Square).then_inc(seeded, 1)

        @block.vector
        def _(dve):
            dve.wait_ge(squared, 1)
            nc.vector.scalar_tensor_tensor(flat(moments[:, 1]), flat(moments[:, 1]), LN2_EPS, flat(work[:, :, :, :]),
                                           ALU.add, ALU.subtract).then_inc(var_ready, 1)
            dve.wait_ge(seeded, 2)
            nc.vector.tensor_tensor(flat(work[:, :, :, :]), flat(work[:, :, :, :]), flat(moments[:, 1]), ALU.mult).then_inc(step, 1)
            dve.wait_ge(step, 1)
            nc.vector.tensor_scalar(flat(work[:, :, :, :]), flat(work[:, :, :, :]), -0.5, 1.5, ALU.mult, ALU.add).then_inc(step, 1)
            dve.wait_ge(step, 2)
            nc.vector.tensor_tensor(flat(rstd[:, :, :, :]), flat(rstd[:, :, :, :]), flat(work[:, :, :, :]), ALU.mult).then_inc(rstd_ready, 1)
            dve.wait_ge(turned_ready, 1)
            rows = left[:, :, :].rearrange("p n c -> p (n c)")
            nc.vector.tensor_copy(left[:, :, :].rearrange("p (k n) c -> p k (n c)", k=banks),
                                  turned[:, :, 0:per_bank * COLS]).then_inc(left_ready, 1)
            for i in range(PARTS):
                dve.wait_ge(left_ready, 1 + i)
                to = part[i][:, :, :].rearrange("p n c -> p (n c)")
                nc.vector.tensor_copy(to, rows).then_inc(part_ready, 1)
                if i < PARTS - 1:
                    dve.wait_ge(part_ready, 1 + i)
                    nc.vector.tensor_tensor(rows, rows, to, ALU.subtract).then_inc(left_ready, 1)

        @block.tensor
        def _(pe):
            pe.wait_ge(ident_ready, 2)
            pe.wait_ge(rstd_ready, 1)
            for n in range(WINDOWS * IMG_GROUPS):
                r, g = n // IMG_GROUPS, n % IMG_GROUPS
                at = n % per_bank * COLS
                i = nc.tensor.transpose(turned[:, n // per_bank, at:at + COLS], rstd[:, g, r], ident[0:COLS, 0:COLS])
            i.then_inc(turned_ready, 1)



def window_loader(x2, rparts, X, R):
    x2_win = x2.rearrange("c (g b) (q r w) -> r g c (b q) w", g=IMG_GROUPS, q=CHUNKS, w=WIN)
    r_win = rparts.rearrange("r g p j s c -> r g p s j c")

    def load(sp, row, g, buf, done):
        sp.dma_start(X[:, buf], x2_win[bass.ds(row, 1), g][0]).then_inc(done, 16)
        for p in range(PARTS):
            sp.dma_start(R[p * STEPS:(p + 1) * STEPS, buf], r_win[bass.ds(row, 1), g, p][0]).then_inc(done, 16)

    return load, x2_win, r_win


WINDOW_INC = 16 * (1 + PARTS)


def pool_constants(nc, pool, R, pick, pick_ready):
    nc.gpsimd.memset(R.rearrange("p k j c -> p (k j c)"), 0.0).then_inc(pick_ready, 1)
    nc.gpsimd.memset(pick.rearrange("p s m -> p (s m)"), 0.0).then_inc(pick_ready, 1)
    for part in range(PARTS):
        pool.wait_ge(pick_ready, 2 + part)
        nc.gpsimd.affine_select(out=pick, in_=pick, compare_op=ALU.not_equal, fill=1.0, base=-part * STEPS,
                                pattern=[[-1, STEPS], [0, 128]], channel_multiplier=1).then_inc(pick_ready, 1)


PICK_READY = 2 + PARTS


def statistics_phase(nc, x2, rparts, W, V, gamma, beta, wT, vT, bias_q):
    with ExitStack() as ctx:
        def sb(name, shape, dt=F32):
            return ctx.enter_context(nc.sbuf_tensor(name, shape, dt))

        def sem(name):
            return ctx.enter_context(nc.semaphore(name))

        quads, BODY = WIN // QUAD, 4
        total = WINDOWS * IMG_GROUPS * quads
        X = sb("X_stat", [128, IMG_GROUPS, COLS, WIN])
        R = sb("R_stat", [128, IMG_GROUPS, BLOCKS, COLS], BF16)
        T = sb("T_stat", [128, BODY, QUAD, COLS])
        rstd_copy = sb("rstd_copy", [128, 2, QUAD, COLS])
        pick = sb("pick_stat", [128, STEPS, 128], BF16)
        parts = sb("bn_parts", [128, total * 6])
        w_in, v_in, ident = sb("w_in", [128, 128]), sb("v_in", [128, 128]), sb("ident", [128, 128])
        small = sb("small", [128, 8])
        gam, bet, row_mean, scale, eps = (small[:, i:i + 1] for i in range(5))
        moments = small[:, 5:7]
        RB, Q = (ctx.enter_context(nc.psum_tensor(name, [128, n, 512], F32))[:, :, 0:QUAD * COLS].rearrange(
            "p i (s c) -> p i s c", c=COLS) for name, n in (("RB_stat", 2), ("Q", BODY)))
        turned = ctx.enter_context(nc.psum_tensor("turned_w", [128, 3, 128], F32))

        params_in, pick_ready, ident_ready = sem("params_in"), sem("pick_ready"), sem("ident_ready_s")
        w_in_x = [sem(f"window_in{g}") for g in range(IMG_GROUPS)]
        spread_done, projected, measured = sem("spread_done"), sem("projected"), sem("measured")
        scaled_even, copied, scaled_odd = sem("scaled_even"), sem("copied"), sem("scaled_odd")
        w_centered, turned_ready, wT_ready, vT_ready = sem("w_centered"), sem("turned_w_ready"), sem("wT_ready"), sem("vT_ready")
        bn_step, std_ready = sem("bn_step"), sem("std_ready")
        load, _, _ = window_loader(x2, rparts, X, R)
        block = ctx.enter_context(nc.Block())

        def run_windows(eng, body):
            bodies = quads // BODY
            for g in range(IMG_GROUPS):
                peeled = 2 if g == 0 else 1
                for j in range(peeled):
                    body(0, g, j, g == 0 and j == 0)
                with eng.Fori(peeled, bodies) as j:
                    body(0, g, eng.snap(j), False)
            with eng.Fori(1, WINDOWS) as row:
                row = eng.snap(row)
                for g in range(IMG_GROUPS):
                    body(row, g, 0, False)
                    with eng.Fori(1, bodies) as j:
                        body(row, g, eng.snap(j), False)

        def quad_index(row, g, j, i):
            return (row * IMG_GROUPS + g) * quads + BODY * j + i

        def pair_index(row, g, j, i):
            return (row * IMG_GROUPS + g) * (quads // 2) + BODY // 2 * j + i // 2

        def window_quad(g, j, i):
            return X[:, g, :, bass.ds(j * (BODY * QUAD) + i * QUAD, QUAD)].rearrange("p c s -> p s c")

        @block.sync
        def _(sp):
            for dst, src in ((w_in[:, :], W), (v_in[:, :], V), (gam, gamma.unsqueeze(1)), (bet, beta.unsqueeze(1))):
                sp.dma_start(dst, src).then_inc(params_in, 16)
            sp.wait_ge(pick_ready, 1)
            for g in range(IMG_GROUPS):
                load(sp, 0, g, g, w_in_x[g])
            with sp.Fori(1, WINDOWS) as row:
                row = sp.snap(row)
                for g in range(IMG_GROUPS):
                    through = sp.snap(pair_index(row - 1, g, quads // BODY, 0))
                    sp.wait_ge(scaled_even, through)
                    sp.wait_ge(scaled_odd, through)
                    sp.wait_ge(params_in, 64)
                    load(sp, row, g, g, w_in_x[g])

        @block.gpsimd
        def _(pool):
            pool_constants(nc, pool, R[:, :, :, :], pick[:, :, :], pick_ready)
            nc.gpsimd.memset(ident[:, :], 0.0).then_inc(ident_ready, 1)
            pool.wait_ge(ident_ready, 1)
            nc.gpsimd.affine_select(out=ident[:, :], in_=ident[:, :], compare_op=ALU.not_equal, fill=1.0, base=0,
                                    pattern=[[-1, 128]], channel_multiplier=1).then_inc(ident_ready, 1)
            nc.gpsimd.memset(eps, BN_EPS).then_inc(ident_ready, 1)

            def body(row, g, j, first):
                for i in (1, 3):
                    n, pair = quad_index(row, g, j, i), pair_index(row, g, j, i)
                    if isinstance(j, int) and j == 0 and i == 1:
                        wait(pool, w_in_x[g], (row + 1) * WINDOW_INC)
                    wait(pool, projected, n - 3)
                    wait(pool, copied, pair + 1)
                    nc.gpsimd.tensor_tensor(T[:, i], window_quad(g, j, i), rstd_copy[:, i // 2], ALU.mult).then_inc(scaled_odd, 1)

            run_windows(pool, body)

        @block.scalar
        def _(act):
            def body(row, g, j, first):
                for i in (1, 3):
                    n, pair = quad_index(row, g, j, i), pair_index(row, g, j, i)
                    wait(act, scaled_odd, pair - 1)
                    wait(act, spread_done, n + 1)
                    nc.scalar.activation(rstd_copy[:, i // 2], RB[:, 1], ACT.Copy).then_inc(copied, 1)

            run_windows(act, body)
            act.wait_ge(bn_step, 1)
            act.wait_ge(ident_ready, 3)
            nc.scalar.activation(scale, moments[:, 1:2], ACT.Sqrt, bias=eps).then_inc(std_ready, 1)

        @block.vector
        def _(dve):
            dve.wait_ge(params_in, 64)
            nc.vector.tensor_reduce(row_mean, w_in[:, :], axis=AX.X, op=ALU.add).then_inc(w_centered, 1)
            dve.wait_ge(w_centered, 1)
            nc.vector.tensor_scalar(row_mean, row_mean, 1.0 / CH, None, ALU.mult).then_inc(w_centered, 1)
            dve.wait_ge(w_centered, 2)
            nc.vector.tensor_scalar(w_in[:, :], w_in[:, :], row_mean, None, ALU.subtract).then_inc(w_centered, 1)
            dve.wait_ge(turned_ready, 1)
            nc.vector.tensor_copy(wT, turned[:, 0]).then_inc(wT_ready, 1)
            nc.vector.tensor_copy(vT, turned[:, 1]).then_inc(vT_ready, 1)

            def measure(n, slot):
                nc.vector.bn_stats(parts[:, bass.ds(6 * n, 6)], Q[:, slot].rearrange("p s c -> p (s c)")).then_inc(measured, 1)

            def body(row, g, j, first):
                for i in (0, 2):
                    n = quad_index(row, g, j, i)
                    if isinstance(j, int) and j == 0 and i == 0:
                        wait(dve, w_in_x[g], (row + 1) * WINDOW_INC)
                    wait(dve, spread_done, n + 1)
                    wait(dve, projected, n - 1)
                    nc.vector.tensor_tensor(T[:, i], window_quad(g, j, i), RB[:, 0], ALU.mult).then_inc(scaled_even, 1)
                    for back in (3, 2):
                        if not first or i >= back:
                            measure(n - back, (i - back) % BODY)

            run_windows(dve, body)
            for n in range(total - 3, total):
                dve.wait_ge(projected, n + 1)
                measure(n, n % BODY)
            dve.wait_ge(measured, total)
            nc.vector.bn_aggr(moments, parts[:, :]).then_inc(bn_step, 1)
            dve.wait_ge(std_ready, 1)
            nc.vector.reciprocal(scale, scale).then_inc(bn_step, 1)
            dve.wait_ge(bn_step, 2)
            nc.vector.tensor_tensor(scale, scale, gam, ALU.mult).then_inc(bn_step, 1)
            dve.wait_ge(bn_step, 3)
            nc.vector.tensor_tensor(row_mean, moments[:, 0:1], scale, ALU.mult).then_inc(bn_step, 1)
            nc.vector.tensor_scalar(w_in[:, :], w_in[:, :], scale, None, ALU.mult).then_inc(w_centered, 1)
            dve.wait_ge(bn_step, 4)
            nc.vector.tensor_tensor(bias_q, bet, row_mean, ALU.subtract).then_inc(bn_step, 1)
            dve.wait_ge(turned_ready, 2)
            nc.vector.tensor_copy(wT, turned[:, 2]).then_inc(wT_ready, 1)
            dve.wait_ge(wT_ready, 2)
            dve.wait_ge(bn_step, 5)

        @block.tensor
        def _(pe):
            pe.wait_ge(ident_ready, 2)
            pe.wait_ge(w_centered, 3)
            nc.tensor.transpose(turned[:, 0], w_in[:, :], ident[:, :])
            nc.tensor.transpose(turned[:, 1], v_in[:, :], ident[:, :]).then_inc(turned_ready, 1)
            pe.wait_ge(pick_ready, PICK_READY)
            pe.wait_ge(wT_ready, 1)

            def project(n, pair, slot):
                wait(pe, scaled_odd if slot % 2 else scaled_even, pair + 1)
                wait(pe, measured, n - BODY + 1)
                nc.tensor.matmul(Q[:, slot].rearrange("p s c -> p (s c)"), wT, T[:, slot].rearrange("p s c -> p (s c)"),
                                 start=True, stop=True).then_inc(projected, 1)

            def body(row, g, j, first):
                for i in range(BODY):
                    n, pair = quad_index(row, g, j, i), pair_index(row, g, j, i)
                    if isinstance(j, int) and j == 0 and i == 0:
                        wait(pe, w_in_x[g], (row + 1) * WINDOW_INC)
                    wait(pe, copied if i % 2 else scaled_even, pair)
                    block_of = R[:, g, bass.ds(j * (BODY // 2) + i // 2, 1)][:, 0]
                    for s in range(QUAD):
                        x = nc.tensor.matmul(RB[:, i % 2, s], pick[:, QUAD * (i % 2) + s], block_of, start=s == 0, stop=s == QUAD - 1)
                    x.then_inc(spread_done, 1)
                    if not first or i >= 2:
                        project(n - 2, pair - 1, (i - 2) % BODY)

            run_windows(pe, body)
            for n in (total - 2, total - 1):
                project(n, n // 2, n % BODY)
            pe.wait_ge(w_centered, 4)
            nc.tensor.transpose(turned[:, 2], w_in[:, :], ident[:, :]).then_inc(turned_ready, 1)


def scan_phase(nc, x2, rparts, wT, vT, bias_q, out):
    with ExitStack() as ctx:
        def sb(name, shape, dt=F32):
            return ctx.enter_context(nc.sbuf_tensor(name, shape, dt))

        def sem(name):
            return ctx.enter_context(nc.semaphore(name))

        X = sb("X_scan", [128, WINDOW_BUFS, COLS, WIN])
        R = sb("R_scan", [128, WINDOW_BUFS, BLOCKS, COLS], BF16)
        T = sb("T_scan", [128, IMG_GROUPS, 2, QUAD, COLS])
        Y = sb("Y", [128, IMG_GROUPS, STEPS, COLS])
        pick = sb("pick_scan", [128, STEPS, 128], BF16)
        y_warm = sb("y_warm", [128, IMG_GROUPS, COLS])
        small = sb("small_scan", [128, 4])
        ones, agreed = small[:, 0:1], small[:, 1:3]
        verdict = sb("verdict", [1, 1], I32)
        Z, RB = (ctx.enter_context(nc.psum_tensor(name, [128, IMG_GROUPS, 2, 512], F32))[:, :, :, 0:QUAD * COLS].rearrange(
            "p g i (s c) -> p g i s c", c=COLS) for name in ("Z", "RB_scan"))

        pick_ready, y_zero = sem("pick_ready_c"), sem("y_zero")
        both = range(IMG_GROUPS)
        window_in, spread_done, scaled, summed, y_ready, added = (
            [sem(f"{name}{g}") for g in both] for name in ("win_in", "spread", "scaled_c", "summed", "y_ready", "added"))
        restarted, out_stored = sem("restarted"), sem("out_stored")
        warm_kept, check_step, check_summed, verdict_in = sem("warm_kept"), sem("check_step"), sem("check_summed"), sem("verdict_in")
        q_in, q_spread, q_scaled, q_summed, q_y, q_added, q_out = (
            sem(n) for n in ("q_in", "q_spread", "q_scaled", "q_summed", "q_y", "q_added", "q_out"))
        load, x2_win, r_win = window_loader(x2, rparts, X, R)
        out_win = out.rearrange("b c h w -> b c (h w)").rearrange("b c (q r w) -> r b c q w", q=CHUNKS, w=WIN)
        block = ctx.enter_context(nc.Block())

        UNITS = 2 * WINDOWS + 2

        def alive(u):
            return tuple(g for g in both if g <= u <= UNITS - 2 + g)

        def run_units(eng, unit):
            for u in (0, 1):
                unit(u, u % 2, alive(u), alive(u + 1))
            with eng.Fori(1, WINDOWS) as k:
                k = eng.snap(k)
                unit(eng.snap(2 * k), 0, (0, 1), (0, 1))
                unit(eng.snap(2 * k + 1), 1, (0, 1), (0, 1))
            for u in (UNITS - 2, UNITS - 1):
                unit(u, u % 2, alive(u), alive(u + 1))

        def run_bodies(eng, u, parity, groups, then, body, before_last=None):
            def place(u, parity, g, b):
                window = (u + 1 - g) // 2
                return (IMG_GROUPS * window + g) % WINDOW_BUFS, (parity + 1 - g) % 2 * HALF + b

            def one(b, last):
                m = {g: (u - g) * HALF + b for g in sorted({*groups, *(then if last else ())})}
                now = {g: place(u, parity, g, b) for g in groups}
                if last:
                    after = {g: place(u + 1, 1 - parity, g, 0) for g in then}
                else:
                    after = {g: place(u, parity, g, b + 1) for g in groups}
                body(m, now, after)

            with eng.Fori(0, HALF - 1) as b:
                one(eng.snap(b), False)
            if before_last is not None:
                before_last()
            one(HALF - 1, True)

        def wait_window(eng, u, parity, then):
            if parity in then:
                wait(eng, window_in[parity], WINDOW_INC + WINDOW_INC * ((u + 2 - parity) // 2))
            if isinstance(u, int) and u == 0:
                wait(eng, window_in[1], WINDOW_INC)


        x_row = X[:, 0, 0:NB]
        t_seq = T[:, 0, 0].rearrange("p s c -> p (s c)")[:, 0:STEPS * NB].rearrange("p (s b) -> p s b", b=NB)
        y_seq = Y[:, 0].rearrange("p s c -> p (s c)")[:, 0:STEPS * NB].rearrange("p (s b) -> p s b", b=NB)
        z_seq = Z[:, 0, 0].rearrange("p s c -> p (s c)")[:, 0:STEPS * NB].rearrange("p (s b) -> p s b", b=NB)
        r_seq = RB[:, 0, 0].rearrange("p s c -> p (s c)")[:, 0:STEPS * NB].rearrange("p (s b) -> p s b", b=NB)
        ROW_INC = 16 * (1 + IMG_GROUPS * PARTS)

        def rows_in_time(eng, row_of, body):
            with eng.Fori(0, CHUNKS) as q:
                q = eng.snap(q)
                with eng.Fori(0, WINDOWS) as r:
                    r = eng.snap(r)
                    n = eng.snap(q * WINDOWS + r)
                    row_of(n, q, r)
                    if body is not None:
                        with eng.Fori(0, BLOCKS) as j:
                            j = eng.snap(j)
                            body(eng.snap(n * BLOCKS + j), n, q, j)

        def one_by_one_sync(sp):
            src = x2.rearrange("c b (q r w) -> r q c b w", q=CHUNKS, w=WIN)
            dst = out.rearrange("b c h w -> b c (h w)").rearrange("b c (q r w) -> q r c b w", q=CHUNKS, w=WIN)

            def row(n, q, r):
                before, through = sp.snap(n * 16 + 16), sp.snap((n + 1) * BLOCKS + 1)
                sp.wait_ge(q_out, before)
                sp.wait_ge(pick_ready, 1)
                sp.dma_start(x_row, src[bass.ds(r, 1), bass.ds(q, 1)][0, 0]).then_inc(q_in, 16)
                for g in both:
                    for p in range(PARTS):
                        sp.dma_start(R[p * STEPS:(p + 1) * STEPS, g], r_win[bass.ds(r, 1), g, p][0]).then_inc(q_in, 16)
                sp.wait_ge(q_added, through)
                sp.wait_ge(pick_ready, 1)
                sp.dma_start(dst[bass.ds(q, 1), bass.ds(r, 1)][0, 0], x_row).then_inc(q_out, 16)

            sp.dma_start(R[0:1, 2, 0], R[0:1, 1, 0]).then_inc(q_out, 16)
            rows_in_time(sp, row, None)
            sp.wait_ge(q_out, (CHUNKS * WINDOWS + 1) * 16)

        def one_by_one_scalar(act):
            def body(m, n, q, j):
                for s in range(STEPS):
                    if s == 0:
                        act.wait_ge(q_added, m + 1)
                    act.wait_ge(q_summed, m * STEPS + s + 1)
                    nc.scalar.activation(y_seq[:, s], z_seq[:, s], ACT.Sigmoid, bias=bias_q).then_inc(q_y, 1)
            rows_in_time(act, lambda n, q, r: None, body)

        def one_by_one_vector(dve):
            nc.vector.memset(y_seq[:, STEPS - 1], 0.0).then_inc(q_y, 1)
            nc.vector.memset(small[:, 3:4], 0.0).then_inc(q_added, 1)

            def body(m, n, q, j):
                part = x_row[:, :, bass.ds(j * STEPS, STEPS)]
                dve.wait_ge(q_in, (n + 1) * ROW_INC)
                dve.wait_ge(q_spread, m + 1)
                nc.vector.tensor_tensor(t_seq, part.rearrange("p b s -> p s b"), r_seq, ALU.mult).then_inc(q_scaled, 1)
                dve.wait_ge(q_y, (m + 1) * STEPS + 1)
                nc.vector.tensor_tensor(part, part, y_seq.rearrange("p s b -> p b s"), ALU.add).then_inc(q_added, 1)
            rows_in_time(dve, lambda n, q, r: None, body)

        def one_by_one_tensor(pe):
            def body(m, n, q, j):
                pe.wait_ge(q_in, (n + 1) * ROW_INC)
                pe.wait_ge(q_added, m + 1)
                for s in range(STEPS):
                    for g in both:
                        of_band = R[:, g, bass.ds(j, 1)][:, 0].rearrange("p (b q) -> p q b", q=CHUNKS)[:, bass.ds(q, 1)][:, 0]
                        x = nc.tensor.matmul(r_seq[:, s, g * IMGS:(g + 1) * IMGS], pick[:, s], of_band, start=True, stop=True)
                x.then_inc(q_spread, 1)
                pe.wait_ge(q_scaled, m + 1)
                nc.tensor.matmul(z_seq.rearrange("p s b -> p (s b)"), wT, t_seq.rearrange("p s b -> p (s b)"),
                                 start=True, stop=False, skip_group_check=True)
                for s in range(STEPS):
                    pe.wait_ge(q_y, m * STEPS + s + 1)
                    nc.tensor.matmul(z_seq[:, s], vT, y_seq[:, (s - 1) % STEPS], start=False, stop=True,
                                     skip_group_check=True).then_inc(q_summed, 1)
            rows_in_time(pe, lambda n, q, r: None, body)

        @block.sync
        def _(sp):
            sp.wait_ge(pick_ready, 1)
            for g in both:
                src, half = x2_win[WINDOWS - 1, g], WIN // 2
                sp.dma_start(X[:, g, 1:COLS, half:WIN], src[:, 0:COLS - 1, half:WIN]).then_inc(window_in[g], 16)
                for p in range(PARTS):
                    r, rows = r_win[WINDOWS - 1, g, p], slice(p * STEPS, (p + 1) * STEPS)
                    sp.dma_start(R[rows, g, HALF:BLOCKS, 1:COLS], r[:, HALF:BLOCKS, 0:COLS - 1]).then_inc(window_in[g], 16)
            sp.wait_ge(scaled[0], 1)
            load(sp, 0, 0, 2, window_in[0])

            def window_through(w, g, refill):
                held = (lambda v: v) if isinstance(w, int) else sp.snap
                buf = held((IMG_GROUPS * w + g) % WINDOW_BUFS)
                through, stored = held(2 * (HALF + BLOCKS * w)), held((IMG_GROUPS * w + g - 1) * IMGS * 16)
                sp.wait_ge(added[g], through)
                sp.wait_ge(pick_ready, 1)
                if not isinstance(w, int) or w > 0:
                    for b in range(IMGS):
                        src = X[:, bass.ds(buf, 1), b * CHUNKS:(b + 1) * CHUNKS][:, 0]
                        sp.dma_start(out_win[bass.ds(w - 1, 1), g * IMGS + b][0], src).then_inc(out_stored, 16)
                if refill:
                    wait(sp, out_stored, stored)
                    sp.wait_ge(pick_ready, 1)
                    load(sp, w + g, 1 - g, buf, window_in[1 - g])

            window_through(0, 0, True)
            window_through(0, 1, True)
            with sp.Fori(1, WINDOWS - 1) as w:
                w = sp.snap(w)
                for g in both:
                    window_through(w, g, True)
            for w in (WINDOWS - 1, WINDOWS):
                for g in both:
                    window_through(w, g, w == WINDOWS - 1 and g == 0)
            sp.wait_ge(out_stored, WINDOWS * NB * 16)
            sp.wait_ge(verdict_in, 1)
            bad = sp.value_load(verdict[0:1, 0:1], min_val=0, max_val=1 << 20)
            with sp.If(bad > 0):
                one_by_one_sync(sp)
            sp.wait_ge(verdict_in, 1)

        @block.gpsimd
        def _(pool):
            pool_constants(nc, pool, R[:, :, :, :], pick[:, :, :], pick_ready)
            nc.gpsimd.memset(Y[:, :, STEPS - 1], 0.0).then_inc(y_zero, 1)
            nc.gpsimd.memset(ones, 1.0).then_inc(y_zero, 1)
            nc.gpsimd.memset(X[:, 0:IMG_GROUPS, 0, WIN // 2:WIN], 0.0).then_inc(y_zero, 1)

        @block.scalar
        def _(act):
            def body(m, now, after):
                for s in range(STEPS):
                    for g in now:
                        if s % QUAD == 0:
                            wait(act, added[g], 2 * m[g] + s // QUAD - 1)
                        wait(act, summed[g], m[g] * STEPS + s + 1)
                        nc.scalar.activation(Y[:, g, s], Z[:, g, s // QUAD, s % QUAD], ACT.Sigmoid, bias=bias_q).then_inc(y_ready[g], 1)

            def unit(u, parity, groups, then):
                with_first = isinstance(u, int) and u < IMG_GROUPS
                if with_first:
                    m = {g: (u - g) * HALF for g in groups}
                    body(m, groups, ())
                    with act.Fori(1, HALF) as b:
                        b = act.snap(b)
                        body({g: (u - g) * HALF + b for g in groups}, groups, ())
                else:
                    with act.Fori(0, HALF) as b:
                        b = act.snap(b)
                        body({g: (u - g) * HALF + b for g in groups}, groups, ())

            run_units(act, unit)
            act.wait_ge(verdict_in, 1)
            bad = act.value_load(verdict[0:1, 0:1], min_val=0, max_val=1 << 20)
            with act.If(bad > 0):
                one_by_one_scalar(act)
            act.wait_ge(verdict_in, 1)

        @block.vector
        def _(dve):
            def scale(g, m_next, place, i):
                buf, j = place
                wait(dve, spread_done[g], 2 * m_next + i + 1)
                src = X[:, buf, :, bass.ds(j * STEPS + i * QUAD, QUAD)].rearrange("p c s -> p s c")
                nc.vector.tensor_tensor(T[:, g, i], src, RB[:, g, i], ALU.mult).then_inc(scaled[g], 1)

            def add_states(g, m, place, i):
                buf, j = place
                wait(dve, y_ready[g], m * STEPS + (i + 1) * QUAD)
                part = X[:, buf, :, bass.ds(j * STEPS + i * QUAD, QUAD)]
                nc.vector.tensor_tensor(part, part, Y[:, g, i * QUAD:(i + 1) * QUAD].rearrange("p s c -> p c s"),
                                        ALU.add).then_inc(added[g], 1)

            def body(m, now, after):
                for i in range(2):
                    for g in after:
                        scale(g, m[g] + 1, after[g], i)
                    for g in now:
                        add_states(g, m[g], now[g], i)

            def unit(u, parity, groups, then):
                run_bodies(dve, u, parity, groups, then, body, lambda: wait_window(dve, u, parity, then))
                if isinstance(u, int) and u < IMG_GROUPS:
                    last = Y[:, u, STEPS - 1]
                    nc.vector.tensor_copy(y_warm[:, u], last).then_inc(warm_kept, 1)
                    dve.wait_ge(warm_kept, u + 1)
                    nc.vector.memset(last.rearrange("p (b q) -> p b q", q=CHUNKS)[:, :, 0:1], 0.0).then_inc(restarted, 1)

            dve.wait_ge(y_zero, 3)
            dve.wait_ge(window_in[0], WINDOW_INC)
            body({0: -1}, {}, {0: (0, HALF)})
            run_units(dve, unit)

            diff = T[:, 0].rearrange("p k s c -> p (k s c)")[:, 0:IMG_GROUPS * IMGS * (CHUNKS - 1)].rearrange(
                "p (g b q) -> p g b q", g=IMG_GROUPS, b=IMGS)
            for g in both:
                nc.vector.tensor_tensor(diff[:, g], Y[:, g, STEPS - 1].rearrange("p (b q) -> p b q", q=CHUNKS)[:, :, 0:CHUNKS - 1],
                                        y_warm[:, g].rearrange("p (b q) -> p b q", q=CHUNKS)[:, :, 1:CHUNKS],
                                        ALU.subtract).then_inc(check_step, 1)
            dve.wait_ge(check_step, 2)
            flat = diff.rearrange("p g b q -> p (g b q)")
            nc.vector.tensor_tensor(flat, flat, flat, ALU.mult).then_inc(check_step, 1)
            dve.wait_ge(check_step, 3)
            nc.vector.tensor_scalar(flat, flat, TOLERANCE * TOLERANCE, None, ALU.is_le).then_inc(check_step, 1)
            dve.wait_ge(check_step, 4)
            nc.vector.tensor_reduce(agreed[:, 0:1], flat, axis=AX.X, op=ALU.add).then_inc(check_step, 1)
            dve.wait_ge(check_summed, 1)
            count = float(CH * NB * (CHUNKS - 1))
            nc.vector.tensor_scalar(verdict[0:1, 0:1], RB[0:1, 0, 0, 0, 0:1], -1.0, count, ALU.mult, ALU.add).then_inc(verdict_in, 1)
            dve.wait_ge(verdict_in, 1)
            bad = dve.value_load(verdict[0:1, 0:1], min_val=0, max_val=1 << 20)
            with dve.If(bad > 0):
                one_by_one_vector(dve)
            dve.wait_ge(verdict_in, 1)

        @block.tensor
        def _(pe):
            def spread(g, place, i, half):
                buf, j = place
                for s in (2 * half, 2 * half + 1):
                    x = nc.tensor.matmul(RB[:, g, i, s], pick[:, QUAD * i + s], R[:, buf, j], start=s == 0, stop=s == QUAD - 1)
                if half == 1:
                    x.then_inc(spread_done[g], 1)

            def project(g, quad, i, half):
                if half == 0:
                    wait(pe, scaled[g], quad + 1)
                two = slice(2 * half, 2 * half + 2)
                nc.tensor.matmul(Z[:, g, i, two].rearrange("p s c -> p (s c)"), wT, T[:, g, i, two].rearrange("p s c -> p (s c)"),
                                 start=half == 0, stop=False, skip_group_check=True)

            def recur(g, m, s):
                wait(pe, y_ready[g], m * STEPS + s)
                nc.tensor.matmul(Z[:, g, s // QUAD, s % QUAD], vT, Y[:, g, (s - 1) % STEPS], start=False, stop=True,
                                 skip_group_check=True).then_inc(summed[g], 1)

            def body(m, now, after):
                for s in range(STEPS):
                    for g in now:
                        recur(g, m[g], s)
                    i, g, half = s // QUAD, s % QUAD // 2, s % 2
                    if (g in now) if i == 0 else (g in after):
                        project(g, 2 * m[g] + i + 1, 1 - i, half)
                    if g in after:
                        spread(g, after[g], i, half)

            def unit(u, parity, groups, then):
                run_bodies(pe, u, parity, groups, then, body, lambda: wait_window(pe, u, parity, then))
                if isinstance(u, int) and u < IMG_GROUPS:
                    pe.wait_ge(restarted, u + 1)

            pe.wait_ge(pick_ready, PICK_READY)
            pe.wait_ge(y_zero, 2)
            pe.wait_ge(window_in[0], WINDOW_INC)
            body({0: -1}, {}, {0: (0, HALF)})
            run_units(pe, unit)
            pe.wait_ge(check_step, 5)
            nc.tensor.matmul(RB[0:1, 0, 0, 0, 0:1], agreed[:, 0:1], ones, start=True, stop=True).then_inc(check_summed, 1)
            pe.wait_ge(verdict_in, 1)
            bad = pe.value_load(verdict[0:1, 0:1], min_val=0, max_val=1 << 20)
            with pe.If(bad > 0):
                one_by_one_tensor(pe)
            pe.wait_ge(verdict_in, 1)


def build(nc, x, conv_weight, W, V, gamma, beta, out):
    x2 = nc.dram_tensor("x2", (CH, NB, HT * WD), F32, kind="Internal").ap()
    stat2 = nc.dram_tensor("stat2", (2, NB, HT * WD), F32, kind="Internal").ap()
    rparts = nc.dram_tensor("rparts", (WINDOWS, IMG_GROUPS, PARTS, BLOCKS, STEPS, COLS), BF16, kind="Internal").ap()
    conv_phase(nc, x, conv_weight, x2, stat2)
    rstd_phase(nc, stat2, rparts)
    with ExitStack() as ctx:
        weights = ctx.enter_context(nc.sbuf_tensor("weights", [128, 2, 128], F32))
        bias = ctx.enter_context(nc.sbuf_tensor("bias", [128, 1], F32))
        statistics_phase(nc, x2, rparts, W, V, gamma, beta, weights[:, 0], weights[:, 1], bias[:, 0:1])
        scan_phase(nc, x2, rparts, weights[:, 0], weights[:, 1], bias[:, 0:1], out)


_INS = ['x', 'L0_conv_weight', 'L0_ffn_W', 'L0_ffn_V', 'L0_ffn_gamma', 'L0_ffn_beta']
_OUTS = [((NB, CH, HT, WD), 'float32')]


def kernel(**inputs):
    import numpy as _np
    import concourse.bacc as _bacc
    from concourse import mybir as _mybir
    from concourse.bass_utils import run_bass_kernel_spmd as _run
    nc = _bacc.Bacc("TRN2", target_bir_lowering=False, num_devices=1)
    arrays, args = {}, []
    for name in _INS:
        a = _np.ascontiguousarray(inputs[name])
        arrays[f"in_{name}_dram"] = a
        args.append(nc.dram_tensor(f"in_{name}_dram", a.shape, _mybir.dt.from_np(a.dtype), kind="ExternalInput").ap())
    for i, (shape, dtype) in enumerate(_OUTS):
        dt = _mybir.dt.from_np(_np.dtype(dtype))
        args.append(nc.dram_tensor(f"out_{i}_dram", shape, dt, kind="ExternalOutput").ap())
    build(nc, *args)
    r = _run(nc, [arrays], core_ids=[0])
    return r.results[0]["out_0_dram"]
```
